# Optimizing a Trainium2 kernel written in Bass

```python
import numpy as np
import jax
import jax.numpy as jnp

def _softmax(x, axis=-1):
    return jax.nn.softmax(x, axis=axis)

def _gelu(x):
    return jax.nn.gelu(x, approximate=True)

def _silu(x):
    return jax.nn.silu(x)

def _sigmoid(x):
    return jax.nn.sigmoid(x)

def _layernorm(x, axis=-1, eps=1e-05):
    m = jnp.mean(x, axis=axis, keepdims=True)
    v = jnp.var(x, axis=axis, keepdims=True)
    return (x - m) / jnp.sqrt(v + eps)

def _scatter_add(tgt, idx, src, axis=0):
    return tgt.at[idx].add(src)

def _segment_sum(src, seg, n):
    return jax.ops.segment_sum(src, seg, n)
kernel_name = 'mk_decoder_preln_d1_seqx_r4_79a0c9'

def setup_inputs(seed: int=0):
    np.random.seed(seed)
    _w = jnp.asarray

    def _rec_inputs():
        import jax
        import jax.numpy as jnp
        _rk = jax.random.key(seed)
        x = -0.000125 + 0.9999 * jax.random.normal(jax.random.fold_in(_rk, 1), (4, 512, 512), jnp.float32)
        _lenS = 512 - jax.random.randint(jax.random.fold_in(_rk, 7), (4,), 0, max(1, 512 // 4) + 1, jnp.int32)
        _lenS2 = 512 - jax.random.randint(jax.random.fold_in(_rk, 8), (4,), 0, max(1, 512 // 4) + 1, jnp.int32)
        itok_BxS_13_99985 = jax.random.randint(jax.random.fold_in(_rk, 11), (4, 512), 13, 99986, jnp.int32)
        _ctx_2048P = jax.random.normal(jax.random.fold_in(_rk, 12), (4, 16, 512), jnp.float32)
        _ctx_2048c = jax.random.dirichlet(jax.random.fold_in(_rk, 512), 0.3 * jnp.ones((16,), jnp.float32), (4, 512))
        _ctx_2048t = jnp.einsum('bsk,bkd->bsd', _ctx_2048c, _ctx_2048P)
        _ctx_2048t = _ctx_2048t * jax.lax.rsqrt(jnp.mean(jnp.square(_ctx_2048t)) + 1e-12) * 0.953939
        ctx_2048 = 6.82029e-06 + 0.0200006 * (_ctx_2048t + 0.3 * jax.random.normal(jax.random.fold_in(_rk, 612), (4, 512, 512), jnp.float32))
        return (x, itok_BxS_13_99985, ctx_2048)
    x, itok_BxS_13_99985, ctx_2048 = _rec_inputs()

    def _L0_attn_setup():
        import jax, jax.numpy as jnp
        import numpy as np
        EPS_NORM = 1e-06
        EPS_Q = 1e-05

        def rmsnorm(x, g):
            var = jnp.mean(jnp.square(x), axis=-1, keepdims=True)
            return x * jax.lax.rsqrt(var + EPS_NORM) * g

        def act_quant(x):
            scale = 127.0 / jnp.clip(jnp.max(jnp.abs(x), axis=-1, keepdims=True), EPS_Q, None)
            return jnp.clip(jnp.round(x * scale), -128.0, 127.0) / scale

        def weight_quant(w):
            scale = 1.0 / jnp.clip(jnp.mean(jnp.abs(w)), EPS_Q, None)
            return jnp.clip(jnp.round(w * scale), -1.0, 1.0) / scale

        def ste(x, fn):
            return x + jax.lax.stop_gradient(fn(x) - x)

        def bitlinear(x, w, g):
            xn = rmsnorm(x, g)
            xq = ste(xn, act_quant)
            wq = ste(w, weight_quant)
            return jnp.einsum('bsd,od->bso', xq, wq)
        key = jax.random.key(seed)
        k1, k2, k3 = jax.random.split(key, 3)
        B, S, D, I = (4, 1024, 512, 1408)
        x = jax.random.normal(k1, (B, S, D), dtype=jnp.float32)
        w_gate = jax.random.normal(k2, (2 * I, D), dtype=jnp.float32) * D ** (-0.5)
        g_gate = jnp.ones((D,), dtype=jnp.float32)
        w_down = jax.random.normal(k3, (D, I), dtype=jnp.float32) * I ** (-0.5)
        g_down = jnp.ones((I,), dtype=jnp.float32)
        return {'x': x, 'w_gate': w_gate, 'g_gate': g_gate, 'w_down': w_down, 'g_down': g_down}
    _L0_attn_all = _L0_attn_setup()
    _L0_attn_in = {k: v for k, v in _L0_attn_all.items() if k in ('w_gate', 'g_gate', 'w_down', 'g_down')}
    del _L0_attn_all

    def _L0_xattn_setup():
        import jax, jax.numpy as jnp
        import numpy as np
        B, S, D = (4, 1024, 512)
        E = 4
        F = 2048 // E
        VOCAB = 25000
        key = jax.random.key(seed)
        k1, k2, k3, k4, k5 = jax.random.split(key, 5)
        hidden_states = jax.random.normal(k1, (B, S, D), dtype=jnp.float32)
        token_ids = jax.random.randint(k2, (B, S), 0, VOCAB, dtype=jnp.int64)
        Wg = jax.random.normal(k3, (E, F, D), dtype=jnp.float32) * 0.02
        Wu = jax.random.normal(k4, (E, F, D), dtype=jnp.float32) * 0.02
        Wd = jax.random.normal(k5, (E, D, F), dtype=jnp.float32) * 0.02
        return {'hidden_states': hidden_states, 'token_ids': token_ids, 'Wg': Wg, 'Wu': Wu, 'Wd': Wd}
    _L0_xattn_all = _L0_xattn_setup()
    _L0_xattn_in = {k: v for k, v in _L0_xattn_all.items() if k in ()}
    del _L0_xattn_all

    def _L0_ffn_setup():
        import jax, jax.numpy as jnp
        import numpy as np
        H = 512
        I = 352
        E = 8
        TOP_K = 2
        N_SHARED = 2
        IS = N_SHARED * I
        key = jax.random.key(seed)
        ks = jax.random.split(key, 8)
        s_h = 1.0 / np.sqrt(H)
        s_i = 1.0 / np.sqrt(I)
        s_is = 1.0 / np.sqrt(IS)
        return {'hidden_states': jax.random.normal(ks[0], (1, 512, H), jnp.float32), 'gate_w': jax.random.normal(ks[1], (E, H), jnp.float32) * s_h, 'w_gate': jax.random.normal(ks[2], (E, H, I), jnp.float32) * s_h, 'w_up': jax.random.normal(ks[3], (E, H, I), jnp.float32) * s_h, 'w_down': jax.random.normal(ks[4], (E, I, H), jnp.float32) * s_i, 'sw_gate': jax.random.normal(ks[5], (H, IS), jnp.float32) * s_h, 'sw_up': jax.random.normal(ks[6], (H, IS), jnp.float32) * s_h, 'sw_down': jax.random.normal(ks[7], (IS, H), jnp.float32) * s_is}
    _L0_ffn_all = _L0_ffn_setup()
    _L0_ffn_in = {k: v for k, v in _L0_ffn_all.items() if k in ('gate_w', 'w_gate', 'w_up', 'w_down', 'sw_gate', 'sw_up', 'sw_down')}
    del _L0_ffn_all
    return {'x': x, 'itok_BxS_13_99985': itok_BxS_13_99985, 'ctx_2048': ctx_2048, 'L0_attn_w_gate': _L0_attn_in['w_gate'], 'L0_attn_g_gate': _L0_attn_in['g_gate'], 'L0_attn_w_down': _L0_attn_in['w_down'], 'L0_attn_g_down': _L0_attn_in['g_down'], 'L0_ffn_gate_w': _L0_ffn_in['gate_w'], 'L0_ffn_w_gate': _L0_ffn_in['w_gate'], 'L0_ffn_w_up': _L0_ffn_in['w_up'], 'L0_ffn_w_down': _L0_ffn_in['w_down'], 'L0_ffn_sw_gate': _L0_ffn_in['sw_gate'], 'L0_ffn_sw_up': _L0_ffn_in['sw_up'], 'L0_ffn_sw_down': _L0_ffn_in['sw_down']}

def reference(x, itok_BxS_13_99985, ctx_2048, L0_attn_w_gate, L0_attn_g_gate, L0_attn_w_down, L0_attn_g_down, L0_ffn_gate_w, L0_ffn_w_gate, L0_ffn_w_up, L0_ffn_w_down, L0_ffn_sw_gate, L0_ffn_sw_up, L0_ffn_sw_down):
    import jax
    import jax.numpy as jnp

    def _L0_attn_ref(x, w_gate, g_gate, w_down, g_down):
        import jax, jax.numpy as jnp
        import numpy as np
        EPS_NORM = 1e-06
        EPS_Q = 1e-05

        def rmsnorm(x, g):
            var = jnp.mean(jnp.square(x), axis=-1, keepdims=True)
            return x * jax.lax.rsqrt(var + EPS_NORM) * g

        def act_quant(x):
            scale = 127.0 / jnp.clip(jnp.max(jnp.abs(x), axis=-1, keepdims=True), EPS_Q, None)
            return jnp.clip(jnp.round(x * scale), -128.0, 127.0) / scale

        def weight_quant(w):
            scale = 1.0 / jnp.clip(jnp.mean(jnp.abs(w)), EPS_Q, None)
            return jnp.clip(jnp.round(w * scale), -1.0, 1.0) / scale

        def ste(x, fn):
            return x + jax.lax.stop_gradient(fn(x) - x)

        def bitlinear(x, w, g):
            xn = rmsnorm(x, g)
            xq = ste(xn, act_quant)
            wq = ste(w, weight_quant)
            return jnp.einsum('bsd,od->bso', xq, wq)
        y = bitlinear(x, w_gate, g_gate)
        gate, v = jnp.split(y, 2, axis=-1)
        swiglu_out = gate * jax.nn.sigmoid(gate) * v
        z = bitlinear(swiglu_out, w_down, g_down)
        return z

    def _L0_xattn_ref(hidden_states, token_ids, Wg, Wu, Wd):
        import jax, jax.numpy as jnp
        import numpy as np
        B, S, D = (4, 1024, 512)
        E = 4
        F = 2048 // E
        VOCAB = 25000
        tokens_per_expert = VOCAB // E
        tid = jnp.clip(token_ids, 0, VOCAB - 1)
        expert_ids = jnp.minimum(tid // tokens_per_expert, E - 1)
        out = jnp.zeros_like(hidden_states)
        for e in range(E):
            g = jax.nn.silu(jnp.einsum('bsd,fd->bsf', hidden_states, Wg[e]))
            u = jnp.einsum('bsd,fd->bsf', hidden_states, Wu[e])
            y = jnp.einsum('bsf,df->bsd', g * u, Wd[e])
            out = jnp.where((expert_ids == e)[..., None], y, out)
        return out

    def _L0_ffn_ref(hidden_states, gate_w, w_gate, w_up, w_down, sw_gate, sw_up, sw_down):
        import jax, jax.numpy as jnp
        import numpy as np
        H = 512
        I = 352
        E = 8
        TOP_K = 2
        N_SHARED = 2
        IS = N_SHARED * I
        B, S, _ = hidden_states.shape
        x = hidden_states.reshape(-1, H)
        N = x.shape[0]
        logits = x @ gate_w.T
        scores = jax.nn.softmax(logits, axis=-1)
        topk_w, topk_i = jax.lax.top_k(scores, TOP_K)
        g = jnp.einsum('nh,ehi->eni', x, w_gate)
        u = jnp.einsum('nh,ehi->eni', x, w_up)
        h = jax.nn.silu(g) * u
        eo = jnp.einsum('eni,eih->enh', h, w_down)
        combine = jnp.zeros((N, E), x.dtype).at[jnp.arange(N)[:, None], topk_i].add(topk_w)
        y = jnp.einsum('ne,enh->nh', combine, eo)
        sh = jax.nn.silu(x @ sw_gate) * (x @ sw_up)
        y = y + sh @ sw_down
        return y.reshape(B, S, H)
    x = x + _L0_attn_ref(_layernorm(x, axis=-1), L0_attn_w_gate, L0_attn_g_gate, L0_attn_w_down, L0_attn_g_down)
    x = x + _L0_xattn_ref(_layernorm(x, axis=-1), itok_BxS_13_99985, ctx_2048, ctx_2048, ctx_2048)
    x = x + _L0_ffn_ref(_layernorm(x, axis=-1), L0_ffn_gate_w, L0_ffn_w_gate, L0_ffn_w_up, L0_ffn_w_down, L0_ffn_sw_gate, L0_ffn_sw_up, L0_ffn_sw_down)
    return x

_drawn_inputs = setup_inputs


def setup_inputs(seed=0):
    import zlib

    import numpy as np

    out = dict(_drawn_inputs(seed))
    spreads = {'L0_attn_g_gate': (1.0, 0.2), 'L0_attn_g_down': (1.0, 0.2)}
    factors = {}
    for name, (base, spread) in spreads.items():
        noise = np.random.default_rng([zlib.crc32(name.encode()), seed]).standard_normal(out[name].shape)
        drawn = base * np.exp(spread * noise) if base else spread * noise
        out[name] = jnp.asarray(drawn.astype(out[name].dtype))
    for name, factor in factors.items():
        out[name] = (out[name] * factor).astype(out[name].dtype)
    return out
```

```python
from collections import namedtuple
from contextlib import ExitStack

import numpy as np
import concourse.bass as bass
import concourse.mybir as mybir

F32, F16, BF16 = mybir.dt.float32, mybir.dt.float16, mybir.dt.bfloat16
I32 = mybir.dt.int32
ALU = mybir.AluOpType
ACT = mybir.ActivationFunctionType
AX = mybir.AxisListType

P = 128
D = 512
KD = D // P
N = 2048
T = N // P
IA = 1408
KI = IA // P
CW = 352
CA = IA // CW
E_B, E_C = 4, 8
J_B = T + E_B - 1
J_C = 2 * T + E_C - 1
VOCAB = 25000
PER_EXPERT = VOCAB // E_B
IC = 352
ICP = 384
IS = 704
ISP = 768
SLOT = KD * 2 * IC + (ICP // P) * D
SHARED = KD * 2 * IS + (ISP // P) * D
LOADS_PER_SLOT = 4
CHUNK = SLOT // LOADS_PER_SLOT
SLOTS = E_C + 2
CHUNKS = SLOTS * LOADS_PER_SLOT
assert SHARED == 2 * SLOT and CHUNK * LOADS_PER_SLOT == SLOT
EPS_LN, EPS_RMS, EPS_Q = 1e-5, 1e-6, 1e-5
MAGIC = 12582912.0
SCALE_B, SCALE_C = 256.0, 64.0

Step = namedtuple("Step", "t u h")


def pipeline(engine, count, stages):
    lags = [g for g, _ in stages]
    first = max(lags) + 2
    turns = (count + min(lags) - first) // 2

    def straight(r):
        for g, stage in stages:
            if 0 <= r - g < count:
                stage(Step(r - g, (r - g) % 2, (r - g) // 2))

    for r in range(min(lags), first):
        straight(r)
    if turns > 0:
        with engine.Fori(0, turns) as i:
            for c in range(2):
                for g, stage in stages:
                    t = first + c - g
                    stage(Step(i * 2 + t, t % 2, i + t // 2))
    for r in range(first + 2 * max(turns, 0), count + max(lags)):
        straight(r)


def before(engine, sem, t, back, per=1):
    if isinstance(t, int) and t < back:
        return
    engine.wait_ge(sem, (t - (back - 1)) * per)


def build(nc, x, tok, wgate, wdown, ggate, gdown, ctxt, gatew, wmoe, out):
    ctx = ExitStack()
    with ctx:
        def sb(name, shape, dt):
            return ctx.enter_context(nc.sbuf_tensor(name, shape, dt))

        def sem(name):
            return ctx.enter_context(nc.semaphore(name))

        def two(name):
            return [sem(f"{name}{i}") for i in range(2)]

        def dram(name, shape, dt):
            return nc.dram_tensor(name, shape, dt, kind="Internal").ap()

        x1_d, x2_d, x3_d = (dram(n, (N, D), F32) for n in ("x1_d", "x2_d", "x3_d"))
        hB_d, hC_d = (dram(n, (N, 2 * D), F16) for n in ("hB_d", "hC_d"))
        yB_d = dram("yB_d", (J_B * P, D), F32)
        yC_d = dram("yC_d", (J_C * P, D), F32)

        w_hi = sb("w_hi", [P, SLOTS * SLOT], F16)
        w_lo = sb("w_lo", [P, SLOTS * SLOT], F16)

        class Carver:

            def __init__(self, tensor, slot, slots):
                self.flat, self.at, self.end = tensor, slot * SLOT, (slot + slots) * SLOT

            def take(self, n, dt):
                words = n * (2 if dt == F32 else 1)
                view = self.flat[:, self.at:self.at + words]
                self.at += words
                assert self.at <= self.end
                return view if dt == F16 else view.bitcast(dt)

        stage_hi, stage_lo = Carver(w_hi, 0, 4), Carver(w_lo, 0, 4)
        OG = 2 * IA
        wg32 = [stage_hi.take(OG, F32) for _ in range(3)] + [stage_lo.take(OG, F32)]
        wd32 = stage_lo.take(KI * D, F32)
        tern_hi, tern_lo = Carver(w_hi, 4, 2), Carver(w_lo, 4, 2)
        wgT = [tern_hi.take(OG, BF16) for _ in range(3)] + [tern_lo.take(OG, BF16)]
        wdT = tern_lo.take(KI * D, BF16)
        a6h, a6l, a9h, a9l = Carver(w_hi, 6, 1), Carver(w_lo, 6, 1), Carver(w_hi, 9, 1), Carver(w_lo, 9, 1)
        xin = [a6h.take(D, F32) for _ in range(2)]
        xcen = [a6h.take(D, F32) for _ in range(2)]
        xq = [a6l.take(D, BF16) for _ in range(2)]
        xqT = [a6l.take(D, BF16) for _ in range(2)]
        xmag = [a6l.take(D, F32) for _ in range(2)]
        gg = a9h.take(D, F32)
        negs = [a9h.take(OG, BF16), a9l.take(OG, BF16)]
        hA = a9l.take(D, F32)
        ah, al = Carver(w_hi, 0, 4), Carver(w_lo, 0, 4)
        sw = [ah.take(IA, F32) for _ in range(2)]
        swg = [ah.take(IA, F32) for _ in range(2)]
        sil = [ah.take(CW, F32) for _ in range(2)]
        squares = ah.take(IA, F32)
        qd = [al.take(IA, BF16) for _ in range(2)]
        qdT = [al.take(IA, BF16) for _ in range(2)]
        xres = [al.take(D, F32) for _ in range(2)]
        x1 = [al.take(D, F32) for _ in range(2)]
        gd = al.take(IA, F32)
        c_hi, c_lo = Carver(w_hi, 7, 2).take(E_B * KD * D, F16), Carver(w_lo, 7, 2).take(E_B * KD * D, F16)
        b9h, b9l = Carver(w_hi, 9, 1), Carver(w_lo, 9, 1)
        bs = [b9h.take(D, F32) for _ in range(2)]
        bpT = [b9h.take(2 * D, F16).rearrange("p (a n) -> p a n", a=2) for _ in range(2)]
        s9h = Carver(w_hi, 9, 1)
        ss = s9h.take(ISP, F32)
        spT = s9h.take(2 * ISP, F16).rearrange("p (a n) -> p a n", a=2)
        hS = s9h.take(D, F32)
        xS = [b9l.take(D, F32) for _ in range(2)]
        yS = [b9l.take(D, F32) for _ in range(2)]
        ch, cl = Carver(w_hi, 0, 2), Carver(w_lo, 0, 2)
        cs = [ch.take(ICP, F32) for _ in range(2)]
        cpT = [ch.take(2 * ICP, F16).rearrange("p (a n) -> p a n", a=2) for _ in range(2)]
        xF = [cl.take(D, F32) for _ in range(2)]
        y1F = [cl.take(D, F32) for _ in range(2)]
        y2F = [ch.take(D, F32) for _ in range(2)]

        wstage = [sb(f"wstage{i}", [P, CHUNK], F32) for i in range(2)]
        rows = [sb(f"rows{i}", [P, 2 * D], F16) for i in range(2)]
        hT = [sb(f"hT{i}", [P, 2 * KD, P], F16) for i in range(2)]
        yrow = [sb(f"yrow{i}", [P, D], F32) for i in range(2)]
        eyeF, eyeH, eyeB = sb("eyeF", [P, P], F32), sb("eyeH", [P, P], F16), sb("eyeB", [P, P], BF16)
        onesF = sb("onesF", [P, P], F32)
        onesH, triH = sb("onesH", [P, P], F16), sb("triH", [P, P], F16)
        iotaI = sb("iotaI", [P, P], I32)
        iotaF = sb("iotaF", [P, P], F32)
        tokidI, tokid = sb("tokidI", [P, T], I32), sb("tokid", [P, T], F32)
        powh, powm = sb("powh", [P, 1], F32), sb("powm", [P, 1], F32)
        asum = sb("asum", [P, KD + 1], F32)
        wmean = sb("wmean", [P, 2], F32)
        thr = sb("thr", [P, 4], F32)
        tokI, tokF = sb("tokI", [P, T], I32), sb("tokF", [P, T], F32)
        gw32 = sb("gw32", [P, KD * E_C], F32)
        gw_hi, gw_lo = sb("gw_hi", [P, KD * E_C], F16), sb("gw_lo", [P, KD * E_C], F16)
        stats = [sb(f"xstats{i}", [P, 6], F32) for i in range(2)]
        mv = [sb(f"xmv{i}", [P, 2], F32) for i in range(2)]
        xmax = [sb(f"xmax{i}", [P, 1], F32) for i in range(2)]
        smA = [sb(f"smA{i}", [P, 8], F32) for i in range(2)]
        cx = [sb(f"cx{i}", [P, 1], F32) for i in range(2)]
        dqx = [sb(f"dqx{i}", [P, 1], F32) for i in range(2)]
        ssq = [sb(f"ssq{i}", [P, 1], F32) for i in range(2)]
        gmax = [sb(f"gmax{i}", [P, 1], F32) for i in range(2)]
        smG = [sb(f"smG{i}", [P, 8], F32) for i in range(2)]
        cg = [sb(f"cg{i}", [P, 1], F32) for i in range(2)]
        dqg = [sb(f"dqg{i}", [P, 1], F32) for i in range(2)]
        stats1 = sb("stats1", [P, 6], F32)
        mv1 = sb("mv1", [P, 2], F32)
        var1 = sb("var1", [P, 1], F32)
        rstd1 = sb("rstd1", [P, 1], F32)
        W2 = T * E_C
        oh = sb("oh", [P, T, E_C], F16)
        oh12 = [sb(f"oh{c}_", [P, T, E_C], F32) for c in range(2)]
        ohsum = sb("ohsum", [P, T + 1, E_C], F16)
        rank = sb("rank", [P, T + 1, E_C], F32)
        rt = sb("rt", [P, T, E_C], F32)
        rt2 = sb("rt2", [P, T, E_C], F32)
        eI = sb("eI", [P, E_C], I32)
        eF = sb("eF", [P, 3, E_C], F32)
        rI = sb("rI", [P, 2, T], I32)
        rF = sb("rF", [P, 4, T], F32)
        posF = sb("posF", [P, T], F32)
        posB = sb("posB", [P, T], I32)
        posC = [sb(f"posC{c}", [P, T], I32) for c in range(2)]
        selR = [sb(f"selR{i}", [P, P], F16) for i in range(2)]
        selJ = [sb(f"selJ{i}", [P, J_C], F16) for i in range(2)]
        jF = [sb(f"jF{i}", [P, J_C], F32) for i in range(2)]
        invB, invC = sb("invB", [P, J_B], I32), sb("invC", [P, J_C], I32)
        expB, expC = sb("expB", [P, J_B], I32), sb("expC", [P, J_C], I32)
        idx = [sb(f"idx{i}", [P, 1], I32) for i in range(2)]
        idy = [sb(f"idy{i}", [P, 1], I32) for i in range(2)]
        logits = sb("logits", [P, T, E_C], F32)
        m12 = sb("m12", [P, 2, T], F32)
        wsum = sb("wsum", [P, T], F32)
        wtop = [sb(f"wtop{c}", [P, T], F32) for c in range(2)]

        banks = ctx.enter_context(nc.psum_tensor("banks", [P, 8, 512], F32))

        def bank(b, n=512, at=0):
            return banks[:, b, at:at + n]

        def wide(b, n):
            return banks[:, b:b + 2, :].rearrange("p a n -> p (a n)")[:, 0:n]

        consts = sem("consts")
        const_steps = sem("const_steps")
        tok_in, gains_in = sem("tok_in"), sem("gains_in")
        gd_in = sem("gd_in")
        wg_in = [sem(f"wg_in{k}") for k in range(KD)]
        wd_in = sem("wd_in")
        abs_done, tot_done, thr_done = sem("abs_done"), sem("tot_done"), sem("thr_done")
        neg_done, tern_done, gw_done = sem("neg_done"), sem("tern_done"), sem("gw_done")
        passed = {n: sem(f"passed_{n}") for n in ("dve", "pool", "pe")}
        x_in = two("x_in")
        x_stats, x_mom, x_cen, x_max = sem("x_stats"), sem("x_mom"), sem("x_cen"), sem("x_max")
        x_small, x_mag, x_q, x_T, x_ev = sem("x_small"), sem("x_mag"), sem("x_q"), sem("x_T"), sem("x_ev")
        gu_done, sil_done, sw_done = sem("gu_done"), sem("sil_done"), sem("sw_done")
        swg_done, sq_done, g_max, g_small = sem("swg_done"), sem("sq_done"), sem("g_max"), sem("g_small")
        d_mag, d_q, d_T, d_ev, z_done = sem("d_mag"), sem("d_q"), sem("d_T"), sem("d_ev"), sem("z_done")
        xr_in, x1_out, hb_out = two("xr_in"), two("x1_out"), two("hb_out")
        x1_done, st1, mo1, rs1 = sem("x1_done"), sem("st1"), sem("mo1"), sem("rs1")
        smA_s, smG_s, smB_s = sem("smA_s"), sem("smG_s"), sem("smB_s")
        h_done, hi_done, lo_done = sem("h_done"), sem("hi_done"), sem("lo_done")
        ctx_in, ctx_hi, ctx_lo = two("ctx_in"), sem("ctx_hi"), sem("ctx_lo")
        route = sem("route")
        route_mm, sel_done, inv_mm = sem("route_mm"), sem("sel_done"), sem("inv_mm")
        routeB, routeC = sem("routeB"), sem("routeC")
        w_in, whi_done, wlo_done = two("w_in"), sem("whi_done"), sem("wlo_done")
        b_idx, b_rows, b_T, b_ev = sem("b_idx"), two("b_rows"), sem("b_T"), sem("b_ev")
        b_t, b_sil, b_a, b_aT = sem("b_t"), sem("b_sil"), sem("b_a"), sem("b_aT")
        b_hi, b_lo, b_y, b_yev, b_out = sem("b_hi"), sem("b_lo"), sem("b_y"), sem("b_yev"), two("b_out")
        s_x, s_idx, s_y = two("s_x"), sem("s_idx"), two("s_y")
        s_x2, s_st, s_mo, s_rs, s_small = sem("s_x2"), sem("s_st"), sem("s_mo"), sem("s_rs"), sem("s_small")
        s_h, s_hi, s_lo, s_x2out, s_hout = sem("s_h"), sem("s_hi"), sem("s_lo"), two("s_x2out"), two("s_hout")
        s_T, s_ev, s_lg, s_lgev = sem("s_T"), sem("s_ev"), sem("s_lg"), sem("s_lgev")
        s_gu, s_sil, s_p, s_pT = sem("s_gu"), sem("s_sil"), sem("s_p"), sem("s_pT")
        s_phi, s_plo, s_dn, s_xr, s_x3, s_x3out = (sem("s_phi"), sem("s_plo"), sem("s_dn"), two("s_xr"),
                                                   sem("s_x3"), two("s_x3out"))
        pad_done, s_pad = sem("pad_done"), sem("s_pad")
        exp_done = sem("exp_done")
        c_idx, c_rows, c_T, c_ev = sem("c_idx"), two("c_rows"), sem("c_T"), sem("c_ev")
        c_gu, c_sil, c_p, c_pT = sem("c_gu"), sem("c_sil"), sem("c_p"), sem("c_pT")
        c_hi_s, c_lo_s, c_dn, c_yev, c_out = sem("c_phi"), sem("c_plo"), sem("c_dn"), sem("c_yev"), two("c_out")
        f_idx, f_x, f_y1, f_y2, f_a, f_o, f_out = (sem("f_idx"), two("f_x"), two("f_y1"), two("f_y2"),
                                                   sem("f_a"), sem("f_o"), two("f_out"))

        HALF = T // 2

        def tiles(ap, t):
            return ap[bass.ds(t * P, P), :]

        def alone(engine, name, s, value):
            engine.wait_ge(s, value)
            engine.sem_inc(passed[name], 1)

        block = ctx.enter_context(nc.Block())

        @block.sync
        def _(sp):
            sp.dma_start(tokI[:], tok[:]).then_inc(tok_in, 16)
            sp.dma_start(gg, ggate.broadcast_to([P, D])).then_inc(gains_in, 16)
            sp.dma_start(gw32[:], gatew[:]).then_inc(gains_in, 16)
            for k in range(KD):
                sp.dma_start(wg32[k], wgate[:, k * OG:(k + 1) * OG]).then_inc(wg_in[k], 16)
                if k < 2:
                    sp.dma_start(xin[k], tiles(x, k)).then_inc(x_in[k], 16)
            sp.dma_start(wd32, wdown[:]).then_inc(wd_in, 16)
            sp.wait_ge(tern_done, KD + 2)
            sp.dma_start(gd, gdown.broadcast_to([P, IA])).then_inc(gd_in, 16)

            def load_x(s):
                if isinstance(s.t, int) and s.t < 2:
                    return
                before(sp, x_cen, s.t, 2)
                before(sp, x_stats, s.t, 2)
                sp.dma_start(xin[s.u], tiles(x, s.t)).then_inc(x_in[s.u], 16)

            def load_res(s):
                before(sp, x1_done, s.t, 2)
                sp.dma_start(xres[s.u], tiles(x, s.t)).then_inc(xr_in[s.u], 16)

            def load_ctx(s):
                before(sp, ctx_lo, s.t, 2)
                sp.dma_start(wstage[s.u][:, 0:D], ctxt[:, bass.ds(s.t * D, D)]).then_inc(ctx_in[s.u], 16)

            def store_x1(s):
                sp.wait_ge(x1_done, s.t + 1)
                sp.dma_start(tiles(x1_d, s.t), x1[s.u]).then_inc(x1_out[s.u], 16)

            def store_hb(s):
                sp.wait_ge(hi_done, s.t + 1)
                sp.wait_ge(lo_done, s.t + 1)
                sp.dma_start(tiles(hB_d, s.t), rows[s.u][:]).then_inc(hb_out[s.u], 16)

            pipeline(sp, T, [(-3, load_x), (0, load_res), (0, load_ctx), (1, store_x1), (2, store_hb)])

            def load_w(q, u, wait):
                if wait:
                    sp.wait_ge(wlo_done, q - 1)
                sp.dma_start(wstage[u][:], wmoe[bass.ds(q * P, P), :]).then_inc(w_in[u], 16)

            def b_load(s):
                if isinstance(s.t, int) and s.t < 2:
                    sp.wait_ge(ctx_lo, T)
                load_w(s.t, s.u, not (isinstance(s.t, int) and s.t < 2))

            def b_store(s):
                sp.wait_ge(b_yev, s.t + 1)
                sp.dma_start(tiles(yB_d, s.t), yrow[s.u][:]).then_inc(b_out[s.u], 16)

            pipeline(sp, J_B, [(-1, b_load), (1, b_store)])

            def s_load(s):
                before(sp, s_x2out[s.u], s.h, 1, 16)
                before(sp, s_h, s.t, 2)
                sp.dma_start(xS[s.u], tiles(x1_d, s.t)).then_inc(s_x[s.u], 16)

            def s_loadw(s):
                load_w(s.t + J_B, (J_B % 2 + s.u) % 2, True)

            def s_storex2(s):
                sp.wait_ge(s_x2, s.t + 1)
                sp.dma_start(tiles(x2_d, s.t), xS[s.u]).then_inc(s_x2out[s.u], 16)

            def s_storeh(s):
                sp.wait_ge(s_hi, s.t + 1)
                sp.wait_ge(s_lo, s.t + 1)
                sp.dma_start(tiles(hC_d, s.t), rows[s.u][:]).then_inc(s_hout[s.u], 16)

            def s_loadres(s):
                sp.wait_ge(s_x2out[s.u], (s.h + 1) * 16)
                before(sp, s_x3out[s.u], s.h, 1, 16)
                if isinstance(s.t, int) and s.t < 2:
                    sp.wait_ge(b_out[0], 16 * ((J_B + 1) // 2))
                    sp.wait_ge(b_out[1], 16 * (J_B // 2))
                sp.dma_start(yrow[s.u][:], tiles(x2_d, s.t)).then_inc(s_xr[s.u], 16)

            def s_storex3(s):
                sp.wait_ge(s_x3, s.t + 1)
                sp.dma_start(tiles(x3_d, s.t), yrow[s.u][:]).then_inc(s_x3out[s.u], 16)

            sp.wait_ge(x1_out[0], 16 * HALF)
            sp.wait_ge(x1_out[1], 16 * HALF)
            sp.wait_ge(b_y, J_B)
            pipeline(sp, T, [(-2, s_load), (-1, s_loadw), (-1, s_storex2), (-1, s_storeh), (0, s_loadres), (1, s_storex3)])

            sp.wait_ge(s_dn, T)
            sp.wait_ge(s_x2out[0], 16 * HALF)
            sp.wait_ge(s_x2out[1], 16 * HALF)
            for q in range(J_B + T, CHUNKS):
                load_w(q, q % 2, True)
            sp.wait_ge(s_x3out[0], 16 * HALF)
            sp.wait_ge(s_x3out[1], 16 * HALF)

            def c_store(s):
                sp.wait_ge(c_yev, s.t + 1)
                sp.dma_start(tiles(yC_d, s.t), yrow[s.u][:]).then_inc(c_out[s.u], 16)

            pipeline(sp, J_C, [(0, c_store)])

            def f_load(s):
                before(sp, f_out[s.u], s.h, 1, 16)
                sp.dma_start(xF[s.u], tiles(x3_d, s.t)).then_inc(f_x[s.u], 16)

            def f_store(s):
                sp.wait_ge(f_o, s.t + 1)
                sp.dma_start(tiles(out, s.t), xF[s.u]).then_inc(f_out[s.u], 16)

            pipeline(sp, T, [(-1, f_load), (0, f_store)])
            for u in range(2):
                sp.wait_ge(f_out[u], 16 * HALF)

        @block.gpsimd
        def _(pool):
            for m in (eyeF, onesF):
                pool.memset(m[:], 0.0 if m is eyeF else 1.0).then_inc(const_steps, 1)
            pool.memset(triH[:], 1.0).then_inc(const_steps, 1)
            pool.memset(onesH[:], 1.0).then_inc(consts, 1)
            pool.memset(powh[:], -0.5).then_inc(consts, 1)
            pool.memset(powm[:], -1.0).then_inc(consts, 1)
            pool.iota(iotaI[:], pattern=[[1, P]], base=0, channel_multiplier=0).then_inc(consts, 1)
            pool.iota(tokidI[:], pattern=[[P, T]], base=0, channel_multiplier=1).then_inc(consts, 1)
            pool.wait_ge(const_steps, 3)
            pool.affine_select(out=eyeF[:], in_=eyeF[:], compare_op=ALU.not_equal, fill=1.0, base=0,
                               pattern=[[-1, P]], channel_multiplier=1).then_inc(consts, 1)
            pool.affine_select(out=triH[:], in_=triH[:], compare_op=ALU.is_gt, fill=0.0, base=0,
                               pattern=[[1, P]], channel_multiplier=-1).then_inc(consts, 1)
            NC = 7
            pool.wait_ge(consts, NC)

            def rsqrt_chain(done, n0, src, eps, tmp, dst, last):
                pool.tensor_scalar(tmp, src, eps, None, ALU.add).then_inc(done, 1)
                alone(pool, "pool", done, n0 + 1)
                pool.tensor_tensor(dst, tmp, powh[:], ALU.pow).then_inc(last, 1)

            def small_x(s):
                m, w, n0 = mv[s.u], smA[s.u], s.t * 9
                alone(pool, "pool", x_mom, s.t + 1)
                before(pool, x_mag, s.t, 2)
                before(pool, sw_done, s.t, 2, CA)
                before(pool, sil_done, s.t, 2, CA)
                pool.sem_inc(passed["pool"], 1)
                rsqrt_chain(smA_s, n0, m[:, 1:2], EPS_LN, w[:, 0:1], w[:, 1:2], smA_s)
                alone(pool, "pool", smA_s, n0 + 2)
                pool.tensor_scalar(w[:, 2:3], m[:, 1:2], w[:, 1:2], w[:, 1:2], ALU.mult, ALU.mult).then_inc(smA_s, 1)
                alone(pool, "pool", smA_s, n0 + 3)
                rsqrt_chain(smA_s, n0 + 3, w[:, 2:3], EPS_RMS, w[:, 3:4], w[:, 4:5], smA_s)
                alone(pool, "pool", smA_s, n0 + 5)
                pool.tensor_tensor(w[:, 5:6], w[:, 1:2], w[:, 4:5], ALU.mult).then_inc(smA_s, 1)
                alone(pool, "pool", smA_s, n0 + 6)
                alone(pool, "pool", x_max, s.t + 1)
                pool.tensor_scalar(w[:, 6:7], xmax[s.u][:], w[:, 5:6], EPS_Q, ALU.mult, ALU.max).then_inc(smA_s, 1)
                alone(pool, "pool", smA_s, n0 + 7)
                if isinstance(s.t, int) and s.t == 0:
                    pool.wait_ge(thr_done, 2)
                pool.tensor_scalar(dqx[s.u][:], w[:, 6:7], wmean[:, 0:1], 1.0 / 127.0, ALU.mult, ALU.mult).then_inc(smA_s, 1)
                pool.tensor_tensor(w[:, 7:8], w[:, 6:7], powm[:], ALU.pow).then_inc(smA_s, 1)
                alone(pool, "pool", smA_s, n0 + 9)
                pool.tensor_scalar(cx[s.u][:], w[:, 7:8], w[:, 5:6], 127.0, ALU.mult, ALU.mult).then_inc(x_small, 1)

            def gains(s):
                alone(pool, "pool", sw_done, (s.t + 1) * CA)
                before(pool, d_q, s.t, 2)
                pool.sem_inc(passed["pool"], 1)
                if isinstance(s.t, int) and s.t == 0:
                    pool.wait_ge(gd_in, 16)
                pool.tensor_tensor(swg[s.u], sw[s.u], gd, ALU.mult).then_inc(swg_done, 1)

            def small_g(s):
                w, n0 = smG[s.u], s.t * 6
                alone(pool, "pool", sq_done, s.t + 1)
                alone(pool, "pool", g_max, s.t + 1)
                before(pool, d_mag, s.t, 2)
                before(pool, x1_done, s.t, 2)
                pool.sem_inc(passed["pool"], 1)
                pool.tensor_scalar(w[:, 0:1], ssq[s.u][:], 1.0 / IA, EPS_RMS, ALU.mult, ALU.add).then_inc(smG_s, 1)
                alone(pool, "pool", smG_s, n0 + 1)
                pool.tensor_tensor(w[:, 1:2], w[:, 0:1], powh[:], ALU.pow).then_inc(smG_s, 1)
                alone(pool, "pool", smG_s, n0 + 2)
                pool.tensor_scalar(w[:, 2:3], gmax[s.u][:], w[:, 1:2], EPS_Q, ALU.mult, ALU.max).then_inc(smG_s, 1)
                alone(pool, "pool", smG_s, n0 + 3)
                pool.tensor_scalar(dqg[s.u][:], w[:, 2:3], wmean[:, 1:2], 1.0 / 127.0, ALU.mult, ALU.mult).then_inc(smG_s, 1)
                pool.tensor_tensor(w[:, 3:4], w[:, 2:3], powm[:], ALU.pow).then_inc(smG_s, 1)
                alone(pool, "pool", smG_s, n0 + 5)
                pool.tensor_scalar(w[:, 4:5], w[:, 3:4], w[:, 1:2], 127.0, ALU.mult, ALU.mult).then_inc(smG_s, 1)
                alone(pool, "pool", smG_s, n0 + 6)
                pool.tensor_copy(cg[s.u][:], w[:, 4:5]).then_inc(g_small, 1)

            def small_b(s):
                alone(pool, "pool", mo1, s.t + 1)
                rsqrt_chain(smB_s, s.t, mv1[:, 1:2], EPS_LN, var1[:], rstd1[:], rs1)

            pool.wait_ge(thr_done, 2)
            for k in range(KD):
                if k >= 2:
                    pool.wait_ge(tern_done, k - 1)
                pool.tensor_scalar(negs[k % 2], wg32[k], thr[:, 1:2], None, ALU.is_lt).then_inc(neg_done, 1)
            pool.wait_ge(thr_done, 4)
            for half in range(2):
                pool.wait_ge(tern_done, KD - 1 + half)
                pool.tensor_scalar(negs[half], wd32[:, half * OG:(half + 1) * OG], thr[:, 3:4], None, ALU.is_lt).then_inc(neg_done, 1)

            pipeline(pool, T, [(0, gains), (-2, small_x), (0, small_g), (1, small_b)])

            def gather(s, order, done, index, inv, dst, table):
                pool.tensor_copy(index[s.u][:], inv[:, bass.ds(s.t, 1)]).then_inc(order, 1)
                alone(pool, "pool", order, s.t + 1)
                pool.indirect_dma_start(out=dst[s.u][:] if dst is rows else dst[s.u], out_offset=None, in_=table[:, :],
                                        in_offset=bass.IndirectOffsetOnAxis(ap=index[s.u][:], axis=0)).then_inc(done[s.u], 16)

            for u in range(2):
                pool.wait_ge(hb_out[u], 16 * HALF)
            pool.wait_ge(routeB, 1)

            def b_gather(s):
                if not (isinstance(s.t, int) and s.t < 2):
                    alone(pool, "pool", b_T, s.t - 1)
                    alone(pool, "pool", b_rows[s.u], s.h * 16)
                gather(s, b_idx, b_rows, idx, invB, rows, hB_d)

            pipeline(pool, J_B, [(-1, b_gather)])

            for u in range(2):
                pool.wait_ge(b_out[u], 16 * ((J_B + 1 - u) // 2))
                pool.wait_ge(b_rows[u], 16 * ((J_B + 1 - u) // 2))

            def s_gather(s):
                if not (isinstance(s.t, int) and s.t < 2):
                    alone(pool, "pool", s_x2, s.t - 1)
                    alone(pool, "pool", s_y[s.u], s.h * 16)
                gather(s, s_idx, s_y, idx, posB, yS, yB_d)

            def s_rstd(s):
                alone(pool, "pool", s_mo, s.t + 1)
                rsqrt_chain(s_small, s.t, mv1[:, 1:2], EPS_LN, var1[:], rstd1[:], s_rs)

            pipeline(pool, T, [(-2, s_gather), (-1, s_rstd)])

            for u in range(2):
                pool.wait_ge(s_hout[u], 16 * HALF)
                pool.wait_ge(s_y[u], 16 * HALF)
            pool.wait_ge(routeC, 1)

            def c_gather(s):
                if not (isinstance(s.t, int) and s.t < 2):
                    alone(pool, "pool", c_T, s.t - 1)
                    alone(pool, "pool", c_rows[s.u], s.h * 16)
                gather(s, c_idx, c_rows, idx, invC, rows, hC_d)

            pipeline(pool, J_C, [(-1, c_gather)])

            for u in range(2):
                pool.wait_ge(c_out[u], 16 * ((J_C + 1 - u) // 2))
                pool.wait_ge(c_rows[u], 16 * ((J_C + 1 - u) // 2))

            def f_gather(s):
                if not (isinstance(s.t, int) and s.t < 2):
                    alone(pool, "pool", f_o, s.t - 1)
                    alone(pool, "pool", f_y1[s.u], s.h * 16)
                    alone(pool, "pool", f_y2[s.u], s.h * 16)
                pool.tensor_copy(idx[s.u][:], posC[0][:, bass.ds(s.t, 1)]).then_inc(f_idx, 1)
                pool.tensor_copy(idy[s.u][:], posC[1][:, bass.ds(s.t, 1)]).then_inc(f_idx, 1)
                alone(pool, "pool", f_idx, s.t * 2 + 2)
                for i, dst, done in ((idx, y1F, f_y1), (idy, y2F, f_y2)):
                    pool.indirect_dma_start(out=dst[s.u], out_offset=None, in_=yC_d[:, :],
                                            in_offset=bass.IndirectOffsetOnAxis(ap=i[s.u][:], axis=0)).then_inc(done[s.u], 16)

            pipeline(pool, T, [(0, f_gather)])

        @block.scalar
        def _(act):
            for k in range(KD):
                act.wait_ge(wg_in[k], 16)
                act.activation(wgT[k], wg32[k], ACT.Abs, accum_out=asum[:, k:k + 1]).then_inc(abs_done, 1)
            act.wait_ge(wd_in, 16)
            act.activation(wdT, wd32, ACT.Abs, accum_out=asum[:, KD:KD + 1]).then_inc(abs_done, 1)
            act.wait_ge(gains_in, 32)
            act.activation(gw_hi[:], gw32[:], ACT.Copy, scale=SCALE_C).then_inc(gw_done, 1)

            def x_round(s):
                act.wait_ge(x_small, s.t + 1)
                act.wait_ge(x_cen, s.t + 1)
                before(act, x_q, s.t, 2)
                act.activation(xmag[s.u], xcen[s.u], ACT.Copy, bias=MAGIC, scale=cx[s.u][:]).then_inc(x_mag, 1)

            def x_evac(s):
                act.wait_ge(x_T, s.t + 1)
                before(act, gu_done, s.t, 2, CA)
                act.copy(xqT[s.u], bank(4, 256).bitcast(BF16)).then_inc(x_ev, 1)

            def silu(s):
                for c in range(CA):
                    act.wait_ge(gu_done, s.t * CA + (c + 1))
                    if not (isinstance(s.t, int) and s.t == 0 and c < 2):
                        act.wait_ge(sw_done, s.t * CA + (c - 1))
                    act.activation(sil[c % 2], bank(c % 2, CW), ACT.Silu, scale=dqx[s.u][:]).then_inc(sil_done, 1)

            def square(s):
                act.wait_ge(sw_done, (s.t + 1) * CA)
                before(act, g_small, s.t, 2)
                before(act, sq_done, s.t, 1)
                act.activation(squares, sw[s.u], ACT.Square, accum_out=ssq[s.u][:]).then_inc(sq_done, 1)

            def d_round(s):
                act.wait_ge(g_small, s.t + 1)
                act.wait_ge(g_max, s.t + 1)
                act.activation(swg[s.u], swg[s.u], ACT.Copy, bias=MAGIC, scale=cg[s.u][:]).then_inc(d_mag, 1)

            def d_evac(s):
                act.wait_ge(d_T, s.t + 1)
                before(act, z_done, s.t, 2)
                act.copy(qdT[s.u], wide(5, IA // 2).bitcast(BF16)).then_inc(d_ev, 1)

            def h_hi(s):
                act.wait_ge(h_done, s.t + 1)
                before(act, hb_out[s.u], s.h, 1, 16)
                act.copy(rows[s.u][:, 0:D], hA).then_inc(hi_done, 1)

            def ctx_split(s):
                act.wait_ge(ctx_in[s.u], (s.h + 1) * 16)
                act.activation(c_hi[:, bass.ds(s.t * D, D)], wstage[s.u][:, 0:D], ACT.Copy, scale=SCALE_B).then_inc(ctx_hi, 1)

            act.wait_ge(tern_done, KD + 2)
            pipeline(act, T, [(0, silu), (-1, x_evac), (1, d_evac), (0, square), (-2, x_round), (0, d_round), (1, h_hi), (0, ctx_split)])

            def split_hi(s, q, u, h):
                act.wait_ge(w_in[u], (h + 1) * 16)
                act.activation(w_hi[:, bass.ds(q * CHUNK, CHUNK)], wstage[u][:], ACT.Copy, scale=SCALE_C).then_inc(whi_done, 1)

            def b_evac(s):
                act.wait_ge(b_T, s.t + 1)
                before(act, b_t, s.t, 2)
                act.copy(hT[s.u][:].rearrange("p a n -> p (a n)"), bank(0).bitcast(F16)).then_inc(b_ev, 1)

            def b_silu(s):
                act.wait_ge(b_t, s.t + 1)
                before(act, b_aT, s.t, 2)
                act.activation(bs[s.u], bank(1 + s.u), ACT.Silu, scale=1.0 / SCALE_B).then_inc(b_sil, 1)

            def b_split(s):
                act.wait_ge(b_aT, s.t + 1)
                before(act, b_y, s.t, 2)
                act.copy(bpT[s.u][:, 0, :], bank(3)).then_inc(b_hi, 1)

            act.wait_ge(z_done, T)
            act.wait_ge(x1_out[0], 16 * HALF)
            act.wait_ge(x1_out[1], 16 * HALF)
            pipeline(act, J_B, [(-1, b_evac), (0, b_silu), (0, b_split), (0, lambda s: split_hi(s, s.t, s.u, s.h))])

            def s_split(s):
                act.wait_ge(s_h, s.t + 1)
                before(act, s_hout[s.u], s.h, 1, 16)
                before(act, s_T, s.t, 2)
                act.copy(rows[s.u][:, 0:D], hS).then_inc(s_hi, 1)

            def s_evac(s):
                act.wait_ge(s_T, s.t + 1)
                before(act, s_gu, s.t, 2, 2)
                act.copy(hT[s.u][:].rearrange("p a n -> p (a n)"), bank(0).bitcast(F16)).then_inc(s_ev, 1)

            def s_silu(s):
                for c in range(2):
                    act.wait_ge(s_gu, s.t * 2 + (c + 1))
                    before(act, s_pT, s.t, 1)
                    act.activation(ss[:, c * CW:(c + 1) * CW], bank(1 + c, CW), ACT.Silu, scale=1.0 / SCALE_C).then_inc(s_sil, 1)

            def s_psplit(s):
                act.wait_ge(s_pT, s.t + 1)
                before(act, s_dn, s.t, 1)
                act.copy(spT[:, 0, :], wide(5, ISP)).then_inc(s_phi, 1)

            def s_w(s):
                q, odd = s.t + J_B, J_B % 2
                c = s.u + odd
                split_hi(s, q, c % 2, s.h + (J_B // 2 + c // 2))

            act.wait_ge(b_y, J_B)
            pipeline(act, T, [(-1, s_split), (-1, s_evac), (0, s_silu), (0, s_psplit), (0, s_w)])

            act.wait_ge(exp_done, 1)
            act.activation(rt[:], rt[:], ACT.Exp).then_inc(exp_done, 1)
            act.wait_ge(s_dn, T)
            for q in range(J_B + T, CHUNKS):
                split_hi(None, q, q % 2, q // 2)

            def c_evac(s):
                act.wait_ge(c_T, s.t + 1)
                before(act, c_gu, s.t, 2)
                act.copy(hT[s.u][:].rearrange("p a n -> p (a n)"), bank(0).bitcast(F16)).then_inc(c_ev, 1)

            def c_silu(s):
                act.wait_ge(c_gu, s.t + 1)
                before(act, c_pT, s.t, 2)
                act.activation(cs[s.u][:, 0:IC], bank(1 + s.u, IC), ACT.Silu, scale=1.0 / SCALE_C).then_inc(c_sil, 1)

            def c_split(s):
                act.wait_ge(c_pT, s.t + 1)
                before(act, c_dn, s.t, 2)
                act.copy(cpT[s.u][:, 0, :], bank(5, ICP)).then_inc(c_hi_s, 1)

            pipeline(act, J_C, [(-1, c_evac), (0, c_silu), (0, c_split)])

        @block.vector
        def _(dve):
            r = [0]

            def step(ins):
                r[0] += 1
                ins.then_inc(route, 1)
                dve.wait_ge(route, r[0])

            def routing(experts, tiles_, chosen, inv, experts_of, pos, done, b_rank, b_inv, n_mm, n_inv, n_sel):
                E = experts
                step(dve.memset(ohsum[:, 0, 0:E], 0.0))
                for t in range(T):
                    step(dve.tensor_tensor(ohsum[:, t + 1, 0:E], ohsum[:, t, 0:E], oh[:, t, 0:E], ALU.add))
                dve.sem_inc(route_mm, 1)
                dve.wait_ge(route_mm, n_mm + 2)
                for t in range(0, 1):
                    step(dve.tensor_copy(rank[:, :, 0:E], bank(b_rank, (T + 1) * E).rearrange("p (t e) -> p t e", e=E)))
                step(dve.tensor_scalar(eI[:, 0:E], rank[:, T, 0:E], float(P - 1), None, ALU.add))
                step(dve.tensor_scalar(eI[:, 0:E], eI[:, 0:E], 7, None, ALU.logical_shift_right))
                step(dve.tensor_copy(eF[:, 0, 0:E], eI[:, 0:E]))
                step(dve.tensor_copy(eF[:, 1, 0:E], eF[:, 0, 0:E]))
                for e in range(1, E):
                    step(dve.tensor_tensor(eF[:, 1, e:e + 1], eF[:, 1, e:e + 1], eF[:, 1, e - 1:e], ALU.add))
                step(dve.tensor_tensor(eF[:, 2, 0:E], eF[:, 1, 0:E], eF[:, 0, 0:E], ALU.subtract))
                step(dve.tensor_scalar(jF[0][:, 0:tiles_], iotaF[:, 0:tiles_], eF[:, 1, 0:1], None, ALU.is_ge))
                for e in range(1, E):
                    step(dve.scalar_tensor_tensor(out=jF[0][:, 0:tiles_], in0=iotaF[:, 0:tiles_], scalar=eF[:, 1, e:e + 1],
                                                  in1=jF[0][:, 0:tiles_], op0=ALU.is_ge, op1=ALU.add))
                step(dve.tensor_scalar(experts_of[:], jF[0][:, 0:tiles_], float(E - 1), None, ALU.min))
                for c, one in enumerate(chosen):
                    step(dve.tensor_tensor(rt2[:, :, 0:E], one[:, :, 0:E], rank[:, 0:T, 0:E], ALU.mult))
                    step(dve.tensor_reduce(rF[:, 0, :], rt2[:, :, 0:E], AX.X, ALU.add))
                    step(dve.tensor_tensor(rt2[:, :, 0:E], one[:, :, 0:E], eF[:, 2:3, 0:E].broadcast_to([P, T, E]), ALU.mult))
                    step(dve.tensor_reduce(rF[:, 1, :], rt2[:, :, 0:E], AX.X, ALU.add))
                    step(dve.tensor_copy(rI[:, 0, :], rF[:, 0, :]))
                    step(dve.tensor_scalar(rI[:, 1, :], rI[:, 0, :], 7, None, ALU.logical_shift_right))
                    step(dve.tensor_copy(rF[:, 2, :], rI[:, 1, :]))
                    step(dve.scalar_tensor_tensor(out=rF[:, 3, :], in0=rF[:, 2, :], scalar=-float(P), in1=rF[:, 0, :],
                                                  op0=ALU.mult, op1=ALU.add))
                    step(dve.tensor_tensor(rF[:, 2, :], rF[:, 2, :], rF[:, 1, :], ALU.add))
                    step(dve.scalar_tensor_tensor(out=posF[:], in0=rF[:, 2, :], scalar=float(P), in1=rF[:, 3, :],
                                                  op0=ALU.mult, op1=ALU.add))
                    step(dve.tensor_copy(pos[c][:], posF[:]))
                    for t in range(T):
                        n = c * T + t
                        if n >= 2:
                            dve.wait_ge(inv_mm, n_inv + n - 1)
                        dve.tensor_scalar(selR[n % 2][:], iotaF[:], rF[:, 3, t:t + 1], None, ALU.is_equal).then_inc(sel_done, 1)
                        dve.tensor_scalar(selJ[n % 2][:, 0:tiles_], iotaF[:, 0:tiles_], rF[:, 2, t:t + 1], tokid[:, t:t + 1],
                                          ALU.is_equal, ALU.mult).then_inc(sel_done, 1)
                dve.wait_ge(inv_mm, n_inv + len(chosen) * T)
                step(dve.tensor_copy(inv[:], bank(b_inv, tiles_)))
                dve.sem_inc(done, 1)

            dve.wait_ge(consts, 7)
            dve.tensor_copy(eyeH[:], eyeF[:]).then_inc(const_steps, 1)
            dve.tensor_copy(eyeB[:], eyeF[:]).then_inc(const_steps, 1)
            step(dve.tensor_copy(iotaF[:], iotaI[:]))
            step(dve.tensor_copy(tokid[:], tokidI[:]))

            dve.wait_ge(tok_in, 16)
            step(dve.tensor_copy(tokF[:], tokI[:]))
            step(dve.memset(oh12[0][:, :, 0:1], 1.0))
            for e in range(1, E_B):
                step(dve.tensor_scalar(oh12[0][:, :, e], tokF[:], float(e * PER_EXPERT), None, ALU.is_ge))
            for e in range(E_B - 1):
                step(dve.tensor_tensor(oh12[0][:, :, e], oh12[0][:, :, e], oh12[0][:, :, e + 1], ALU.subtract))
            step(dve.tensor_copy(oh[:, :, 0:E_B], oh12[0][:, :, 0:E_B]))
            routing(E_B, J_B, oh12[:1], invB, expB, [posB], routeB, 6, 7, 0, 0, 0)

            dve.wait_ge(gains_in, 32)
            dve.wait_ge(gw_done, 1)
            dve.scalar_tensor_tensor(out=gw_lo[:], in0=gw32[:], scalar=SCALE_C, in1=gw_hi[:],
                                     op0=ALU.mult, op1=ALU.subtract).then_inc(gw_done, 1)
            dve.wait_ge(tot_done, 1)
            step(dve.tensor_reduce(wmean[:, 0:1], bank(7, KD, 128), AX.X, ALU.add))
            step(dve.tensor_scalar(wmean[:, 0:1], wmean[:, 0:1], 1.0 / (OG * D), EPS_Q, ALU.mult, ALU.max))
            dve.tensor_scalar(thr[:, 0:1], wmean[:, 0:1], 0.5, None, ALU.mult).then_inc(thr_done, 1)
            dve.tensor_scalar(thr[:, 1:2], wmean[:, 0:1], -0.5, None, ALU.mult).then_inc(thr_done, 1)
            step(dve.tensor_scalar(wmean[:, 1:2], bank(7, 1, 128 + KD), 1.0 / (IA * D), EPS_Q, ALU.mult, ALU.max))
            dve.tensor_scalar(thr[:, 2:3], wmean[:, 1:2], 0.5, None, ALU.mult).then_inc(thr_done, 1)
            dve.tensor_scalar(thr[:, 3:4], wmean[:, 1:2], -0.5, None, ALU.mult).then_inc(thr_done, 1)

            def x_norm(s):
                dve.wait_ge(x_in[s.u], (s.h + 1) * 16)
                before(dve, x_small, s.t, 2)
                dve.bn_stats(stats[s.u][:], xin[s.u]).then_inc(x_stats, 1)
                alone(dve, "dve", x_stats, s.t + 1)
                dve.bn_aggr(mv[s.u][:], stats[s.u][:]).then_inc(x_mom, 1)
                before(dve, x_mag, s.t, 2)
                dve.wait_ge(x_mom, s.t + 1)
                if isinstance(s.t, int) and s.t == 0:
                    dve.wait_ge(gains_in, 32)
                dve.scalar_tensor_tensor(out=xcen[s.u], in0=xin[s.u], scalar=mv[s.u][:, 0:1], in1=gg,
                                         op0=ALU.subtract, op1=ALU.mult).then_inc(x_cen, 1)
                dve.wait_ge(x_cen, s.t + 1)
                dve.tensor_reduce(xmax[s.u][:], xcen[s.u], AX.X, ALU.max, apply_absolute_value=True).then_inc(x_max, 1)

            def x_int(s):
                dve.wait_ge(x_mag, s.t + 1)
                before(dve, x_T, s.t, 2)
                dve.tensor_scalar(xq[s.u], xmag[s.u], MAGIC, 127.0, ALU.subtract, ALU.min).then_inc(x_q, 1)

            def swiglu(s):
                for c in range(CA):
                    dve.wait_ge(sil_done, s.t * CA + (c + 1))
                    if c == 0:
                        before(dve, sq_done, s.t, 2)
                        before(dve, swg_done, s.t, 2)
                    dve.scalar_tensor_tensor(out=sw[s.u][:, c * CW:(c + 1) * CW], in0=bank(2 + c % 2, CW), scalar=dqx[s.u][:],
                                             in1=sil[c % 2], op0=ALU.mult, op1=ALU.mult).then_inc(sw_done, 1)

            def g_absmax(s):
                dve.wait_ge(swg_done, s.t + 1)
                before(dve, g_small, s.t, 2)
                dve.tensor_reduce(gmax[s.u][:], swg[s.u], AX.X, ALU.max, apply_absolute_value=True).then_inc(g_max, 1)

            def d_int(s):
                dve.wait_ge(d_mag, s.t + 1)
                before(dve, d_T, s.t, 2)
                dve.tensor_scalar(qd[s.u], swg[s.u], MAGIC, 127.0, ALU.subtract, ALU.min).then_inc(d_q, 1)

            def residual1(s):
                dve.wait_ge(z_done, s.t + 1)
                dve.wait_ge(xr_in[s.u], (s.h + 1) * 16)
                before(dve, x1_out[s.u], s.h, 1, 16)
                before(dve, h_done, s.t, 2)
                dve.scalar_tensor_tensor(out=x1[s.u], in0=bank(7), scalar=dqg[s.u][:], in1=xres[s.u],
                                         op0=ALU.mult, op1=ALU.add).then_inc(x1_done, 1)
                dve.wait_ge(x1_done, s.t + 1)
                before(dve, rs1, s.t, 1)
                dve.bn_stats(stats1[:], x1[s.u]).then_inc(st1, 1)
                alone(dve, "dve", st1, s.t + 1)
                before(dve, h_done, s.t, 1)
                dve.sem_inc(passed["dve"], 1)
                dve.bn_aggr(mv1[:], stats1[:]).then_inc(mo1, 1)

            def norm1(s):
                dve.wait_ge(rs1, s.t + 1)
                before(dve, hi_done, s.t, 1)
                before(dve, lo_done, s.t, 1)
                dve.tensor_scalar(hA, x1[s.u], mv1[:, 0:1], rstd1[:], ALU.subtract, ALU.mult).then_inc(h_done, 1)
                dve.wait_ge(hi_done, s.t + 1)
                before(dve, hb_out[s.u], s.h, 1, 16)
                dve.tensor_tensor(rows[s.u][:, D:2 * D], hA, rows[s.u][:, 0:D], ALU.subtract).then_inc(lo_done, 1)

            def ctx_rest(s):
                dve.wait_ge(ctx_hi, s.t + 1)
                at = bass.ds(s.t * D, D)
                dve.scalar_tensor_tensor(out=c_lo[:, at], in0=wstage[s.u][:, 0:D], scalar=SCALE_B, in1=c_hi[:, at],
                                         op0=ALU.mult, op1=ALU.subtract).then_inc(ctx_lo, 1)

            dve.wait_ge(abs_done, KD + 1)
            for k in range(KD):
                dve.wait_ge(neg_done, k + 1)
                dve.scalar_tensor_tensor(out=wgT[k], in0=wg32[k], scalar=thr[:, 0:1], in1=negs[k % 2],
                                         op0=ALU.is_gt, op1=ALU.subtract).then_inc(tern_done, 1)
            for half in range(2):
                at = slice(half * OG, (half + 1) * OG)
                dve.wait_ge(neg_done, KD + half + 1)
                dve.scalar_tensor_tensor(out=wdT[:, at], in0=wd32[:, at], scalar=thr[:, 2:3], in1=negs[half],
                                         op0=ALU.is_gt, op1=ALU.subtract).then_inc(tern_done, 1)

            pipeline(dve, T, [(-1, x_int), (0, swiglu), (-2, x_norm), (0, g_absmax), (1, residual1), (0, d_int), (1, norm1), (0, ctx_rest)])

            def split_lo(q, u):
                at = bass.ds(q * CHUNK, CHUNK)
                dve.wait_ge(whi_done, q + 1)
                dve.scalar_tensor_tensor(out=w_lo[:, at], in0=wstage[u][:], scalar=SCALE_C, in1=w_hi[:, at],
                                         op0=ALU.mult, op1=ALU.subtract).then_inc(wlo_done, 1)

            def b_prod(s):
                dve.wait_ge(b_sil, s.t + 1)
                dve.tensor_tensor(bs[s.u], bank(1 + s.u), bs[s.u], ALU.mult).then_inc(b_a, 1)

            def b_rest(s):
                dve.wait_ge(b_hi, s.t + 1)
                dve.tensor_tensor(bpT[s.u][:, 1, :], bank(3), bpT[s.u][:, 0, :], ALU.subtract).then_inc(b_lo, 1)

            def b_rows_out(s):
                dve.wait_ge(b_y, s.t + 1)
                before(dve, b_out[s.u], s.h, 1, 16)
                dve.tensor_copy(yrow[s.u][:], bank(4 + s.u)).then_inc(b_yev, 1)

            pipeline(dve, J_B, [(0, b_prod), (0, b_rest), (1, b_rows_out), (0, lambda s: split_lo(s.t, s.u))])

            def residual2(s):
                dve.wait_ge(s_x[s.u], (s.h + 1) * 16)
                dve.wait_ge(s_y[s.u], (s.h + 1) * 16)
                dve.scalar_tensor_tensor(out=xS[s.u], in0=yS[s.u], scalar=1.0 / SCALE_B ** 2, in1=xS[s.u],
                                         op0=ALU.mult, op1=ALU.add).then_inc(s_x2, 1)
                dve.wait_ge(s_x2, s.t + 1)
                before(dve, s_rs, s.t, 1)
                dve.bn_stats(stats1[:], xS[s.u]).then_inc(s_st, 1)
                alone(dve, "dve", s_st, s.t + 1)
                before(dve, s_h, s.t, 1)
                dve.sem_inc(passed["dve"], 1)
                dve.bn_aggr(mv1[:], stats1[:]).then_inc(s_mo, 1)

            def norm2(s):
                dve.wait_ge(s_rs, s.t + 1)
                before(dve, s_hi, s.t, 1)
                before(dve, s_lo, s.t, 1)
                dve.tensor_scalar(hS, xS[s.u], mv1[:, 0:1], rstd1[:], ALU.subtract, ALU.mult).then_inc(s_h, 1)
                dve.wait_ge(s_hi, s.t + 1)
                dve.tensor_tensor(rows[s.u][:, D:2 * D], hS, rows[s.u][:, 0:D], ALU.subtract).then_inc(s_lo, 1)

            def keep_logits(s):
                dve.wait_ge(s_lg, s.t + 1)
                dve.tensor_scalar(logits[:, bass.ds(s.t, 1), :].rearrange("p a e -> p (a e)"), bank(6, E_C, 256),
                                  1.0 / SCALE_C, None, ALU.mult).then_inc(s_lgev, 1)

            def s_prod(s):
                for c in range(2):
                    dve.wait_ge(s_sil, s.t * 2 + (c + 1))
                    at = ss[:, c * CW:(c + 1) * CW]
                    dve.tensor_tensor(at, bank(3 + c, CW), at, ALU.mult).then_inc(s_p, 1)

            def s_rest(s):
                dve.wait_ge(s_phi, s.t + 1)
                dve.tensor_tensor(spT[:, 1, :], wide(5, ISP), spT[:, 0, :], ALU.subtract).then_inc(s_plo, 1)

            def residual3(s):
                dve.wait_ge(s_dn, s.t + 1)
                dve.wait_ge(s_xr[s.u], (s.h + 1) * 16)
                dve.scalar_tensor_tensor(out=yrow[s.u][:], in0=bank(7), scalar=1.0 / SCALE_C ** 2, in1=yrow[s.u][:],
                                         op0=ALU.mult, op1=ALU.add).then_inc(s_x3, 1)

            def s_w(s):
                split_lo(s.t + J_B, (s.u + J_B) % 2)

            dve.wait_ge(b_y, J_B)
            dve.memset(ss[:, IS:ISP], 0.0).then_inc(s_pad, 1)
            pipeline(dve, T, [(-1, residual2), (-1, norm2), (0, keep_logits), (0, s_prod), (0, s_rest), (0, s_w), (1, residual3)])

            dve.wait_ge(s_lgev, T)
            step(dve.tensor_copy(rt2[:], logits[:]))
            iota_e = iotaF[:, 0:E_C].rearrange("p (a e) -> p a e", a=1).broadcast_to([P, T, E_C])

            def over_e(ap):
                return ap.rearrange("p (t a) -> p t a", a=1).broadcast_to([P, T, E_C])

            for c in range(2):
                step(dve.tensor_reduce(m12[:, c, :], rt2[:], AX.X, ALU.max))
                step(dve.tensor_tensor(oh12[c][:], rt2[:], over_e(m12[:, c, :]), ALU.not_equal))
                step(dve.scalar_tensor_tensor(out=oh12[c][:].rearrange("p t e -> p (t e)"), in0=oh12[c][:].rearrange("p t e -> p (t e)"),
                                              scalar=64.0, in1=iota_e, op0=ALU.mult, op1=ALU.add) if False else
                     dve.tensor_scalar(oh12[c][:], oh12[c][:], 64.0, None, ALU.mult))
                step(dve.tensor_tensor(oh12[c][:], oh12[c][:], iota_e, ALU.add))
                step(dve.tensor_reduce(wsum[:], oh12[c][:], AX.X, ALU.min))
                step(dve.tensor_tensor(oh12[c][:], iota_e, over_e(wsum[:]), ALU.is_equal))
                if c == 0:
                    step(dve.tensor_scalar(rt[:], oh12[c][:], -3.0e38, None, ALU.mult))
                    step(dve.tensor_tensor(rt2[:], rt2[:], rt[:], ALU.add))
            step(dve.tensor_tensor(rt[:], logits[:], over_e(m12[:, 0, :]), ALU.subtract))
            dve.sem_inc(exp_done, 1)
            step(dve.tensor_tensor(oh[:], oh12[0][:], oh12[1][:], ALU.add))
            routing(E_C, J_C, oh12, invC, expC, posC, routeC, 5, 6, 2, T, 2 * T)
            dve.wait_ge(exp_done, 2)
            step(dve.tensor_reduce(wsum[:], rt[:], AX.X, ALU.add))
            step(dve.reciprocal(wsum[:], wsum[:]))
            step(dve.tensor_scalar(wsum[:], wsum[:], 1.0 / SCALE_C ** 2, None, ALU.mult))
            for c in range(2):
                step(dve.tensor_tensor(rt2[:], oh12[c][:], rt[:], ALU.mult))
                step(dve.tensor_reduce(posF[:], rt2[:], AX.X, ALU.add))
                step(dve.tensor_tensor(wtop[c][:], posF[:], wsum[:], ALU.mult))
            for q in range(J_B + T, CHUNKS):
                split_lo(q, q % 2)

            def c_prod(s):
                dve.wait_ge(c_sil, s.t + 1)
                dve.tensor_tensor(cs[s.u][:, 0:IC], bank(3 + s.u, IC), cs[s.u][:, 0:IC], ALU.mult).then_inc(c_p, 1)

            def c_rest(s):
                dve.wait_ge(c_hi_s, s.t + 1)
                dve.tensor_tensor(cpT[s.u][:, 1, :], bank(5, ICP), cpT[s.u][:, 0, :], ALU.subtract).then_inc(c_lo_s, 1)

            def c_rows_out(s):
                dve.wait_ge(c_dn, s.t + 1)
                before(dve, c_out[s.u], s.h, 1, 16)
                dve.tensor_copy(yrow[s.u][:], bank(6 + s.u)).then_inc(c_yev, 1)

            dve.wait_ge(s_x3out[0], 16 * HALF)
            dve.wait_ge(s_x3out[1], 16 * HALF)
            dve.wait_ge(s_dn, T)
            for u in range(2):
                dve.memset(cs[u][:, IC:ICP], 0.0).then_inc(pad_done, 1)
            pipeline(dve, J_C, [(0, c_prod), (0, c_rest), (1, c_rows_out)])

            def f_first(s):
                dve.wait_ge(f_x[s.u], (s.h + 1) * 16)
                dve.wait_ge(f_y1[s.u], (s.h + 1) * 16)
                dve.scalar_tensor_tensor(out=xF[s.u], in0=y1F[s.u], scalar=wtop[0][:, bass.ds(s.t, 1)], in1=xF[s.u],
                                         op0=ALU.mult, op1=ALU.add).then_inc(f_a, 1)
                dve.wait_ge(f_a, s.t + 1)
                dve.wait_ge(f_y2[s.u], (s.h + 1) * 16)
                dve.scalar_tensor_tensor(out=xF[s.u], in0=y2F[s.u], scalar=wtop[1][:, bass.ds(s.t, 1)], in1=xF[s.u],
                                         op0=ALU.mult, op1=ALU.add).then_inc(f_o, 1)

            pipeline(dve, T, [(0, f_first)])

        @block.tensor
        def _(pe):
            def route_sums(experts, n_mm, b):
                E = experts
                pe.wait_ge(route_mm, n_mm + 1)
                pe.matmul(bank(b, (T + 1) * E), onesH[:], ohsum[:, :, 0:E], start=True, stop=False)
                pe.matmul(bank(b, T * E), triH[:], oh[:, :, 0:E], start=False, stop=True).then_inc(route_mm, 1)

            def route_inverse(tiles_, count, b, n_inv, n_sel):
                for n in range(count):
                    pe.wait_ge(sel_done, n_sel + 2 * n + 2)
                    pe.matmul(bank(b, tiles_), selR[n % 2][:], selJ[n % 2][:, 0:tiles_],
                              start=(n == 0), stop=(n == count - 1)).then_inc(inv_mm, 1)

            pe.wait_ge(consts, 7)
            pe.wait_ge(const_steps, 5)
            route_sums(E_B, 0, 6)
            route_inverse(J_B, T, 7, 0, 0)
            pe.wait_ge(abs_done, KD + 1)
            pe.wait_ge(routeB, 1)
            pe.matmul(bank(7, KD + 1, 128), onesF[:], asum[:], start=True, stop=True).then_inc(tot_done, 1)

            def x_turn(s):
                pe.wait_ge(x_q, s.t + 1)
                before(pe, x_ev, s.t, 1)
                for k in range(KD):
                    mm = pe.transpose(bank(4, 256).bitcast(BF16)[:, k * P:(k + 1) * P], xq[s.u][:, k * P:(k + 1) * P], eyeB[:])
                mm.then_inc(x_T, 1)

            def gate_up(s):
                pe.wait_ge(x_ev, s.t + 1)
                for c in range(CA):
                    if not (isinstance(s.t, int) and s.t == 0 and c < 2):
                        pe.wait_ge(sw_done, s.t * CA + (c - 1))
                    for half in range(2):
                        at = half * IA + c * CW
                        for k in range(KD):
                            mm = pe.matmul(bank(2 * half + c % 2, CW), xqT[s.u][:, k * P:(k + 1) * P], wgT[k][:, at:at + CW],
                                           start=(k == 0), stop=(k == KD - 1))
                    mm.then_inc(gu_done, 1)

            def d_turn(s):
                pe.wait_ge(d_q, s.t + 1)
                before(pe, d_ev, s.t, 1)
                for k in range(KI):
                    mm = pe.transpose(wide(5, IA // 2).bitcast(BF16)[:, k * P:(k + 1) * P], qd[s.u][:, k * P:(k + 1) * P], eyeB[:])
                mm.then_inc(d_T, 1)

            def down(s):
                pe.wait_ge(d_ev, s.t + 1)
                before(pe, x1_done, s.t, 1)
                for k in range(KI):
                    mm = pe.matmul(bank(7), qdT[s.u][:, k * P:(k + 1) * P], wdT[:, k * D:(k + 1) * D],
                                   start=(k == 0), stop=(k == KI - 1))
                mm.then_inc(z_done, 1)

            pe.wait_ge(tern_done, KD + 2)
            pipeline(pe, T, [(0, gate_up), (-1, x_turn), (1, d_turn), (1, down)])

            def turn_rows(s, rows_in, evacuated, done):
                pe.wait_ge(rows_in, (s.h + 1) * 16)
                before(pe, evacuated, s.t, 1)
                for k in range(2 * KD):
                    mm = pe.transpose(bank(0).bitcast(F16)[:, k * P:(k + 1) * P], rows[s.u][:, k * P:(k + 1) * P], eyeH[:])
                mm.then_inc(done, 1)

            def split_product(to, a, w, steps):
                for k in range(steps):
                    for n, (pa, pw) in enumerate(((0, 0), (0, 1), (1, 0))):
                        mm = pe.matmul(to, a(k, pa), w(k, pw), start=(k == 0 and n == 0), stop=(k == steps - 1 and n == 2))
                return mm

            def b_turn(s):
                turn_rows(s, b_rows[s.u], b_ev, b_T)

            expert = {}

            def b_first(s):
                pe.wait_ge(b_ev, s.t + 1)
                before(pe, b_a, s.t, 2)
                pe.sem_inc(passed["pe"], 1)
                e = pe.value_load(expB[0:1, bass.ds(s.t, 1)], min_val=0, max_val=E_B - 1)
                split_product(bank(1 + s.u), lambda k, p: hT[s.u][:, p * KD + k, :],
                              lambda k, p: (c_hi, c_lo)[p][:, bass.ds(e * (KD * D) + k * D, D)], KD).then_inc(b_t, 1)

            def b_turn_a(s):
                pe.wait_ge(b_a, s.t + 1)
                before(pe, b_lo, s.t, 1)
                for k in range(KD):
                    mm = pe.transpose(bank(3, P, k * P), bs[s.u][:, k * P:(k + 1) * P], eyeF[:])
                mm.then_inc(b_aT, 1)

            def b_second(s):
                pe.wait_ge(b_lo, s.t + 1)
                before(pe, b_yev, s.t, 2)
                pe.sem_inc(passed["pe"], 1)
                e = pe.value_load(expB[0:1, bass.ds(s.t, 1)], min_val=0, max_val=E_B - 1)
                split_product(bank(4 + s.u), lambda k, p: bpT[s.u][:, p, k * P:(k + 1) * P],
                              lambda k, p: (c_hi, c_lo)[p][:, bass.ds(e * (KD * D) + k * D, D)], KD).then_inc(b_y, 1)

            pe.wait_ge(ctx_lo, T)
            pe.wait_ge(x1_done, T)
            pipeline(pe, J_B, [(0, b_first), (-1, b_turn), (1, b_second), (0, b_turn_a)])

            def s_turn(s):
                pe.wait_ge(s_hi, s.t + 1)
                pe.wait_ge(s_lo, s.t + 1)
                before(pe, s_ev, s.t, 1)
                for k in range(2 * KD):
                    mm = pe.transpose(bank(0).bitcast(F16)[:, k * P:(k + 1) * P], rows[s.u][:, k * P:(k + 1) * P], eyeH[:])
                mm.then_inc(s_T, 1)

            def s_router(s):
                pe.wait_ge(s_ev, s.t + 1)
                before(pe, s_lgev, s.t, 1)
                before(pe, s_plo, s.t, 1)
                split_product(bank(6, E_C, 256), lambda k, p: hT[s.u][:, p * KD + k, :],
                              lambda k, p: (gw_hi, gw_lo)[p][:, k * E_C:(k + 1) * E_C], KD).then_inc(s_lg, 1)

            def s_gate_up(s):
                for c in range(2):
                    before(pe, s_p, s.t, 1, 2)
                    for half in range(2):
                        split_product(bank(1 + 2 * half + c, CW), lambda k, p: hT[s.u][:, p * KD + k, :],
                                      lambda k, p: (w_hi, w_lo)[p][:, (2 * k + half) * IS + c * CW:(2 * k + half) * IS + (c + 1) * CW],
                                      KD) if half == 0 else \
                            split_product(bank(1 + 2 * half + c, CW), lambda k, p: hT[s.u][:, p * KD + k, :],
                                          lambda k, p: (w_hi, w_lo)[p][:, (2 * k + half) * IS + c * CW:(2 * k + half) * IS + (c + 1) * CW],
                                          KD).then_inc(s_gu, 1)

            def s_turn_p(s):
                pe.wait_ge(s_p, s.t * 2 + 2)
                pe.wait_ge(s_lgev, s.t + 1)
                before(pe, s_plo, s.t, 1)
                for k in range(ISP // P):
                    mm = pe.transpose(wide(5, ISP)[:, k * P:(k + 1) * P], ss[:, k * P:(k + 1) * P], eyeF[:])
                mm.then_inc(s_pT, 1)

            def s_down(s):
                pe.wait_ge(s_plo, s.t + 1)
                before(pe, s_x3, s.t, 1)
                base = KD * 2 * IS
                split_product(bank(7), lambda k, p: spT[:, p, k * P:(k + 1) * P],
                              lambda k, p: (w_hi, w_lo)[p][:, base + k * D:base + (k + 1) * D], ISP // P).then_inc(s_dn, 1)

            pe.wait_ge(gw_done, 2)
            pe.wait_ge(wlo_done, 2 * LOADS_PER_SLOT)
            pe.wait_ge(b_yev, J_B)
            pe.wait_ge(s_pad, 1)
            pipeline(pe, T, [(0, s_router), (0, s_gate_up), (-1, s_turn), (1, s_down), (0, s_turn_p)])

            pe.wait_ge(s_plo, T)
            pe.wait_ge(s_x3, T)
            route_sums(E_C, 2, 5)
            route_inverse(J_C, 2 * T, 6, T, 2 * T)

            def c_turn(s):
                turn_rows(s, c_rows[s.u], c_ev, c_T)

            def at_expert(s):
                return pe.value_load(expC[0:1, bass.ds(s.t, 1)], min_val=0, max_val=E_C - 1)

            def c_gate_up(s):
                pe.wait_ge(c_ev, s.t + 1)
                before(pe, c_p, s.t, 2)
                pe.sem_inc(passed["pe"], 1)
                e = at_expert(s)
                for half in range(2):
                    mm = split_product(bank(1 + 2 * half + s.u, IC), lambda k, p: hT[s.u][:, p * KD + k, :],
                                       lambda k, p: (w_hi, w_lo)[p][:, bass.ds(e * SLOT + (2 * SLOT + (2 * k + half) * IC), IC)], KD)
                mm.then_inc(c_gu, 1)

            def c_turn_p(s):
                pe.wait_ge(c_p, s.t + 1)
                before(pe, c_lo_s, s.t, 1)
                for k in range(ICP // P):
                    mm = pe.transpose(bank(5, P, k * P), cs[s.u][:, k * P:(k + 1) * P], eyeF[:])
                mm.then_inc(c_pT, 1)

            def c_down(s):
                pe.wait_ge(c_lo_s, s.t + 1)
                before(pe, c_yev, s.t, 2)
                pe.sem_inc(passed["pe"], 1)
                e = at_expert(s)
                split_product(bank(6 + s.u), lambda k, p: cpT[s.u][:, p, k * P:(k + 1) * P],
                              lambda k, p: (w_hi, w_lo)[p][:, bass.ds(e * SLOT + (2 * SLOT + KD * 2 * IC + k * D), D)],
                              ICP // P).then_inc(c_dn, 1)

            pe.wait_ge(routeC, 1)
            pe.wait_ge(wlo_done, CHUNKS)
            pe.wait_ge(pad_done, 2)
            pipeline(pe, J_C, [(0, c_gate_up), (-1, c_turn), (1, c_down), (0, c_turn_p)])


def layouts(x, tok, w_gate, g_gate, w_down, g_down, ctx, gate_w, we_gate, we_up, we_down, sw_gate, sw_up, sw_down):
    def steps(w):
        return w.reshape(-1, P, w.shape[1]).transpose(1, 0, 2)

    def padded(w, rows):
        return np.concatenate([w, np.zeros((rows - w.shape[0], w.shape[1]), w.dtype)])

    slots = []
    both = np.concatenate([steps(sw_gate), steps(sw_up)], axis=2).reshape(P, -1)
    slots.append(np.concatenate([both, steps(padded(sw_down, ISP)).reshape(P, -1)], axis=1))
    for e in range(E_C):
        both = np.concatenate([steps(we_gate[e]), steps(we_up[e])], axis=2).reshape(P, -1)
        slots.append(np.concatenate([both, steps(padded(we_down[e], ICP)).reshape(P, -1)], axis=1))
    moe = np.concatenate(slots, axis=1)
    return {
        "x": x.reshape(N, D),
        "tok": tok.reshape(T, P).T,
        "wgate": steps(w_gate.T).reshape(P, -1),
        "wdown": steps(w_down.T).reshape(P, -1),
        "ggate": g_gate.reshape(1, D),
        "gdown": g_down.reshape(1, IA),
        "ctxt": np.concatenate([steps(ctx[e].T) for e in range(E_B)], axis=1).reshape(P, -1),
        "gatew": steps(gate_w.T).reshape(P, -1),
        "wmoe": moe.reshape(P, CHUNKS, CHUNK).transpose(1, 0, 2).reshape(CHUNKS * P, CHUNK),
    }


_NAMES = ["x", "itok_BxS_13_99985", "L0_attn_w_gate", "L0_attn_g_gate", "L0_attn_w_down", "L0_attn_g_down", "ctx_2048",
          "L0_ffn_gate_w", "L0_ffn_w_gate", "L0_ffn_w_up", "L0_ffn_w_down", "L0_ffn_sw_gate", "L0_ffn_sw_up", "L0_ffn_sw_down"]


def kernel(**inputs):
    import concourse.bacc as bacc
    from concourse.bass_utils import run_bass_kernel_spmd

    given = [np.asarray(inputs[n]) for n in _NAMES]
    arrays = {f"in_{n}": np.ascontiguousarray(a) for n, a in layouts(*given).items()}
    nc = bacc.Bacc("TRN2", target_bir_lowering=False, num_devices=1)
    args = {n[3:]: nc.dram_tensor(n, a.shape, mybir.dt.from_np(a.dtype), kind="ExternalInput").ap() for n, a in arrays.items()}
    out = nc.dram_tensor("out_x", (N, D), F32, kind="ExternalOutput").ap()
    build(nc, out=out, **args)
    result = run_bass_kernel_spmd(nc, [arrays], core_ids=[0])
    return result.results[0]["out_x"].reshape(given[0].shape)
```

```python
from collections import namedtuple
from contextlib import ExitStack

import numpy as np
import concourse.bass as bass
import concourse.mybir as mybir

F32, F16, BF16 = mybir.dt.float32, mybir.dt.float16, mybir.dt.bfloat16
I32 = mybir.dt.int32
ALU = mybir.AluOpType
ACT = mybir.ActivationFunctionType
AX = mybir.AxisListType

P = 128
D = 512
KD = D // P
N = 2048
T = N // P
IA = 1408
KI = IA // P
CW = 352
HALVES = 2
CA = IA // CW
E_B, E_C = 4, 8
J_B = T + E_B - 1
J_C = 2 * T + E_C - 1
VOCAB = 25000
PER_EXPERT = VOCAB // E_B
IC = 352
ICP = 384
IS = 704
SHARES = IS // IC
SLOT = KD * 2 * IC + (ICP // P) * D
LOADS_PER_SLOT = 4
CHUNK = SLOT // LOADS_PER_SLOT
SLOTS = SHARES + E_C
CHUNKS = SLOTS * LOADS_PER_SLOT
assert SHARES == 2 and CHUNK * LOADS_PER_SLOT == SLOT
EPS_LN, EPS_RMS, EPS_Q = 1e-5, 1e-6, 1e-5
MAGIC = 12582912.0
SCALE_B, SCALE_C = 256.0, 64.0

R0 = 24
R1 = R0 + J_C
TILES = SHARES * T + J_C
S_ROUNDS = T - 1
PAIRS = T // 2
SELS = 8

Step = namedtuple("Step", "t u h first")


def pipeline(engine, count, stages, begin=None, end=None, kind=None):
    todo = [(g, stage, *(span[0] if span else (0, count))) for g, stage, *span in stages]
    begin = min(g + lo for g, _, lo, _ in todo) if begin is None else begin
    end = max(g + hi for g, _, _, hi in todo) if end is None else end
    k_lo, k_hi = kind or (0, count)
    first = max(begin, max(g + max(lo + 2, k_lo) for g, _, lo, _ in todo))
    turns = max(0, (min(end, min(g + min(hi, k_hi) for g, _, _, hi in todo)) - first) // 2)

    def straight(rounds):
        for r in rounds:
            for g, stage, lo, hi in todo:
                if lo <= r - g < hi:
                    stage(Step(r - g, (r - g) % 2, (r - g) // 2, r - g))

    if turns == 0:
        straight(range(begin, end))
        return
    straight(range(begin, first))
    with engine.Fori(0, turns) as i:
        for c in range(2):
            for g, stage, _, _ in todo:
                t = first + c - g
                stage(Step(i * 2 + t, t % 2, i + t // 2, t))
    straight(range(first + 2 * turns, end))


def routed(s):
    return R0 <= s.first < R1


def shared_part(s):
    skip = 0 if s.first < R0 else J_C
    k = s.first - skip
    return s.h + (k // SHARES - s.first // 2), k % SHARES, s.t - skip


def rows_count(s):
    if routed(s):
        return s.h - (R0 // 2 - 1)
    if s.first < R0:
        return s.h + 1
    return s.h - ((R1 + (R1 + s.u) % 2) // 2 - R0 // 2 - 1)


def output_pair(s):
    k = s.first - (TILES - PAIRS)
    return s.t - (TILES - PAIRS), k % 2, s.h + (k // 2 - s.first // 2)


def before(engine, sem, t, back, per=1):
    if isinstance(t, int) and t < back:
        return
    engine.wait_ge(sem, (t - (back - 1)) * per)


def build(nc, x, tok, wgate, wdown, ggate, gdown, ctxt, gatew, wmoe, out):
    ctx = ExitStack()
    with ctx:
        def sb(name, shape, dt):
            return ctx.enter_context(nc.sbuf_tensor(name, shape, dt))

        def sem(name):
            return ctx.enter_context(nc.semaphore(name))

        def two(name):
            return [sem(f"{name}{i}") for i in range(2)]

        def dram(name, shape, dt):
            return nc.dram_tensor(name, shape, dt, kind="Internal").ap()

        x1_d, x2_d = (dram(n, (N, D), F32) for n in ("x1_d", "x2_d"))
        hB_d, hC_d = (dram(n, (N, 2 * D), F16) for n in ("hB_d", "hC_d"))
        yB_d = dram("yB_d", (J_B * P, D), F32)
        yC_d = dram("yC_d", (J_C * P, D), F32)
        yS_d = dram("yS_d", (SHARES * N, D), F32)

        w_hi = sb("w_hi", [P, SLOTS * SLOT], F16)
        w_lo = sb("w_lo", [P, SLOTS * SLOT], F16)

        class Carver:

            def __init__(self, tensor, slot, slots):
                self.flat, self.at, self.end = tensor, slot * SLOT, (slot + slots) * SLOT

            def take(self, n, dt):
                words = n * (2 if dt == F32 else 1)
                view = self.flat[:, self.at:self.at + words]
                self.at += words
                assert self.at <= self.end
                return view if dt == F16 else view.bitcast(dt)

        stage_hi, stage_lo = Carver(w_hi, 0, 4), Carver(w_lo, 0, 4)
        OG = 2 * IA
        wg32 = [stage_hi.take(OG, F32) for _ in range(3)] + [stage_lo.take(OG, F32)]
        wd32 = stage_lo.take(KI * D, F32)
        tern_hi, tern_lo = Carver(w_hi, 4, 2), Carver(w_lo, 4, 2)
        wgT = [tern_hi.take(OG, BF16) for _ in range(3)] + [tern_lo.take(OG, BF16)]
        wdT = tern_lo.take(KI * D, BF16)
        a6h, a6l, a9h, a9l = Carver(w_hi, 6, 1), Carver(w_lo, 6, 1), Carver(w_hi, 9, 1), Carver(w_lo, 9, 1)
        xin = [a6h.take(D, F32) for _ in range(2)]
        xcen = [a6h.take(D, F32) for _ in range(2)]
        xq = [a6l.take(D, BF16) for _ in range(2)]
        xqT = [a6l.take(D, BF16) for _ in range(2)]
        xmag = [a6l.take(D, F32) for _ in range(2)]
        gg = a9h.take(D, F32)
        hA = a9l.take(D, F32)
        ah, al = Carver(w_hi, 0, 4), Carver(w_lo, 0, 4)
        sw = [ah.take(IA, F32) for _ in range(2)]
        swg = [ah.take(IA, F32) for _ in range(2)]
        sil = [ah.take(CW, F32) for _ in range(2)]
        gd = ah.take(IA, F32)
        squares = ah.take(IA, BF16)
        qd = [al.take(IA, BF16) for _ in range(2)]
        qdT = [al.take(IA, BF16) for _ in range(2)]
        xres = [al.take(D, F32) for _ in range(2)]
        x1 = [al.take(D, F32) for _ in range(2)]
        c_hi, c_lo = Carver(w_hi, 7, 2).take(E_B * KD * D, F16), Carver(w_lo, 7, 2).take(E_B * KD * D, F16)
        b9h = Carver(w_hi, 9, 1)
        bs = [b9h.take(D, F32) for _ in range(2)]
        bpT = [b9h.take(2 * D, F16).rearrange("p (a n) -> p a n", a=2) for _ in range(2)]
        s9h, s9l = Carver(w_hi, 9, 1), Carver(w_lo, 9, 1)
        hS = s9h.take(D, F32)
        xS = [s9h.take(D, F32) for _ in range(2)]
        hTS = s9h.take(2 * D, F16).rearrange("p (a n) -> p a n", n=P)
        yS = [s9l.take(D, F32) for _ in range(2)]
        rowsS = [s9l.take(2 * D, F16) for _ in range(2)]
        fh, fl = Carver(w_hi, SHARES, 3), Carver(w_lo, SHARES, 3)
        xF = [fh.take(D, F32) for _ in range(4)]
        shF = [fl.take(SHARES * D, F32).rearrange("p (a n) -> p a n", a=SHARES) for _ in range(4)]
        yF = [[carver.take(D, F32) for _ in range(4)] for carver in (fh, fl)]

        wstage = [sb(f"wstage{i}", [P, CHUNK], F32) for i in range(2)]
        rows = [sb(f"rows{i}", [P, 2 * D], F16) for i in range(2)]
        hT = [sb(f"hT{i}", [P, 2 * KD, P], F16) for i in range(2)]
        yrow = [sb(f"yrow{i}", [P, D], F32) for i in range(2)]
        cs = sb("cs", [P, ICP], F32)
        cpT = sb("cpT", [P, 2, ICP], F16)
        eyeF, eyeH, eyeB = sb("eyeF", [P, P], F32), sb("eyeH", [P, P], F16), sb("eyeB", [P, P], BF16)
        onesF = sb("onesF", [P, P], F32)
        onesH, triH = sb("onesH", [P, P], F16), sb("triH", [P, P], F16)
        iotaI = sb("iotaI", [P, P], I32)
        iotaF = sb("iotaF", [P, P], F32)
        tokidI, tokid = sb("tokidI", [P, T], I32), sb("tokid", [P, T], F32)
        powh = sb("powh", [P, 1], F32)
        asum = sb("asum", [P, KD + 2], F32)
        wmean = sb("wmean", [P, 2], F32)
        wm127 = sb("wm127", [P, 2], F32)
        winv = sb("winv", [P, 2], F32)
        tokI, tokF = sb("tokI", [P, T], I32), sb("tokF", [P, T], F32)
        gw32 = sb("gw32", [P, KD * E_C], F32)
        gw_hi, gw_lo = sb("gw_hi", [P, KD * E_C], F16), sb("gw_lo", [P, KD * E_C], F16)
        stats = [sb(f"xstats{i}", [P, 6], F32) for i in range(2)]
        mv = [sb(f"xmv{i}", [P, 2], F32) for i in range(2)]
        xmax = [sb(f"xmax{i}", [P, 1], F32) for i in range(2)]
        smA = [sb(f"smA{i}", [P, 3], F32) for i in range(2)]
        cx = [sb(f"cx{i}", [P, 1], F32) for i in range(2)]
        dqx = [sb(f"dqx{i}", [P, 1], F32) for i in range(2)]
        dqg = [sb(f"dqg{i}", [P, 1], F32) for i in range(2)]
        ssq = [sb(f"ssq{i}", [P, 1], F32) for i in range(2)]
        gmax = [sb(f"gmax{i}", [P, 1], F32) for i in range(2)]
        smG = [sb(f"smG{i}", [P, 3], F32) for i in range(2)]
        cg = [sb(f"cg{i}", [P, 1], F32) for i in range(2)]
        stats1 = sb("stats1", [P, 6], F32)
        mv1 = sb("mv1", [P, 2], F32)
        var1 = sb("var1", [P, 1], F32)
        rstd1 = sb("rstd1", [P, 1], F32)
        W2 = T * E_C
        oh = sb("oh", [P, T, E_C], F16)
        oh12 = [sb(f"oh{c}_", [P, T, E_C], F32) for c in range(2)]
        ohsum = sb("ohsum", [P, T + 1, E_C], F16)
        rank = sb("rank", [P, T + 1, E_C], F32)
        rt = sb("rt", [P, T, E_C], F32)
        rt2 = sb("rt2", [P, T, E_C], F32)
        eI = sb("eI", [P, E_C], I32)
        eF = sb("eF", [P, 3, E_C], F32)
        rI = sb("rI", [P, 2, T], I32)
        rF = sb("rF", [P, 4, T], F32)
        posF = sb("posF", [P, T], F32)
        posB = sb("posB", [P, T], I32)
        posC = [sb(f"posC{c}", [P, T], I32) for c in range(2)]
        selR = [sb(f"selR{i}", [P, P], F16) for i in range(SELS)]
        selJ = [sb(f"selJ{i}", [P, J_C], F16) for i in range(SELS)]
        jF = sb("jF", [P, J_C], F32)
        invB, invC = sb("invB", [P, J_B], I32), sb("invC", [P, J_C], I32)
        expB, expC = sb("expB", [P, J_B], I32), sb("expC", [P, J_C], I32)
        idx = [sb(f"idx{i}", [P, 1], I32) for i in range(2)]
        idf = [[sb(f"idf{c}{i}", [P, 1], I32) for i in range(4)] for c in range(2)]
        logits = sb("logits", [P, T, E_C], F32)
        m12 = sb("m12", [P, 2, T], F32)
        wsum = sb("wsum", [P, T], F32)
        wtop = [sb(f"wtop{c}", [P, T], F32) for c in range(2)]

        banks = ctx.enter_context(nc.psum_tensor("banks", [P, 8, 512], F32))

        def bank(b, n=512, at=0):
            return banks[:, b, at:at + n]

        def wide(b, n):
            return banks[:, b:b + 2, :].rearrange("p a n -> p (a n)")[:, 0:n]

        consts, CONSTS = sem("consts"), 6
        const_steps = sem("const_steps")
        tok_in, gains_in = sem("tok_in"), sem("gains_in")
        gd_in = sem("gd_in")
        wg_in = [sem(f"wg_in{k}") for k in range(KD)]
        wd_in = sem("wd_in")
        abs_done, tot_done, means_done = sem("abs_done"), sem("tot_done"), sem("means_done")
        silu_table = sem("silu_table")
        round_done, clip_done = sem("round_done"), sem("clip_done")
        tern_done, gw_done = sem("tern_done"), sem("gw_done")
        passed = {n: sem(f"passed_{n}") for n in ("dve", "pool", "pe", "sp")}
        x_in = two("x_in")
        x_stats, x_mom, x_cen, x_max = sem("x_stats"), sem("x_mom"), sem("x_cen"), sem("x_max")
        x_rec, g_rec, x_dq, g_dq = sem("x_rec"), sem("g_rec"), sem("x_dq"), sem("g_dq")
        x_small, x_mag, x_q, x_T, x_ev = sem("x_small"), sem("x_mag"), sem("x_q"), sem("x_T"), sem("x_ev")
        gu_done, sil_done, sw_done = sem("gu_done"), sem("sil_done"), sem("sw_done")
        swg_done, sq_done, g_max, g_small = sem("swg_done"), sem("sq_done"), sem("g_max"), sem("g_small")
        d_mag, d_q, d_T, d_ev, z_done = sem("d_mag"), sem("d_q"), sem("d_T"), sem("d_ev"), sem("z_done")
        xr_in, x1_out, hb_out = two("xr_in"), two("x1_out"), two("hb_out")
        x1_done, st1, mo1, rs1 = sem("x1_done"), sem("st1"), sem("mo1"), sem("rs1")
        smA_s, smG_s, smB_s = sem("smA_s"), sem("smG_s"), sem("smB_s")
        h_done, hi_done, lo_done = sem("h_done"), sem("hi_done"), sem("lo_done")
        ctx_in, ctx_hi, ctx_lo = two("ctx_in"), sem("ctx_hi"), sem("ctx_lo")
        route = sem("route")
        route_mm, sel_done, inv_mm = sem("route_mm"), sem("sel_done"), sem("inv_mm")
        routeB, routeC = sem("routeB"), sem("routeC")
        w_in, whi_done, wlo_done = two("w_in"), sem("whi_done"), sem("wlo_done")
        b_idx, b_rows, b_T, b_ev = sem("b_idx"), two("b_rows"), sem("b_T"), sem("b_ev")
        b_t, b_sil, b_a, b_aT = sem("b_t"), sem("b_sil"), sem("b_a"), sem("b_aT")
        b_hi, b_lo, b_y, b_yev, b_out = sem("b_hi"), sem("b_lo"), sem("b_y"), sem("b_yev"), two("b_out")
        s_x, s_idx, s_y = two("s_x"), sem("s_idx"), two("s_y")
        s_x2, s_st, s_mo, s_rs, s_small = sem("s_x2"), sem("s_st"), sem("s_mo"), sem("s_rs"), sem("s_small")
        s_h, s_hi, s_lo, s_x2out, s_hout = sem("s_h"), sem("s_hi"), sem("s_lo"), two("s_x2out"), two("s_hout")
        s_T, s_ev, s_lg, s_lgev = sem("s_T"), sem("s_ev"), sem("s_lg"), sem("s_lgev")
        pad_done = sem("pad_done")
        exp_done = sem("exp_done")
        c_idx, c_shared, c_rows, c_T, c_ev = sem("c_idx"), two("c_shared"), two("c_rows"), sem("c_T"), sem("c_ev")
        c_gu, c_sil, c_p, c_pT = sem("c_gu"), sem("c_sil"), sem("c_p"), sem("c_pT")
        c_hi_s, c_lo_s, c_dn, c_yev, c_out = sem("c_phi"), sem("c_plo"), sem("c_dn"), sem("c_yev"), two("c_out")
        f_idx, f_a, f_o = sem("f_idx"), sem("f_a"), sem("f_o")
        f_x, f_y, f_out = ([sem(f"{n}{i}") for i in range(4)] for n in ("f_x", "f_y", "f_out"))

        HALF = T // 2

        def tiles(ap, t):
            return ap[bass.ds(t * P, P), :]

        def alone(engine, name, s, value):
            engine.wait_ge(s, value)
            engine.sem_inc(passed[name], 1)

        def slot_9_free(engine):
            engine.wait_ge(s_lg, T)
            engine.wait_ge(s_hi, T)
            engine.wait_ge(s_lo, T)
            for u in range(2):
                engine.wait_ge(s_hout[u], 16 * HALF)
                engine.wait_ge(s_x2out[u], 16 * HALF)

        W_REST = CHUNKS - J_B
        W_FREE = (SLOTS - 1) * LOADS_PER_SLOT - J_B

        block = ctx.enter_context(nc.Block())

        @block.sync
        def _(sp):
            sp.dma_start(tokI[:], tok[:]).then_inc(tok_in, 16)
            sp.dma_start(gg, ggate.broadcast_to([P, D])).then_inc(gains_in, 16)
            sp.dma_start(gw32[:], gatew[:]).then_inc(gains_in, 16)
            for k in range(KD):
                sp.dma_start(wg32[k], wgate[:, k * OG:(k + 1) * OG]).then_inc(wg_in[k], 16)
                if k < 2:
                    sp.dma_start(xin[k], tiles(x, k)).then_inc(x_in[k], 16)
            sp.dma_start(wd32, wdown[:]).then_inc(wd_in, 16)

            def load_x(s):
                if isinstance(s.t, int) and s.t < 2:
                    return
                before(sp, x_cen, s.t, 2)
                before(sp, x_stats, s.t, 2)
                sp.dma_start(xin[s.u], tiles(x, s.t)).then_inc(x_in[s.u], 16)

            def load_res(s):
                if isinstance(s.t, int) and s.t == 0:
                    sp.wait_ge(tern_done, KD + 2)
                before(sp, x1_done, s.t, 2)
                sp.dma_start(xres[s.u], tiles(x, s.t)).then_inc(xr_in[s.u], 16)

            def load_ctx(s):
                before(sp, ctx_lo, s.t, 2)
                sp.dma_start(wstage[s.u][:, 0:D], ctxt[:, bass.ds(s.t * D, D)]).then_inc(ctx_in[s.u], 16)

            def store_x1(s):
                sp.wait_ge(x1_done, s.t + 1)
                sp.dma_start(tiles(x1_d, s.t), x1[s.u]).then_inc(x1_out[s.u], 16)

            def store_hb(s):
                sp.wait_ge(hi_done, s.t + 1)
                sp.wait_ge(lo_done, s.t + 1)
                sp.dma_start(tiles(hB_d, s.t), rows[s.u][:]).then_inc(hb_out[s.u], 16)

            stages = [(3, store_x1), (1, load_res), (0, load_ctx), (3, store_hb), (-5, load_x)]
            pipeline(sp, T, stages, end=-2)
            sp.wait_ge(tern_done, KD)
            sp.dma_start(gd, gdown.broadcast_to([P, IA])).then_inc(gd_in, 16)
            pipeline(sp, T, stages, begin=-2)

            def load_w(q, u, wait):
                if wait:
                    sp.wait_ge(wlo_done, q - 1)
                sp.dma_start(wstage[u][:], wmoe[bass.ds(q * P, P), :]).then_inc(w_in[u], 16)

            def b_load(s):
                if isinstance(s.t, int) and s.t < 2:
                    sp.wait_ge(ctx_lo, T)
                load_w(s.t, s.u, not (isinstance(s.t, int) and s.t < 2))

            def b_store(s):
                sp.wait_ge(b_yev, s.t + 1)
                sp.dma_start(tiles(yB_d, s.t), yrow[s.u][:]).then_inc(b_out[s.u], 16)

            pipeline(sp, J_B, [(-1, b_load), (1, b_store)])

            def s_load(s):
                before(sp, s_x2out[s.u], s.h, 1, 16)
                before(sp, s_h, s.t, 2)
                sp.dma_start(xS[s.u], tiles(x1_d, s.t)).then_inc(s_x[s.u], 16)

            def s_storex2(s):
                sp.wait_ge(s_x2, s.t + 1)
                sp.dma_start(tiles(x2_d, s.t), xS[s.u]).then_inc(s_x2out[s.u], 16)

            def s_storeh(s):
                sp.wait_ge(s_hi, s.t + 1)
                sp.wait_ge(s_lo, s.t + 1)
                sp.dma_start(tiles(hC_d, s.t), rowsS[s.u]).then_inc(s_hout[s.u], 16)

            def s_stored(s):
                alone(sp, "sp", s_hout[s.u], (s.h + 1) * 16)

            def s_loadw(s):
                load_w(s.t + J_B, (s.u + J_B) % 2, True)

            def c_rows_in(s):
                if isinstance(s.t, int) and s.t < 2:
                    sp.wait_ge(b_T, J_B)
                before(sp, c_T, s.t, 2)
                sp.dma_start(rows[s.u][:], tiles(hC_d, shared_part(s)[0])).then_inc(c_shared[s.u], 16)

            def c_store(s):
                sp.wait_ge(c_yev, s.t + 1)
                to = tiles(yC_d, s.t - R0) if routed(s) else tiles(yS_d, shared_part(s)[2])
                sp.dma_start(to, yrow[s.u][:]).then_inc(c_out[s.u], 16)

            sp.wait_ge(x1_out[0], 16 * HALF)
            sp.wait_ge(x1_out[1], 16 * HALF)
            sp.wait_ge(b_y, J_B)
            shared_first, shared_last = (0, R0), (R1, TILES)
            pipeline(sp, TILES, [(-2, s_stored, (0, T)), (-2, c_rows_in, shared_first), (-3, s_storex2, (0, T)),
                                 (-3, s_storeh, (0, T)), (-5, s_load, (0, T)), (-2, s_loadw, (0, W_REST)), (1, c_store)],
                     end=S_ROUNDS)
            pipeline(sp, TILES, [(-2, c_rows_in, shared_first), (-2, s_loadw, (0, W_REST)), (1, c_store)],
                     begin=S_ROUNDS, end=R0)
            pipeline(sp, TILES, [(1, c_store)], begin=R0, end=R1 - 2, kind=(R0, R1))

            def f_load(s):
                pair, odd, turn = output_pair(s)
                if isinstance(pair, int) and pair == 0:
                    sp.wait_ge(c_dn, R1)
                alone(sp, "sp", c_out[s.u], (s.h + 1) * 16)
                alone(sp, "sp", c_out[1 - s.u], (s.h + s.u) * 16)
                for i in range(2):
                    slot, t = odd * 2 + i, pair * 2 + i
                    if not (isinstance(pair, int) and pair < 2):
                        alone(sp, "sp", f_out[slot], turn * 16)
                    sp.dma_start(xF[slot], tiles(x2_d, t)).then_inc(f_x[slot], 16)
                    halves = yS_d[bass.ds(t * (SHARES * P), SHARES * P), :].rearrange("(a p) d -> p a d", p=P)
                    sp.dma_start(shF[slot], halves).then_inc(f_x[slot], 16)

            def f_store(s):
                pair, odd, _ = output_pair(s)
                for i in range(2):
                    alone(sp, "sp", f_o, pair * 2 + (i + 1))
                    sp.dma_start(tiles(out, pair * 2 + i), xF[odd * 2 + i]).then_inc(f_out[odd * 2 + i], 16)

            last = (TILES - PAIRS, TILES)
            pipeline(sp, TILES, [(-2, c_rows_in, shared_last), (1, c_store), (3, f_store, last), (2, f_load, last)], begin=R1 - 2)
            for slot in range(4):
                sp.wait_ge(f_out[slot], 16 * T // 4)

        @block.gpsimd
        def _(pool):
            for m in (eyeF, onesF):
                pool.memset(m[:], 0.0 if m is eyeF else 1.0).then_inc(const_steps, 1)
            pool.memset(triH[:], 1.0).then_inc(const_steps, 1)
            pool.memset(onesH[:], 1.0).then_inc(consts, 1)
            pool.memset(powh[:], -0.5).then_inc(consts, 1)
            pool.iota(iotaI[:], pattern=[[1, P]], base=0, channel_multiplier=0).then_inc(consts, 1)
            pool.iota(tokidI[:], pattern=[[P, T]], base=0, channel_multiplier=1).then_inc(consts, 1)
            pool.wait_ge(const_steps, 3)
            pool.affine_select(out=eyeF[:], in_=eyeF[:], compare_op=ALU.not_equal, fill=1.0, base=0,
                               pattern=[[-1, P]], channel_multiplier=1).then_inc(consts, 1)
            pool.affine_select(out=triH[:], in_=triH[:], compare_op=ALU.is_gt, fill=0.0, base=0,
                               pattern=[[1, P]], channel_multiplier=-1).then_inc(consts, 1)
            pool.wait_ge(consts, CONSTS)

            def rsqrt_chain(done, n0, src, eps, tmp, dst, last):
                pool.tensor_scalar(tmp, src, eps, None, ALU.add).then_inc(done, 1)
                alone(pool, "pool", done, n0 + 1)
                pool.tensor_tensor(dst, tmp, powh[:], ALU.pow).then_inc(last, 1)

            def small_x(s):
                w, n0 = smA[s.u], s.t * 3
                alone(pool, "pool", x_mom, s.t + 1)
                before(pool, x_small, s.t, 2)
                before(pool, x_dq, s.t, 2)
                pool.sem_inc(passed["pool"], 1)
                pool.tensor_scalar(w[:, 0:1], mv[s.u][:, 1:2], 1.0 + EPS_RMS, EPS_RMS * EPS_LN, ALU.mult, ALU.add).then_inc(smA_s, 1)
                alone(pool, "pool", smA_s, n0 + 1)
                pool.tensor_tensor(w[:, 1:2], w[:, 0:1], powh[:], ALU.pow).then_inc(smA_s, 1)
                alone(pool, "pool", smA_s, n0 + 2)
                alone(pool, "pool", x_max, s.t + 1)
                pool.tensor_scalar(w[:, 2:3], xmax[s.u][:], w[:, 1:2], EPS_Q, ALU.mult, ALU.max).then_inc(smA_s, 1)

            def gains(s, half):
                at = slice(half * IA // HALVES, (half + 1) * IA // HALVES)
                alone(pool, "pool", sw_done, s.t * CA + (half + 1) * CA // HALVES)
                before(pool, d_q, s.t, 2)
                pool.sem_inc(passed["pool"], 1)
                if isinstance(s.t, int) and s.t == 0:
                    pool.wait_ge(gd_in, 16)
                pool.tensor_tensor(swg[s.u][:, at], sw[s.u][:, at], gd[:, at], ALU.mult).then_inc(swg_done, 1)

            def small_g(s):
                w, n0 = smG[s.u], s.t * 3
                alone(pool, "pool", sq_done, s.t + 1)
                alone(pool, "pool", g_max, s.t + 1)
                before(pool, g_small, s.t, 2)
                before(pool, g_dq, s.t, 2)
                pool.sem_inc(passed["pool"], 1)
                pool.tensor_scalar(w[:, 0:1], ssq[s.u][:], 1.0 / IA, EPS_RMS, ALU.mult, ALU.add).then_inc(smG_s, 1)
                alone(pool, "pool", smG_s, n0 + 1)
                pool.tensor_tensor(w[:, 1:2], w[:, 0:1], powh[:], ALU.pow).then_inc(smG_s, 1)
                alone(pool, "pool", smG_s, n0 + 2)
                pool.tensor_scalar(w[:, 2:3], gmax[s.u][:], w[:, 1:2], EPS_Q, ALU.mult, ALU.max).then_inc(smG_s, 1)

            def small_b(s):
                alone(pool, "pool", mo1, s.t + 1)
                rsqrt_chain(smB_s, s.t, mv1[:, 1:2], EPS_LN, var1[:], rstd1[:], rs1)

            def h_lo(s):
                alone(pool, "pool", hi_done, s.t + 1)
                before(pool, hb_out[s.u], s.h, 1, 16)
                pool.sem_inc(passed["pool"], 1)
                pool.tensor_tensor(rows[s.u][:, D:2 * D], hA, rows[s.u][:, 0:D], ALU.subtract).then_inc(lo_done, 1)

            pipeline(pool, T, [(-2, small_x), (1, small_g), (3, small_b), (0, lambda s: gains(s, 0)),
                               (0, lambda s: gains(s, 1)), (3, h_lo)])

            def gather(s, order, done, index, inv, dst, table, t0=0):
                pool.tensor_copy(index[s.u][:], inv[:, bass.ds(s.t - t0, 1)]).then_inc(order, 1)
                alone(pool, "pool", order, s.t + (1 - t0))
                pool.indirect_dma_start(out=dst[s.u][:] if dst is rows else dst[s.u], out_offset=None, in_=table[:, :],
                                        in_offset=bass.IndirectOffsetOnAxis(ap=index[s.u][:], axis=0)).then_inc(done[s.u], 16)

            for u in range(2):
                pool.wait_ge(hb_out[u], 16 * HALF)
            pool.wait_ge(routeB, 1)

            def b_gather(s):
                if not (isinstance(s.t, int) and s.t < 2):
                    alone(pool, "pool", b_T, s.t - 1)
                    alone(pool, "pool", b_rows[s.u], s.h * 16)
                gather(s, b_idx, b_rows, idx, invB, rows, hB_d)

            pipeline(pool, J_B, [(-1, b_gather)])

            for u in range(2):
                pool.wait_ge(b_out[u], 16 * ((J_B + 1 - u) // 2))
                pool.wait_ge(b_rows[u], 16 * ((J_B + 1 - u) // 2))

            def s_gather(s):
                if not (isinstance(s.t, int) and s.t < 2):
                    alone(pool, "pool", s_x2, s.t - 1)
                    alone(pool, "pool", s_y[s.u], s.h * 16)
                gather(s, s_idx, s_y, idx, posB, yS, yB_d)

            def s_rstd(s):
                alone(pool, "pool", s_mo, s.t + 1)
                rsqrt_chain(s_small, s.t, mv1[:, 1:2], EPS_LN, var1[:], rstd1[:], s_rs)

            pipeline(pool, T, [(-4, s_gather), (-3, s_rstd)])

            for u in range(2):
                pool.wait_ge(s_hout[u], 16 * HALF)
                pool.wait_ge(s_y[u], 16 * HALF)
            pool.wait_ge(routeC, 1)

            def c_gather(s):
                alone(pool, "pool", c_T, s.t - 1)
                if not (isinstance(s.t, int) and s.t < R0 + 2):
                    alone(pool, "pool", c_rows[s.u], (s.h - R0 // 2) * 16)
                gather(s, c_idx, c_rows, idx, invC, rows, hC_d, R0)

            pipeline(pool, TILES, [(-1, c_gather, (R0, R1))], kind=(R0, R1))

            for u in range(2):
                pool.wait_ge(c_out[u], 16 * ((R1 + 1 - u) // 2))

            def f_gather(s):
                pair, odd, turn = output_pair(s)
                for i in range(2):
                    slot, n = odd * 2 + i, pair * 2 + i
                    if not (isinstance(pair, int) and pair < 2):
                        alone(pool, "pool", f_o, n - 3)
                        alone(pool, "pool", f_y[slot], turn * 32)
                    for c in range(2):
                        pool.tensor_copy(idf[c][slot][:], posC[c][:, bass.ds(n, 1)]).then_inc(f_idx, 1)
                    alone(pool, "pool", f_idx, n * 2 + 2)
                    for c in range(2):
                        pool.indirect_dma_start(out=yF[c][slot], out_offset=None, in_=yC_d[:, :],
                                                in_offset=bass.IndirectOffsetOnAxis(ap=idf[c][slot][:], axis=0)).then_inc(f_y[slot], 16)

            pipeline(pool, TILES, [(1, f_gather, (TILES - PAIRS, TILES))])

        @block.scalar
        def _(act):
            act.wait_ge(consts, CONSTS)
            act.activation(dqx[0][:], powh[:], ACT.Silu).then_inc(silu_table, 1)
            for k in range(KD):
                act.wait_ge(wg_in[k], 16)
                act.activation(wgT[k], wg32[k], ACT.Abs, accum_out=asum[:, k:k + 1]).then_inc(abs_done, 1)
            act.wait_ge(gains_in, 32)
            act.activation(gw_hi[:], gw32[:], ACT.Copy, scale=SCALE_C).then_inc(gw_done, 1)

            def x_round(s):
                act.wait_ge(x_small, s.t + 1)
                act.wait_ge(x_cen, s.t + 1)
                before(act, x_q, s.t, 2)
                act.activation(xmag[s.u], xcen[s.u], ACT.Copy, bias=MAGIC, scale=cx[s.u][:]).then_inc(x_mag, 1)

            def x_evac(s):
                act.wait_ge(x_T, s.t + 1)
                before(act, gu_done, s.t, 2, CA)
                act.copy(xqT[s.u], bank(4, 256).bitcast(BF16)).then_inc(x_ev, 1)

            def silu(s, c):
                if c == 0:
                    act.wait_ge(x_dq, s.t + 1)
                act.wait_ge(gu_done, s.t * CA + (c + 1))
                if not (isinstance(s.t, int) and s.t == 0 and c < 2):
                    act.wait_ge(sw_done, s.t * CA + (c - 1))
                act.activation(sil[c % 2], bank(c % 2, CW), ACT.Silu, scale=dqx[s.u][:]).then_inc(sil_done, 1)

            def dequant_x(s):
                act.wait_ge(smA_s, (s.t + 1) * 3)
                before(act, sw_done, s.t, 2, CA)
                if isinstance(s.t, int) and s.t == 0:
                    act.wait_ge(silu_table, 1)
                act.activation(dqx[s.u][:], smA[s.u][:, 2:3], ACT.Copy, scale=wm127[:, 0:1]).then_inc(x_dq, 1)

            def dequant_g(s):
                act.wait_ge(smG_s, (s.t + 1) * 3)
                before(act, x1_done, s.t, 2)
                act.activation(dqg[s.u][:], smG[s.u][:, 2:3], ACT.Copy, scale=wm127[:, 1:2]).then_inc(g_dq, 1)

            def square(s):
                act.wait_ge(sw_done, (s.t + 1) * CA)
                before(act, g_small, s.t, 2)
                before(act, sq_done, s.t, 1)
                act.activation(squares, sw[s.u], ACT.Square, accum_out=ssq[s.u][:]).then_inc(sq_done, 1)

            def d_round(s):
                act.wait_ge(g_small, s.t + 1)
                act.wait_ge(g_max, s.t + 1)
                act.activation(swg[s.u], swg[s.u], ACT.Copy, bias=MAGIC, scale=cg[s.u][:]).then_inc(d_mag, 1)

            def d_evac(s):
                act.wait_ge(d_T, s.t + 1)
                before(act, z_done, s.t, 2)
                act.copy(qdT[s.u], wide(5, IA // 2).bitcast(BF16)).then_inc(d_ev, 1)

            def h_hi(s):
                act.wait_ge(h_done, s.t + 1)
                before(act, hb_out[s.u], s.h, 1, 16)
                act.copy(rows[s.u][:, 0:D], hA).then_inc(hi_done, 1)

            def ctx_split(s):
                act.wait_ge(ctx_in[s.u], (s.h + 1) * 16)
                act.activation(c_hi[:, bass.ds(s.t * D, D)], wstage[s.u][:, 0:D], ACT.Copy, scale=SCALE_B).then_inc(ctx_hi, 1)

            act.wait_ge(means_done, 1)
            for k in range(KD):
                act.activation(wg32[k], wg32[k], ACT.Copy, bias=MAGIC, scale=winv[:, 0:1]).then_inc(round_done, 1)
            stages = [(0, lambda s: silu(s, 0)), (2, d_evac), (0, lambda s: silu(s, 1)), (0, ctx_split), (0, lambda s: silu(s, 2)),
                      (0, lambda s: silu(s, 3)), (1, d_round), (-1, x_evac), (3, h_hi), (1, dequant_g), (0, square), (-2, x_round),
                      (-2, dequant_x)]
            pipeline(act, T, stages, end=0)
            act.wait_ge(wd_in, 16)
            for half in range(2):
                at = slice(half * OG, (half + 1) * OG)
                act.activation(wdT[:, at], wd32[:, at], ACT.Abs, accum_out=asum[:, KD + half:KD + half + 1]).then_inc(abs_done, 1)
            pipeline(act, T, stages, begin=0, end=1)
            act.wait_ge(means_done, 2)
            for half in range(2):
                at = slice(half * OG, (half + 1) * OG)
                act.activation(wd32[:, at], wd32[:, at], ACT.Copy, bias=MAGIC, scale=winv[:, 1:2]).then_inc(round_done, 1)
            pipeline(act, T, stages, begin=1)

            def split_hi(s, q, u, h):
                act.wait_ge(w_in[u], (h + 1) * 16)
                act.activation(w_hi[:, bass.ds(q * CHUNK, CHUNK)], wstage[u][:], ACT.Copy, scale=SCALE_C).then_inc(whi_done, 1)

            def b_evac(s):
                act.wait_ge(b_T, s.t + 1)
                before(act, b_t, s.t, 2)
                act.copy(hT[s.u][:].rearrange("p a n -> p (a n)"), bank(0).bitcast(F16)).then_inc(b_ev, 1)

            def b_silu(s):
                act.wait_ge(b_t, s.t + 1)
                before(act, b_aT, s.t, 2)
                act.activation(bs[s.u], bank(1 + s.u), ACT.Silu, scale=1.0 / SCALE_B).then_inc(b_sil, 1)

            def b_split(s):
                act.wait_ge(b_aT, s.t + 1)
                before(act, b_y, s.t, 2)
                act.copy(bpT[s.u][:, 0, :], bank(3)).then_inc(b_hi, 1)

            act.wait_ge(z_done, T)
            act.wait_ge(x1_out[0], 16 * HALF)
            act.wait_ge(x1_out[1], 16 * HALF)
            pipeline(act, J_B, [(-1, b_evac), (0, b_silu), (0, b_split), (0, lambda s: split_hi(s, s.t, s.u, s.h))])

            def s_split(s):
                act.wait_ge(s_h, s.t + 1)
                before(act, s_hout[s.u], s.h, 1, 16)
                before(act, s_T, s.t, 2)
                act.copy(rowsS[s.u][:, 0:D], hS).then_inc(s_hi, 1)

            def s_evac(s):
                act.wait_ge(s_T, s.t + 1)
                before(act, s_lg, s.t, 1)
                act.copy(hTS.rearrange("p a n -> p (a n)"), bank(0).bitcast(F16)).then_inc(s_ev, 1)

            def s_w(s):
                if isinstance(s.t, int) and s.t == W_FREE:
                    slot_9_free(act)
                q, odd = s.t + J_B, J_B % 2
                c = s.u + odd
                split_hi(s, q, c % 2, s.h + (J_B // 2 + c // 2))

            def c_evac(s):
                act.wait_ge(c_T, s.t + 1)
                before(act, c_gu, s.t, 2)
                act.copy(hT[s.u][:].rearrange("p a n -> p (a n)"), bank(0).bitcast(F16)).then_inc(c_ev, 1)

            def c_silu(s):
                act.wait_ge(c_gu, s.t + 1)
                before(act, c_pT, s.t, 1)
                act.activation(cs[:, 0:IC], bank(1 + s.u, IC), ACT.Silu, scale=1.0 / SCALE_C).then_inc(c_sil, 1)

            def c_split(s):
                act.wait_ge(c_pT, s.t + 1)
                before(act, c_dn, s.t, 1)
                act.copy(cpT[:, 0, :], bank(5, ICP)).then_inc(c_hi_s, 1)

            act.wait_ge(b_y, J_B)
            pipeline(act, TILES, [(0, c_silu), (-1, c_evac), (-1, s_w, (0, W_REST)), (-3, s_split, (0, T)), (-2, s_evac, (0, T)),
                                  (0, c_split)], end=S_ROUNDS)
            act.wait_ge(exp_done, 1)
            act.activation(rt[:], rt[:], ACT.Exp).then_inc(exp_done, 1)
            pipeline(act, TILES, [(0, c_silu), (-1, c_evac), (-1, s_w, (0, W_REST)), (0, c_split)], begin=S_ROUNDS, end=R0)
            pipeline(act, TILES, [(0, c_silu), (-1, c_evac), (0, c_split)], begin=R0, kind=(R0, R1))

        @block.vector
        def _(dve):
            r = [0]

            def step(ins):
                r[0] += 1
                ins.then_inc(route, 1)
                dve.wait_ge(route, r[0])

            def routing(experts, tiles_, chosen, inv, experts_of, pos, done, rank_sums, inv_sums, n_mm, n_inv, n_sel, beside):
                E = experts
                step(dve.memset(ohsum[:, 0, 0:E], 0.0))
                for t in range(T):
                    step(dve.tensor_tensor(ohsum[:, t + 1, 0:E], ohsum[:, t, 0:E], oh[:, t, 0:E], ALU.add))
                dve.sem_inc(route_mm, 1)
                beside()
                dve.wait_ge(route_mm, n_mm + 2)
                step(dve.tensor_copy(rank[:, :, 0:E], rank_sums.rearrange("p (t e) -> p t e", e=E)))
                step(dve.tensor_scalar(eI[:, 0:E], rank[:, T, 0:E], float(P - 1), None, ALU.add))
                step(dve.tensor_scalar(eI[:, 0:E], eI[:, 0:E], 7, None, ALU.logical_shift_right))
                step(dve.tensor_copy(eF[:, 0, 0:E], eI[:, 0:E]))
                step(dve.tensor_copy(eF[:, 1, 0:E], eF[:, 0, 0:E]))
                for e in range(1, E):
                    step(dve.tensor_tensor(eF[:, 1, e:e + 1], eF[:, 1, e:e + 1], eF[:, 1, e - 1:e], ALU.add))
                step(dve.tensor_tensor(eF[:, 2, 0:E], eF[:, 1, 0:E], eF[:, 0, 0:E], ALU.subtract))
                step(dve.tensor_scalar(jF[:, 0:tiles_], iotaF[:, 0:tiles_], eF[:, 1, 0:1], None, ALU.is_ge))
                for e in range(1, E):
                    step(dve.scalar_tensor_tensor(out=jF[:, 0:tiles_], in0=iotaF[:, 0:tiles_], scalar=eF[:, 1, e:e + 1],
                                                  in1=jF[:, 0:tiles_], op0=ALU.is_ge, op1=ALU.add))
                step(dve.tensor_scalar(experts_of[:], jF[:, 0:tiles_], float(E - 1), None, ALU.min))
                for c, one in enumerate(chosen):
                    step(dve.tensor_tensor(rt2[:, :, 0:E], one[:, :, 0:E], rank[:, 0:T, 0:E], ALU.mult))
                    step(dve.tensor_reduce(rF[:, 0, :], rt2[:, :, 0:E], AX.X, ALU.add))
                    step(dve.tensor_tensor(rt2[:, :, 0:E], one[:, :, 0:E], eF[:, 2:3, 0:E].broadcast_to([P, T, E]), ALU.mult))
                    step(dve.tensor_reduce(rF[:, 1, :], rt2[:, :, 0:E], AX.X, ALU.add))
                    step(dve.tensor_copy(rI[:, 0, :], rF[:, 0, :]))
                    step(dve.tensor_scalar(rI[:, 1, :], rI[:, 0, :], 7, None, ALU.logical_shift_right))
                    step(dve.tensor_copy(rF[:, 2, :], rI[:, 1, :]))
                    step(dve.scalar_tensor_tensor(out=rF[:, 3, :], in0=rF[:, 2, :], scalar=-float(P), in1=rF[:, 0, :],
                                                  op0=ALU.mult, op1=ALU.add))
                    step(dve.tensor_tensor(rF[:, 2, :], rF[:, 2, :], rF[:, 1, :], ALU.add))
                    step(dve.scalar_tensor_tensor(out=posF[:], in0=rF[:, 2, :], scalar=float(P), in1=rF[:, 3, :],
                                                  op0=ALU.mult, op1=ALU.add))
                    step(dve.tensor_copy(pos[c][:], posF[:]))
                    beside()
                    for t in range(T):
                        n = c * T + t
                        if n >= SELS:
                            dve.wait_ge(inv_mm, n_inv + n - SELS + 1)
                        dve.tensor_scalar(selR[n % SELS][:], iotaF[:], rF[:, 3, t:t + 1], None, ALU.is_equal).then_inc(sel_done, 1)
                        dve.tensor_scalar(selJ[n % SELS][:, 0:tiles_], iotaF[:, 0:tiles_], rF[:, 2, t:t + 1], tokid[:, t:t + 1],
                                          ALU.is_equal, ALU.mult).then_inc(sel_done, 1)
                        if t == T // 2 - 1:
                            beside()
                beside()
                dve.wait_ge(inv_mm, n_inv + len(chosen) * T)
                step(dve.tensor_copy(inv[:], inv_sums))
                dve.sem_inc(done, 1)

            dve.wait_ge(consts, CONSTS)
            dve.tensor_copy(eyeH[:], eyeF[:]).then_inc(const_steps, 1)
            dve.tensor_copy(eyeB[:], eyeF[:]).then_inc(const_steps, 1)
            step(dve.tensor_copy(iotaF[:], iotaI[:]))
            step(dve.tensor_copy(tokid[:], tokidI[:]))

            dve.wait_ge(tok_in, 16)
            step(dve.tensor_copy(tokF[:], tokI[:]))
            step(dve.memset(oh12[0][:, :, 0:1], 1.0))
            for e in range(1, E_B):
                step(dve.tensor_scalar(oh12[0][:, :, e], tokF[:], float(e * PER_EXPERT), None, ALU.is_ge))
            for e in range(E_B - 1):
                step(dve.tensor_tensor(oh12[0][:, :, e], oh12[0][:, :, e], oh12[0][:, :, e + 1], ALU.subtract))
            step(dve.tensor_copy(oh[:, :, 0:E_B], oh12[0][:, :, 0:E_B]))
            routing(E_B, J_B, oh12[:1], invB, expB, [posB], routeB, bank(6, (T + 1) * E_B), bank(7, J_B), 0, 0, 0, lambda: None)

            def x_moments(s):
                dve.wait_ge(x_in[s.u], (s.h + 1) * 16)
                before(dve, x_small, s.t, 2)
                dve.bn_stats(stats[s.u][:], xin[s.u]).then_inc(x_stats, 1)
                alone(dve, "dve", x_stats, s.t + 1)
                dve.bn_aggr(mv[s.u][:], stats[s.u][:]).then_inc(x_mom, 1)

            def x_center(s):
                before(dve, x_mag, s.t, 2)
                dve.wait_ge(x_mom, s.t + 1)
                if isinstance(s.t, int) and s.t == 0:
                    dve.wait_ge(gains_in, 32)
                dve.scalar_tensor_tensor(out=xcen[s.u], in0=xin[s.u], scalar=mv[s.u][:, 0:1], in1=gg,
                                         op0=ALU.subtract, op1=ALU.mult).then_inc(x_cen, 1)

            def x_absmax(s):
                dve.wait_ge(x_cen, s.t + 1)
                dve.tensor_reduce(xmax[s.u][:], xcen[s.u], AX.X, ALU.max, apply_absolute_value=True).then_inc(x_max, 1)

            def x_factor(s):
                dve.wait_ge(smA_s, (s.t + 1) * 3)
                before(dve, x_mag, s.t, 2)
                dve.reciprocal(cx[s.u][:], smA[s.u][:, 2:3]).then_inc(x_rec, 1)
                dve.wait_ge(x_rec, s.t + 1)
                dve.tensor_scalar(cx[s.u][:], cx[s.u][:], smA[s.u][:, 1:2], 127.0, ALU.mult, ALU.mult).then_inc(x_small, 1)

            def g_factor(s):
                dve.wait_ge(smG_s, (s.t + 1) * 3)
                before(dve, d_mag, s.t, 2)
                dve.reciprocal(cg[s.u][:], smG[s.u][:, 2:3]).then_inc(g_rec, 1)
                dve.wait_ge(g_rec, s.t + 1)
                dve.tensor_scalar(cg[s.u][:], cg[s.u][:], smG[s.u][:, 1:2], 127.0, ALU.mult, ALU.mult).then_inc(g_small, 1)

            def x_int(s):
                dve.wait_ge(x_mag, s.t + 1)
                before(dve, x_T, s.t, 2)
                dve.tensor_scalar(xq[s.u], xmag[s.u], MAGIC, 127.0, ALU.subtract, ALU.min).then_inc(x_q, 1)

            def swiglu(s, c):
                dve.wait_ge(sil_done, s.t * CA + (c + 1))
                if c == 0:
                    before(dve, sq_done, s.t, 2)
                    before(dve, swg_done, s.t, 2, HALVES)
                    dve.wait_ge(x_dq, s.t + 1)
                dve.scalar_tensor_tensor(out=sw[s.u][:, c * CW:(c + 1) * CW], in0=bank(2 + c % 2, CW), scalar=dqx[s.u][:],
                                         in1=sil[c % 2], op0=ALU.mult, op1=ALU.mult).then_inc(sw_done, 1)

            def g_absmax(s):
                dve.wait_ge(swg_done, (s.t + 1) * HALVES)
                before(dve, g_small, s.t, 2)
                dve.tensor_reduce(gmax[s.u][:], swg[s.u], AX.X, ALU.max, apply_absolute_value=True).then_inc(g_max, 1)

            def d_int(s):
                dve.wait_ge(d_mag, s.t + 1)
                before(dve, d_T, s.t, 2)
                dve.tensor_scalar(qd[s.u], swg[s.u], MAGIC, 127.0, ALU.subtract, ALU.min).then_inc(d_q, 1)

            def residual1(s):
                dve.wait_ge(z_done, s.t + 1)
                dve.wait_ge(g_dq, s.t + 1)
                dve.wait_ge(xr_in[s.u], (s.h + 1) * 16)
                before(dve, x1_out[s.u], s.h, 1, 16)
                before(dve, h_done, s.t, 2)
                dve.scalar_tensor_tensor(out=x1[s.u], in0=bank(7), scalar=dqg[s.u][:], in1=xres[s.u],
                                         op0=ALU.mult, op1=ALU.add).then_inc(x1_done, 1)

            def moments1(s):
                dve.wait_ge(x1_done, s.t + 1)
                before(dve, rs1, s.t, 1)
                dve.bn_stats(stats1[:], x1[s.u]).then_inc(st1, 1)
                alone(dve, "dve", st1, s.t + 1)
                before(dve, h_done, s.t, 1)
                dve.sem_inc(passed["dve"], 1)
                dve.bn_aggr(mv1[:], stats1[:]).then_inc(mo1, 1)

            def norm1(s):
                dve.wait_ge(rs1, s.t + 1)
                before(dve, hi_done, s.t, 1)
                before(dve, lo_done, s.t, 1)
                dve.tensor_scalar(hA, x1[s.u], mv1[:, 0:1], rstd1[:], ALU.subtract, ALU.mult).then_inc(h_done, 1)

            def ctx_rest(s):
                dve.wait_ge(ctx_hi, s.t + 1)
                at = bass.ds(s.t * D, D)
                dve.scalar_tensor_tensor(out=c_lo[:, at], in0=wstage[s.u][:, 0:D], scalar=SCALE_B, in1=c_hi[:, at],
                                         op0=ALU.mult, op1=ALU.subtract).then_inc(ctx_lo, 1)

            stages = [(3, residual1), (0, lambda s: swiglu(s, 0)), (1, g_absmax), (0, lambda s: swiglu(s, 1)),
                      (-3, x_moments), (3, moments1), (-2, x_factor), (-1, x_int), (0, lambda s: swiglu(s, 2)), (1, g_factor),
                      (3, norm1), (-3, x_center), (0, lambda s: swiglu(s, 3)), (-3, x_absmax), (0, ctx_rest), (1, d_int)]
            pipeline(dve, T, stages, end=-2)

            dve.wait_ge(gw_done, 1)
            dve.scalar_tensor_tensor(out=gw_lo[:], in0=gw32[:], scalar=SCALE_C, in1=gw_hi[:],
                                     op0=ALU.mult, op1=ALU.subtract).then_inc(gw_done, 1)
            def mean(i, pieces, b_at, size):
                dve.wait_ge(tot_done, i + 1)
                step(dve.tensor_reduce(wmean[:, i:i + 1], bank(7, pieces, b_at), AX.X, ALU.add))
                step(dve.tensor_scalar(wmean[:, i:i + 1], wmean[:, i:i + 1], 1.0 / size, EPS_Q, ALU.mult, ALU.max))
                step(dve.tensor_scalar(wm127[:, i:i + 1], wmean[:, i:i + 1], 1.0 / 127.0, None, ALU.mult))
                dve.reciprocal(winv[:, i:i + 1], wmean[:, i:i + 1]).then_inc(means_done, 1)

            def ternary(dst, rounded, n):
                dve.wait_ge(round_done, n + 1)
                dve.tensor_scalar(dst, rounded, MAGIC, 1.0, ALU.subtract, ALU.min).then_inc(clip_done, 1)
                dve.wait_ge(clip_done, n + 1)
                dve.tensor_scalar(dst, dst, -1.0, None, ALU.max).then_inc(tern_done, 1)

            mean(0, KD, 128, OG * D)
            for k in range(KD):
                ternary(wgT[k], wg32[k], k)
            pipeline(dve, T, stages, begin=-2, end=1)
            mean(1, 2, 0, IA * D)
            for half in range(2):
                at = slice(half * OG, (half + 1) * OG)
                ternary(wdT[:, at], wd32[:, at], KD + half)
            pipeline(dve, T, stages, begin=1)

            def split_lo(q, u):
                at = bass.ds(q * CHUNK, CHUNK)
                dve.wait_ge(whi_done, q + 1)
                dve.scalar_tensor_tensor(out=w_lo[:, at], in0=wstage[u][:], scalar=SCALE_C, in1=w_hi[:, at],
                                         op0=ALU.mult, op1=ALU.subtract).then_inc(wlo_done, 1)

            def b_prod(s):
                dve.wait_ge(b_sil, s.t + 1)
                dve.tensor_tensor(bs[s.u], bank(1 + s.u), bs[s.u], ALU.mult).then_inc(b_a, 1)

            def b_rest(s):
                dve.wait_ge(b_hi, s.t + 1)
                dve.tensor_tensor(bpT[s.u][:, 1, :], bank(3), bpT[s.u][:, 0, :], ALU.subtract).then_inc(b_lo, 1)

            def b_rows_out(s):
                dve.wait_ge(b_y, s.t + 1)
                before(dve, b_out[s.u], s.h, 1, 16)
                dve.tensor_copy(yrow[s.u][:], bank(4 + s.u)).then_inc(b_yev, 1)

            pipeline(dve, J_B, [(0, b_prod), (0, b_rest), (1, b_rows_out), (0, lambda s: split_lo(s.t, s.u))])

            def residual2(s):
                dve.wait_ge(s_x[s.u], (s.h + 1) * 16)
                dve.wait_ge(s_y[s.u], (s.h + 1) * 16)
                dve.scalar_tensor_tensor(out=xS[s.u], in0=yS[s.u], scalar=1.0 / SCALE_B ** 2, in1=xS[s.u],
                                         op0=ALU.mult, op1=ALU.add).then_inc(s_x2, 1)
                dve.wait_ge(s_x2, s.t + 1)
                before(dve, s_rs, s.t, 1)
                dve.bn_stats(stats1[:], xS[s.u]).then_inc(s_st, 1)
                alone(dve, "dve", s_st, s.t + 1)
                before(dve, s_h, s.t, 1)
                dve.sem_inc(passed["dve"], 1)
                dve.bn_aggr(mv1[:], stats1[:]).then_inc(s_mo, 1)

            def norm2(s):
                dve.wait_ge(s_rs, s.t + 1)
                before(dve, s_hi, s.t, 1)
                before(dve, s_lo, s.t, 1)
                dve.tensor_scalar(hS, xS[s.u], mv1[:, 0:1], rstd1[:], ALU.subtract, ALU.mult).then_inc(s_h, 1)

            def s_rest(s):
                dve.wait_ge(s_hi, s.t + 1)
                dve.tensor_tensor(rowsS[s.u][:, D:2 * D], hS, rowsS[s.u][:, 0:D], ALU.subtract).then_inc(s_lo, 1)

            def keep_logits(s):
                dve.wait_ge(s_lg, s.t + 1)
                dve.tensor_scalar(logits[:, bass.ds(s.t, 1), :].rearrange("p a e -> p (a e)"), bank(7, E_C),
                                  1.0 / SCALE_C, None, ALU.mult).then_inc(s_lgev, 1)

            def s_w(s):
                if isinstance(s.t, int) and s.t == W_FREE:
                    slot_9_free(dve)
                split_lo(s.t + J_B, (s.u + J_B) % 2)

            def c_prod(s):
                dve.wait_ge(c_sil, s.t + 1)
                dve.tensor_tensor(cs[:, 0:IC], bank(3 + s.u, IC), cs[:, 0:IC], ALU.mult).then_inc(c_p, 1)

            def c_rest(s):
                dve.wait_ge(c_hi_s, s.t + 1)
                dve.tensor_tensor(cpT[:, 1, :], bank(5, ICP), cpT[:, 0, :], ALU.subtract).then_inc(c_lo_s, 1)

            def c_rows_out(s):
                dve.wait_ge(c_dn, s.t + 1)
                if isinstance(s.t, int) and s.t < 2:
                    dve.wait_ge(b_out[s.u], 16 * ((J_B + 1 - s.u) // 2))
                before(dve, c_out[s.u], s.h, 1, 16)
                dve.tensor_copy(yrow[s.u][:], bank(6)).then_inc(c_yev, 1)

            dve.wait_ge(b_y, J_B)
            dve.memset(cs[:, IC:ICP], 0.0).then_inc(pad_done, 1)
            beside_stages = [(0, c_prod), (-1, s_w, (0, W_REST)), (0, c_rest), (1, c_rows_out)]
            pipeline(dve, TILES, [(-3, residual2, (0, T)), (0, c_prod), (-1, keep_logits, (0, T)), (-3, norm2, (0, T)),
                                  (-1, s_w, (0, W_REST)), (-3, s_rest, (0, T)), (0, c_rest), (1, c_rows_out)], end=S_ROUNDS)
            rounds_beside = iter(range(S_ROUNDS, TILES))

            def beside():
                r = next(rounds_beside)
                pipeline(dve, TILES, beside_stages, begin=r, end=r + 1)

            dve.wait_ge(s_lgev, T)
            step(dve.tensor_copy(rt2[:], logits[:]))
            iota_e = iotaF[:, 0:E_C].rearrange("p (a e) -> p a e", a=1).broadcast_to([P, T, E_C])

            def over_e(ap):
                return ap.rearrange("p (t a) -> p t a", a=1).broadcast_to([P, T, E_C])

            for c in range(2):
                step(dve.tensor_reduce(m12[:, c, :], rt2[:], AX.X, ALU.max))
                step(dve.tensor_tensor(oh12[c][:], rt2[:], over_e(m12[:, c, :]), ALU.not_equal))
                step(dve.tensor_scalar(oh12[c][:], oh12[c][:], 64.0, None, ALU.mult))
                step(dve.tensor_tensor(oh12[c][:], oh12[c][:], iota_e, ALU.add))
                step(dve.tensor_reduce(wsum[:], oh12[c][:], AX.X, ALU.min))
                step(dve.tensor_tensor(oh12[c][:], iota_e, over_e(wsum[:]), ALU.is_equal))
                if c == 0:
                    step(dve.tensor_scalar(rt[:], oh12[c][:], -3.0e38, None, ALU.mult))
                    step(dve.tensor_tensor(rt2[:], rt2[:], rt[:], ALU.add))
            step(dve.tensor_tensor(rt[:], logits[:], over_e(m12[:, 0, :]), ALU.subtract))
            dve.sem_inc(exp_done, 1)
            beside()
            step(dve.tensor_tensor(oh[:], oh12[0][:], oh12[1][:], ALU.add))
            routing(E_C, J_C, oh12, invC, expC, posC, routeC, bank(7, (T + 1) * E_C), bank(7, J_C, 256), 2, T, 2 * T, beside)
            dve.wait_ge(exp_done, 2)
            step(dve.tensor_reduce(wsum[:], rt[:], AX.X, ALU.add))
            step(dve.reciprocal(wsum[:], wsum[:]))
            step(dve.tensor_scalar(wsum[:], wsum[:], 1.0 / SCALE_C ** 2, None, ALU.mult))
            for c in range(2):
                step(dve.tensor_tensor(rt2[:], oh12[c][:], rt[:], ALU.mult))
                step(dve.tensor_reduce(posF[:], rt2[:], AX.X, ALU.add))
                step(dve.tensor_tensor(wtop[c][:], posF[:], wsum[:], ALU.mult))
            pipeline(dve, TILES, beside_stages, begin=next(rounds_beside), end=R0)
            pipeline(dve, TILES, [(0, c_prod), (0, c_rest), (1, c_rows_out)], begin=R0, end=R1 + 2, kind=(R0, R1))

            def f_sum(s):
                pair, odd, turn = output_pair(s)
                for i in range(2):
                    slot, n = odd * 2 + i, pair * 2 + i
                    terms = ((shF[slot][:, 0, :], 1.0 / SCALE_C ** 2), (shF[slot][:, 1, :], 1.0 / SCALE_C ** 2),
                             (yF[0][slot], wtop[0][:, bass.ds(n, 1)]), (yF[1][slot], wtop[1][:, bass.ds(n, 1)]))
                    dve.wait_ge(f_x[slot], (turn + 1) * 32)
                    for k, (term, factor) in enumerate(terms):
                        if k > 0:
                            dve.wait_ge(f_a, n * 3 + k)
                        if k == 2:
                            dve.wait_ge(f_y[slot], (turn + 1) * 32)
                        dve.scalar_tensor_tensor(out=xF[slot], in0=term, scalar=factor, in1=xF[slot],
                                                 op0=ALU.mult, op1=ALU.add).then_inc(f_a if k < 3 else f_o, 1)

            pipeline(dve, TILES, [(0, c_prod), (0, c_rest), (1, c_rows_out), (2, f_sum, (TILES - PAIRS, TILES))], begin=R1 + 2)

        @block.tensor
        def _(pe):
            def route_sums(experts, n_mm, b):
                E = experts
                pe.wait_ge(route_mm, n_mm + 1)
                pe.matmul(bank(b, (T + 1) * E), onesH[:], ohsum[:, :, 0:E], start=True, stop=False)
                pe.matmul(bank(b, T * E), triH[:], oh[:, :, 0:E], start=False, stop=True).then_inc(route_mm, 1)

            def route_inverse(to, tiles_, numbers, count, n_sel):
                for n in numbers:
                    pe.wait_ge(sel_done, n_sel + 2 * n + 2)
                    pe.matmul(to, selR[n % SELS][:], selJ[n % SELS][:, 0:tiles_],
                              start=(n == 0), stop=(n == count - 1)).then_inc(inv_mm, 1)

            pe.wait_ge(consts, CONSTS)
            pe.wait_ge(const_steps, 5)
            route_sums(E_B, 0, 6)
            route_inverse(bank(7, J_B), J_B, range(T), T, 0)
            pe.wait_ge(abs_done, KD)
            pe.wait_ge(routeB, 1)
            pe.matmul(bank(7, KD, 128), onesF[:], asum[:, 0:KD], start=True, stop=True).then_inc(tot_done, 1)

            def x_turn(s):
                pe.wait_ge(x_q, s.t + 1)
                before(pe, x_ev, s.t, 1)
                for k in range(KD):
                    mm = pe.transpose(bank(4, 256).bitcast(BF16)[:, k * P:(k + 1) * P], xq[s.u][:, k * P:(k + 1) * P], eyeB[:])
                mm.then_inc(x_T, 1)

            def gate_up(s, c):
                if c == 0:
                    if isinstance(s.t, int) and s.t == 0:
                        pe.wait_ge(tern_done, KD)
                    pe.wait_ge(x_ev, s.t + 1)
                if not (isinstance(s.t, int) and s.t == 0 and c < 2):
                    pe.wait_ge(sw_done, s.t * CA + (c - 1))
                for half in range(2):
                    at = half * IA + c * CW
                    for k in range(KD):
                        mm = pe.matmul(bank(2 * half + c % 2, CW), xqT[s.u][:, k * P:(k + 1) * P], wgT[k][:, at:at + CW],
                                       start=(k == 0), stop=(k == KD - 1))
                mm.then_inc(gu_done, 1)

            def d_turn(s):
                pe.wait_ge(d_q, s.t + 1)
                before(pe, d_ev, s.t, 1)
                for k in range(KI):
                    mm = pe.transpose(wide(5, IA // 2).bitcast(BF16)[:, k * P:(k + 1) * P], qd[s.u][:, k * P:(k + 1) * P], eyeB[:])
                mm.then_inc(d_T, 1)

            def down(s):
                if isinstance(s.t, int) and s.t == 0:
                    pe.wait_ge(tern_done, KD + 2)
                pe.wait_ge(d_ev, s.t + 1)
                before(pe, x1_done, s.t, 1)
                for k in range(KI):
                    mm = pe.matmul(bank(7), qdT[s.u][:, k * P:(k + 1) * P], wdT[:, k * D:(k + 1) * D],
                                   start=(k == 0), stop=(k == KI - 1))
                mm.then_inc(z_done, 1)

            stages = [(0, lambda s: gate_up(s, 0)), (2, d_turn), (0, lambda s: gate_up(s, 1)), (2, down),
                      (0, lambda s: gate_up(s, 2)), (0, lambda s: gate_up(s, 3)), (-1, x_turn)]
            pipeline(pe, T, stages, end=1)
            pe.wait_ge(abs_done, KD + 2)
            pe.matmul(bank(7, 2), onesF[:], asum[:, KD:KD + 2], start=True, stop=True).then_inc(tot_done, 1)
            pipeline(pe, T, stages, begin=1)

            def turn_rows(s, rows_in, count, evacuated, done):
                pe.wait_ge(rows_in, count * 16)
                before(pe, evacuated, s.t, 1)
                for k in range(2 * KD):
                    mm = pe.transpose(bank(0).bitcast(F16)[:, k * P:(k + 1) * P], rows[s.u][:, k * P:(k + 1) * P], eyeH[:])
                mm.then_inc(done, 1)

            def split_product(to, a, w, steps):
                for k in range(steps):
                    for n, (pa, pw) in enumerate(((0, 0), (0, 1), (1, 0))):
                        mm = pe.matmul(to, a(k, pa), w(k, pw), start=(k == 0 and n == 0), stop=(k == steps - 1 and n == 2))
                return mm

            def b_turn(s):
                turn_rows(s, b_rows[s.u], s.h + 1, b_ev, b_T)

            expert = {}

            def b_first(s):
                pe.wait_ge(b_ev, s.t + 1)
                before(pe, b_a, s.t, 2)
                pe.sem_inc(passed["pe"], 1)
                e = pe.value_load(expB[0:1, bass.ds(s.t, 1)], min_val=0, max_val=E_B - 1)
                split_product(bank(1 + s.u), lambda k, p: hT[s.u][:, p * KD + k, :],
                              lambda k, p: (c_hi, c_lo)[p][:, bass.ds(e * (KD * D) + k * D, D)], KD).then_inc(b_t, 1)

            def b_turn_a(s):
                pe.wait_ge(b_a, s.t + 1)
                before(pe, b_lo, s.t, 1)
                for k in range(KD):
                    mm = pe.transpose(bank(3, P, k * P), bs[s.u][:, k * P:(k + 1) * P], eyeF[:])
                mm.then_inc(b_aT, 1)

            def b_second(s):
                pe.wait_ge(b_lo, s.t + 1)
                before(pe, b_yev, s.t, 2)
                pe.sem_inc(passed["pe"], 1)
                e = pe.value_load(expB[0:1, bass.ds(s.t, 1)], min_val=0, max_val=E_B - 1)
                split_product(bank(4 + s.u), lambda k, p: bpT[s.u][:, p, k * P:(k + 1) * P],
                              lambda k, p: (c_hi, c_lo)[p][:, bass.ds(e * (KD * D) + k * D, D)], KD).then_inc(b_y, 1)

            pe.wait_ge(ctx_lo, T)
            pe.wait_ge(x1_done, T)
            pipeline(pe, J_B, [(0, b_first), (-1, b_turn), (1, b_second), (0, b_turn_a)])

            def s_turn(s):
                pe.wait_ge(s_hi, s.t + 1)
                pe.wait_ge(s_lo, s.t + 1)
                before(pe, c_ev, s.t, 1)
                for k in range(2 * KD):
                    mm = pe.transpose(bank(0).bitcast(F16)[:, k * P:(k + 1) * P], rowsS[s.u][:, k * P:(k + 1) * P], eyeH[:])
                mm.then_inc(s_T, 1)

            def s_router(s):
                pe.wait_ge(s_ev, s.t + 1)
                before(pe, s_lgev, s.t, 1)
                split_product(bank(7, E_C), lambda k, p: hTS[:, p * KD + k, :],
                              lambda k, p: (gw_hi, gw_lo)[p][:, k * E_C:(k + 1) * E_C], KD).then_inc(s_lg, 1)

            def c_turn(s):
                pe.wait_ge(s_ev, min(s.t + 1, T) if isinstance(s.t, int) else T if routed(s) or s.first >= R1 else s.t + 1)
                turn_rows(s, (c_rows if routed(s) else c_shared)[s.u], rows_count(s), c_ev, c_T)

            def slot_of(s):
                if not routed(s):
                    return shared_part(s)[1] * SLOT
                e = pe.value_load(expC[0:1, bass.ds(s.t - R0, 1)], min_val=0, max_val=E_C - 1)
                return e * SLOT + SHARES * SLOT

            def weights(slot, p, at, n):
                return (w_hi, w_lo)[p][:, bass.ds(slot + at, n)]

            def c_gate_up(s):
                pe.wait_ge(c_ev, s.t + 1)
                before(pe, c_p, s.t, 2)
                pe.sem_inc(passed["pe"], 1)
                slot = slot_of(s)
                for half in range(2):
                    mm = split_product(bank(1 + 2 * half + s.u, IC), lambda k, p: hT[s.u][:, p * KD + k, :],
                                       lambda k, p: weights(slot, p, (2 * k + half) * IC, IC), KD)
                mm.then_inc(c_gu, 1)

            def c_turn_p(s):
                pe.wait_ge(c_p, s.t + 1)
                before(pe, c_lo_s, s.t, 1)
                for k in range(ICP // P):
                    mm = pe.transpose(bank(5, P, k * P), cs[:, k * P:(k + 1) * P], eyeF[:])
                mm.then_inc(c_pT, 1)

            def c_down(s):
                pe.wait_ge(c_lo_s, s.t + 1)
                before(pe, c_yev, s.t, 1)
                pe.sem_inc(passed["pe"], 1)
                slot = slot_of(s)
                split_product(bank(6), lambda k, p: cpT[:, p, k * P:(k + 1) * P],
                              lambda k, p: weights(slot, p, KD * 2 * IC + k * D, D), ICP // P).then_inc(c_dn, 1)

            c_stages = [(0, c_gate_up), (-1, c_turn), (1, c_down), (0, c_turn_p)]
            pe.wait_ge(gw_done, 2)
            pe.wait_ge(wlo_done, SHARES * LOADS_PER_SLOT)
            pe.wait_ge(b_yev, J_B)
            pe.wait_ge(pad_done, 1)
            pipeline(pe, TILES, [(0, c_gate_up), (-1, c_turn), (-1, s_router, (0, T)), (1, c_down), (-2, s_turn, (0, T)),
                                 (0, c_turn_p)], end=S_ROUNDS)
            pipeline(pe, TILES, c_stages, begin=S_ROUNDS, end=S_ROUNDS + 1)
            pe.wait_ge(s_lgev, T)
            route_sums(E_C, 2, 7)
            pipeline(pe, TILES, c_stages, begin=S_ROUNDS + 1, end=S_ROUNDS + 3)
            for r in range(S_ROUNDS + 3, S_ROUNDS + 7):
                pipeline(pe, TILES, c_stages, begin=r, end=r + 1)
                n = (r - S_ROUNDS - 3) * (T // 2)
                route_inverse(bank(7, J_C, 256), J_C, range(n, n + T // 2), 2 * T, 2 * T)
            pipeline(pe, TILES, c_stages, begin=S_ROUNDS + 7, end=R0)
            pe.wait_ge(routeC, 1)
            pe.wait_ge(wlo_done, CHUNKS)
            pipeline(pe, TILES, c_stages, begin=R0, kind=(R0, R1))


def layouts(x, tok, w_gate, g_gate, w_down, g_down, ctx, gate_w, we_gate, we_up, we_down, sw_gate, sw_up, sw_down):
    def steps(w):
        return w.reshape(-1, P, w.shape[1]).transpose(1, 0, 2)

    def padded(w, rows):
        return np.concatenate([w, np.zeros((rows - w.shape[0], w.shape[1]), w.dtype)])

    def slot(gate, up, down):
        both = np.concatenate([steps(gate), steps(up)], axis=2).reshape(P, -1)
        return np.concatenate([both, steps(padded(down, ICP)).reshape(P, -1)], axis=1)

    parts = [slice(h * IC, (h + 1) * IC) for h in range(SHARES)]
    slots = [slot(sw_gate[:, a], sw_up[:, a], sw_down[a]) for a in parts]
    slots += [slot(we_gate[e], we_up[e], we_down[e]) for e in range(E_C)]
    moe = np.concatenate(slots, axis=1)
    return {
        "x": x.reshape(N, D),
        "tok": tok.reshape(T, P).T,
        "wgate": steps(w_gate.T).reshape(P, -1),
        "wdown": steps(w_down.T).reshape(P, -1),
        "ggate": g_gate.reshape(1, D),
        "gdown": g_down.reshape(1, IA),
        "ctxt": np.concatenate([steps(ctx[e].T) for e in range(E_B)], axis=1).reshape(P, -1),
        "gatew": steps(gate_w.T).reshape(P, -1),
        "wmoe": moe.reshape(P, CHUNKS, CHUNK).transpose(1, 0, 2).reshape(CHUNKS * P, CHUNK),
    }


_NAMES = ["x", "itok_BxS_13_99985", "L0_attn_w_gate", "L0_attn_g_gate", "L0_attn_w_down", "L0_attn_g_down", "ctx_2048",
          "L0_ffn_gate_w", "L0_ffn_w_gate", "L0_ffn_w_up", "L0_ffn_w_down", "L0_ffn_sw_gate", "L0_ffn_sw_up", "L0_ffn_sw_down"]


def kernel(**inputs):
    import concourse.bacc as bacc
    from concourse.bass_utils import run_bass_kernel_spmd

    given = [np.asarray(inputs[n]) for n in _NAMES]
    arrays = {f"in_{n}": np.ascontiguousarray(a) for n, a in layouts(*given).items()}
    nc = bacc.Bacc("TRN2", target_bir_lowering=False, num_devices=1)
    args = {n[3:]: nc.dram_tensor(n, a.shape, mybir.dt.from_np(a.dtype), kind="ExternalInput").ap() for n, a in arrays.items()}
    out = nc.dram_tensor("out_x", (N, D), F32, kind="ExternalOutput").ap()
    build(nc, out=out, **args)
    result = run_bass_kernel_spmd(nc, [arrays], core_ids=[0])
    return result.results[0]["out_x"].reshape(given[0].shape)
```

```python
from collections import namedtuple
from contextlib import ExitStack

import numpy as np
import concourse.bass as bass
import concourse.mybir as mybir

F32, F16, BF16 = mybir.dt.float32, mybir.dt.float16, mybir.dt.bfloat16
I32 = mybir.dt.int32
ALU = mybir.AluOpType
ACT = mybir.ActivationFunctionType
AX = mybir.AxisListType

P = 128
D = 512
KD = D // P
N = 2048
T = N // P
IA = 1408
KI = IA // P
CW = 352
HALVES = 2
CA = IA // CW
E_B, E_C = 4, 8
J_B = T + E_B - 1
J_C = 2 * T + E_C - 1
VOCAB = 25000
PER_EXPERT = VOCAB // E_B
IC = 352
ICP = 384
IS = 704
SHARES = IS // IC
SLOT = KD * 2 * IC + (ICP // P) * D
LOADS_PER_SLOT = 4
CHUNK = SLOT // LOADS_PER_SLOT
SLOTS = SHARES + E_C
CHUNKS = SLOTS * LOADS_PER_SLOT
assert SHARES == 2 and CHUNK * LOADS_PER_SLOT == SLOT
EPS_LN, EPS_RMS, EPS_Q = 1e-5, 1e-6, 1e-5
MAGIC = 12582912.0
SCALE_B, SCALE_C = 256.0, 64.0

R0 = 24
R1 = R0 + J_C
TILES = SHARES * T + J_C
PAIRS = T // 2
S_ROUNDS = T - 1
SELS = 8

Step = namedtuple("Step", "t u h first")


def pipeline(engine, count, stages, begin=None, end=None, kind=None):
    todo = [(g, stage, *(span[0] if span else (0, count))) for g, stage, *span in stages]
    begin = min(g + lo for g, _, lo, _ in todo) if begin is None else begin
    end = max(g + hi for g, _, _, hi in todo) if end is None else end
    k_lo, k_hi = kind or (0, count)
    first = max(begin, max(g + max(lo, k_lo) + 2 for g, _, lo, _ in todo))
    turns = max(0, (min(end, min(g + min(hi, k_hi) for g, _, _, hi in todo)) - first) // 2)

    def straight(rounds):
        for r in rounds:
            for g, stage, lo, hi in todo:
                if lo <= r - g < hi:
                    stage(Step(r - g, (r - g) % 2, (r - g) // 2, r - g))

    if turns == 0:
        straight(range(begin, end))
        return
    straight(range(begin, first))
    with engine.Fori(0, turns) as i:
        for c in range(2):
            for g, stage, _, _ in todo:
                t = first + c - g
                stage(Step(i * 2 + t, t % 2, i + t // 2, t))
    straight(range(first + 2 * turns, end))


def routed(s):
    return R0 <= s.first < R1


def shared_part(s):
    k = s.first - (0 if s.first < R0 else J_C)
    return s.h + (k // SHARES - s.first // 2), k % SHARES


def results_before(s):
    if routed(s):
        return s.t - (R0 - R0 // SHARES)
    return shared_part(s)[0] + (0 if s.first < R0 else J_C)


def rows_slot(s):
    return s.u if routed(s) else (s.first - shared_part(s)[1]) % 2


def output_pair(s):
    k = s.first - (TILES - PAIRS)
    return s.t - (TILES - PAIRS), k % 2, s.h + (k // 2 - s.first // 2)


def before(engine, sem, t, back, per=1):
    if isinstance(t, int) and t < back:
        return
    engine.wait_ge(sem, (t - (back - 1)) * per)


def build(nc, x, tok, wgate, wdown, ggate, gdown, ctxt, gatew, wmoe, out):
    ctx = ExitStack()
    with ctx:
        def sb(name, shape, dt):
            return ctx.enter_context(nc.sbuf_tensor(name, shape, dt))

        def sem(name):
            return ctx.enter_context(nc.semaphore(name))

        def two(name):
            return [sem(f"{name}{i}") for i in range(2)]

        def dram(name, shape, dt):
            return nc.dram_tensor(name, shape, dt, kind="Internal").ap()

        x1_d, x2_d = (dram(n, (N, D), F32) for n in ("x1_d", "x2_d"))
        hB_d, hC_d = (dram(n, (N, 2 * D), F16) for n in ("hB_d", "hC_d"))
        yB_d = dram("yB_d", (J_B * P, D), F32)
        yC_d = dram("yC_d", (J_C * P, D), F32)
        x3_d = dram("x3_d", (N, D), F32)

        w_hi = sb("w_hi", [P, SLOTS * SLOT], F16)
        w_lo = sb("w_lo", [P, SLOTS * SLOT], F16)

        class Carver:

            def __init__(self, tensor, slot, slots):
                self.flat, self.at, self.end = tensor, slot * SLOT, (slot + slots) * SLOT

            def take(self, n, dt):
                words = n * (2 if dt == F32 else 1)
                view = self.flat[:, self.at:self.at + words]
                self.at += words
                assert self.at <= self.end
                return view if dt == F16 else view.bitcast(dt)

        stage_hi, stage_lo = Carver(w_hi, 0, 4), Carver(w_lo, 0, 4)
        OG = 2 * IA
        wg32 = [stage_hi.take(OG, F32) for _ in range(3)] + [stage_lo.take(OG, F32)]
        wd32 = stage_lo.take(KI * D, F32)
        tern_hi, tern_lo = Carver(w_hi, 4, 2), Carver(w_lo, 4, 2)
        wgT = [tern_hi.take(OG, BF16) for _ in range(3)] + [tern_lo.take(OG, BF16)]
        wdT = tern_lo.take(KI * D, BF16)
        a6h, a6l, a9h, a9l = Carver(w_hi, 6, 1), Carver(w_lo, 6, 1), Carver(w_hi, 9, 1), Carver(w_lo, 9, 1)
        xin = [a6h.take(D, F32) for _ in range(2)]
        xcen = [a6h.take(D, F32) for _ in range(2)]
        xq = [a6l.take(D, BF16) for _ in range(2)]
        xqT = [a6l.take(D, BF16) for _ in range(2)]
        xmag = [a6l.take(D, F32) for _ in range(2)]
        gg = a9h.take(D, F32)
        hA = a9l.take(D, F32)
        eyeB, onesF, iotaI = a9l.take(P, BF16), a9l.take(P, F32), a9l.take(P, F32).bitcast(I32)
        ah, al = Carver(w_hi, 0, 4), Carver(w_lo, 0, 4)
        sw = [ah.take(IA, F32) for _ in range(2)]
        swg = [ah.take(IA, F32) for _ in range(2)]
        sil = [ah.take(CW, F32) for _ in range(2)]
        gd = ah.take(IA, F32)
        squares = ah.take(IA, BF16)
        qd = [al.take(IA, BF16) for _ in range(2)]
        qdT = [al.take(IA, BF16) for _ in range(2)]
        xres = [al.take(D, F32) for _ in range(2)]
        x1 = [al.take(D, F32) for _ in range(2)]
        c_hi, c_lo = Carver(w_hi, 7, 2).take(E_B * KD * D, F16), Carver(w_lo, 7, 2).take(E_B * KD * D, F16)
        b9h = Carver(w_hi, 9, 1)
        bs = [b9h.take(D, F32) for _ in range(2)]
        bpT = [b9h.take(2 * D, F16).rearrange("p (a n) -> p a n", a=2) for _ in range(2)]
        s9h, s9l = Carver(w_hi, 9, 1), Carver(w_lo, 9, 1)
        hS = s9h.take(D, F32)
        xS = [s9h.take(D, F32) for _ in range(2)]
        hTS = s9h.take(2 * D, F16).rearrange("p (a n) -> p a n", n=P)
        yS = [s9l.take(D, F32) for _ in range(2)]
        rowsS = [s9l.take(2 * D, F16) for _ in range(2)]
        xF = Carver(w_hi, SHARES, 4).take(T * D, F32)
        yF = [Carver(w_lo, SHARES, 4).take(T * D, F32), Carver(w_hi, SHARES + 4, 4).take(T * D, F32)]

        wstage = [sb(f"wstage{i}", [P, CHUNK], F32) for i in range(2)]
        rows = [sb(f"rows{i}", [P, 2 * D], F16) for i in range(2)]
        hT = [sb(f"hT{i}", [P, 2 * KD, P], F16) for i in range(2)]
        yrow = [sb(f"yrow{i}", [P, D], F32) for i in range(2)]
        cs = sb("cs", [P, ICP], F32)
        cpT = sb("cpT", [P, 2, ICP], F16)
        eyeF, eyeH = sb("eyeF", [P, P], F32), sb("eyeH", [P, P], F16)
        onesH, triH = sb("onesH", [P, P], F16), sb("triH", [P, P], F16)
        iotaF = sb("iotaF", [P, P], F32)
        tokidI, tokid = sb("tokidI", [P, T], I32), sb("tokid", [P, T], F32)
        powh = sb("powh", [P, 1], F32)
        asum = sb("asum", [P, KD + 2], F32)
        wmean = sb("wmean", [P, 2], F32)
        wm127 = sb("wm127", [P, 2], F32)
        winv = sb("winv", [P, 2], F32)
        tokI, tokF = sb("tokI", [P, T], I32), sb("tokF", [P, T], F32)
        gw32 = sb("gw32", [P, KD * E_C], F32)
        gw_hi, gw_lo = sb("gw_hi", [P, KD * E_C], F16), sb("gw_lo", [P, KD * E_C], F16)
        stats = [sb(f"xstats{i}", [P, 6], F32) for i in range(2)]
        mv = [sb(f"xmv{i}", [P, 2], F32) for i in range(2)]
        xmax = [sb(f"xmax{i}", [P, 1], F32) for i in range(2)]
        smA = [sb(f"smA{i}", [P, 3], F32) for i in range(2)]
        cx = [sb(f"cx{i}", [P, 1], F32) for i in range(2)]
        dqx = [sb(f"dqx{i}", [P, 1], F32) for i in range(2)]
        dqg = [sb(f"dqg{i}", [P, 1], F32) for i in range(2)]
        ssq = [sb(f"ssq{i}", [P, 1], F32) for i in range(2)]
        gmax = [sb(f"gmax{i}", [P, 1], F32) for i in range(2)]
        smG = [sb(f"smG{i}", [P, 3], F32) for i in range(2)]
        cg = [sb(f"cg{i}", [P, 1], F32) for i in range(2)]
        stats1 = sb("stats1", [P, 6], F32)
        mv1 = sb("mv1", [P, 2], F32)
        var1 = sb("var1", [P, 1], F32)
        rstd1 = sb("rstd1", [P, 1], F32)
        W2 = T * E_C
        oh = sb("oh", [P, T, E_C], F16)
        oh12 = sb("oh12", [P, 2, T, E_C], F32)
        zeroH = sb("zeroH", [P, 1, E_C], F16)
        rank = sb("rank", [P, T + 1, E_C], F32)
        rt = sb("rt", [P, T, E_C], F32)
        rt2 = sb("rt2", [P, 2, T, E_C], F32)
        upto = sb("upto", [P, E_C, E_C], F32)
        cmpJ = sb("cmpJ", [P, J_C * E_C], F32)
        eI = sb("eI", [P, E_C], I32)
        eF = sb("eF", [P, 3, E_C], F32)
        rI = sb("rI", [P, 2, 2, T], I32)
        rF = sb("rF", [P, 4, 2, T], F32)
        posF = sb("posF", [P, 2, T], F32)
        posB, posC = sb("posB", [P, 1, T], I32), sb("posC", [P, 2, T], I32)
        selR = sb("selR", [P, SELS, P], F16)
        selJ = sb("selJ", [P, SELS * J_C], F16)
        jF = sb("jF", [P, J_C], F32)
        invB, invC = sb("invB", [P, J_B], I32), sb("invC", [P, J_C], I32)
        expB, expC = sb("expB", [P, J_B], I32), sb("expC", [P, J_C], I32)
        idx = [sb(f"idx{i}", [P, 1], I32) for i in range(2)]
        logits = sb("logits", [P, T, E_C], F32)
        m12 = sb("m12", [P, 2, T], F32)
        wsum = sb("wsum", [P, T], F32)
        wtop = [sb(f"wtop{c}", [P, T], F32) for c in range(2)]

        banks = ctx.enter_context(nc.psum_tensor("banks", [P, 8, 512], F32))

        def bank(b, n=512, at=0):
            return banks[:, b, at:at + n]

        def wide(b, n):
            return banks[:, b:b + 2, :].rearrange("p a n -> p (a n)")[:, 0:n]

        consts, CONSTS = sem("consts"), 6
        const_steps = sem("const_steps")
        tok_in, gains_in = sem("tok_in"), sem("gains_in")
        gd_in = sem("gd_in")
        wg_in = [sem(f"wg_in{k}") for k in range(KD)]
        wd_in = sem("wd_in")
        abs_done, tot_done, means_done = sem("abs_done"), sem("tot_done"), sem("means_done")
        silu_table = sem("silu_table")
        round_done, clip_done = sem("round_done"), sem("clip_done")
        tern_done, gw_done = sem("tern_done"), sem("gw_done")
        passed = {n: sem(f"passed_{n}") for n in ("dve", "pool", "pe", "sp")}
        x_in = two("x_in")
        x_stats, x_mom, x_cen, x_max = sem("x_stats"), sem("x_mom"), sem("x_cen"), sem("x_max")
        x_rec, g_rec, x_dq, g_dq = sem("x_rec"), sem("g_rec"), sem("x_dq"), sem("g_dq")
        x_small, x_mag, x_q, x_T, x_ev = sem("x_small"), sem("x_mag"), sem("x_q"), sem("x_T"), sem("x_ev")
        gu_done, sil_done, sw_done = sem("gu_done"), sem("sil_done"), sem("sw_done")
        swg_done, sq_done, g_max, g_small = sem("swg_done"), sem("sq_done"), sem("g_max"), sem("g_small")
        d_mag, d_q, d_T, d_ev, z_done = sem("d_mag"), sem("d_q"), sem("d_T"), sem("d_ev"), sem("z_done")
        xr_in, x1_out, hb_out = two("xr_in"), two("x1_out"), two("hb_out")
        x1_done, st1, mo1, rs1 = sem("x1_done"), sem("st1"), sem("mo1"), sem("rs1")
        smA_s, smG_s, smB_s = sem("smA_s"), sem("smG_s"), sem("smB_s")
        h_done, hi_done, lo_done = sem("h_done"), sem("hi_done"), sem("lo_done")
        ctx_in, ctx_hi, ctx_lo = two("ctx_in"), sem("ctx_hi"), sem("ctx_lo")
        route = sem("route")
        route_mm, sel_done, inv_mm = sem("route_mm"), sem("sel_done"), sem("inv_mm")
        routeB, routeC = sem("routeB"), sem("routeC")
        w_in, whi_done, wlo_done = two("w_in"), sem("whi_done"), sem("wlo_done")
        b_idx, b_rows, b_T, b_ev = sem("b_idx"), two("b_rows"), sem("b_T"), sem("b_ev")
        b_t, b_sil, b_a, b_aT = sem("b_t"), sem("b_sil"), sem("b_a"), sem("b_aT")
        b_hi, b_lo, b_y, b_yev, b_out = sem("b_hi"), sem("b_lo"), sem("b_y"), sem("b_yev"), two("b_out")
        s_x, s_idx, s_y = two("s_x"), sem("s_idx"), two("s_y")
        s_x2, s_st, s_mo, s_rs, s_small = sem("s_x2"), sem("s_st"), sem("s_mo"), sem("s_rs"), sem("s_small")
        s_h, s_hi, s_lo, s_x2out, s_hout = sem("s_h"), sem("s_hi"), sem("s_lo"), two("s_x2out"), two("s_hout")
        s_T, s_ev, s_lg, s_lgev = sem("s_T"), sem("s_ev"), sem("s_lg"), sem("s_lgev")
        pad_done = sem("pad_done")
        exp_done = sem("exp_done")
        c_idx, c_shared, c_rows, c_T, c_ev = sem("c_idx"), two("c_shared"), two("c_rows"), sem("c_T"), sem("c_ev")
        c_gu, c_sil, c_p, c_pT = sem("c_gu"), sem("c_sil"), sem("c_p"), sem("c_pT")
        c_hi_s, c_lo_s, c_dn, c_yev, c_out = sem("c_phi"), sem("c_plo"), sem("c_dn"), sem("c_yev"), two("c_out")
        sh_x, sh_out = sem("sh_x"), sem("sh_out")
        f_a, f_o = sem("f_a"), sem("f_o")
        f_x, f_y, f_out = two("f_x"), [sem(f"f_y{i}") for i in range(4)], two("f_out")

        CTX = 2 * D
        CTX_CHUNKS = E_B * KD * D // CTX
        CTX_ROUNDS = CTX_CHUNKS // 2
        CTX_FROM = T + 3 - CTX_ROUNDS

        def ctx_chunks(stage):
            return (CTX_FROM, lambda s: [stage(Step(s.t * 2 + u, u, s.t, s.t * 2 + u)) for u in range(2)], (0, CTX_ROUNDS))
        HALF = T // 2

        def tiles(ap, t):
            return ap[bass.ds(t * P, P), :]

        def alone(engine, name, s, value):
            engine.wait_ge(s, value)
            engine.sem_inc(passed[name], 1)

        def slot_9_free(engine):
            engine.wait_ge(s_lg, T)
            engine.wait_ge(s_hi, T)
            engine.wait_ge(s_lo, T)
            for u in range(2):
                engine.wait_ge(s_hout[u], 16 * HALF)
                engine.wait_ge(s_x2out[u], 16 * HALF)

        def out_tiles(flat, n):
            return flat[:, bass.ds(n * D, D)]

        F_LAG = 2
        last = (TILES - PAIRS, TILES)
        summed_first = (TILES - PAIRS, TILES - PAIRS + R0 // SHARES // 2)
        summed_last = (summed_first[1], TILES)
        W_B = J_B // 2 * 2
        W_REST = CHUNKS - W_B
        W_FREE = W_REST - LOADS_PER_SLOT
        W_LAG = -1
        whole = (0, T)
        assert W_LAG + W_FREE >= S_ROUNDS and W_LAG + W_REST <= R0

        block = ctx.enter_context(nc.Block())

        @block.sync
        def _(sp):
            sp.dma_start(tokI[:], tok[:]).then_inc(tok_in, 16)
            sp.dma_start(gg, ggate.broadcast_to([P, D])).then_inc(gains_in, 16)
            sp.dma_start(gw32[:], gatew[:]).then_inc(gains_in, 16)
            for k in range(KD):
                sp.dma_start(wg32[k], wgate[:, k * OG:(k + 1) * OG]).then_inc(wg_in[k], 16)
                if k < 2:
                    sp.dma_start(xin[k], tiles(x, k)).then_inc(x_in[k], 16)

            def load_x(s):
                if isinstance(s.t, int) and s.t < 2:
                    return
                before(sp, x_cen, s.t, 2)
                before(sp, x_stats, s.t, 2)
                sp.dma_start(xin[s.u], tiles(x, s.t)).then_inc(x_in[s.u], 16)

            def load_res(s):
                if isinstance(s.t, int) and s.t == 0:
                    sp.wait_ge(tern_done, KD + 2)
                before(sp, x1_done, s.t, 2)
                sp.dma_start(xres[s.u], tiles(x, s.t)).then_inc(xr_in[s.u], 16)

            def load_ctx(s):
                before(sp, ctx_lo, s.t, 2)
                sp.dma_start(wstage[s.u][:, 0:CTX], ctxt[:, bass.ds(s.t * CTX, CTX)]).then_inc(ctx_in[s.u], 16)

            def store_x1(s):
                sp.wait_ge(x1_done, s.t + 1)
                sp.dma_start(tiles(x1_d, s.t), x1[s.u]).then_inc(x1_out[s.u], 16)

            def store_hb(s):
                sp.wait_ge(hi_done, s.t + 1)
                sp.wait_ge(lo_done, s.t + 1)
                sp.dma_start(tiles(hB_d, s.t), rows[s.u][:]).then_inc(hb_out[s.u], 16)

            stages = [(3, store_x1), (1, load_res), (3, store_hb), (-5, load_x)]
            pipeline(sp, T, stages, end=-2)
            sp.dma_start(wd32, wdown[:]).then_inc(wd_in, 16)
            sp.wait_ge(tern_done, KD)
            sp.dma_start(gd, gdown.broadcast_to([P, IA])).then_inc(gd_in, 16)
            pipeline(sp, T, stages, begin=-2, end=CTX_FROM - 2)
            load_ctx_pair = ctx_chunks(load_ctx)
            pipeline(sp, T, stages + [(load_ctx_pair[0] - 2, *load_ctx_pair[1:])], begin=CTX_FROM - 2)

            def load_w(q, u, wait):
                if wait:
                    sp.wait_ge(wlo_done, q - 1)
                sp.dma_start(wstage[u][:], wmoe[bass.ds(q * P, P), :]).then_inc(w_in[u], 16)

            def b_load(s):
                if isinstance(s.t, int) and s.t < 2:
                    sp.wait_ge(ctx_lo, CTX_CHUNKS)
                load_w(s.t, s.u, not (isinstance(s.t, int) and s.t < 2))

            def b_store(s):
                sp.wait_ge(b_yev, s.t + 1)
                sp.dma_start(tiles(yB_d, s.t), yrow[s.u][:]).then_inc(b_out[s.u], 16)

            pipeline(sp, J_B, [(-1, b_load, (0, W_B)), (1, b_store)])

            def s_load(s):
                before(sp, s_x2out[s.u], s.h, 1, 16)
                before(sp, s_h, s.t, 2)
                sp.dma_start(xS[s.u], tiles(x1_d, s.t)).then_inc(s_x[s.u], 16)

            def s_storex2(s):
                sp.wait_ge(s_x2, s.t + 1)
                sp.dma_start(tiles(x2_d, s.t), xS[s.u]).then_inc(s_x2out[s.u], 16)

            def s_storeh(s):
                sp.wait_ge(s_hi, s.t + 1)
                sp.wait_ge(s_lo, s.t + 1)
                sp.dma_start(tiles(hC_d, s.t), rowsS[s.u]).then_inc(s_hout[s.u], 16)

            def s_stored(s):
                alone(sp, "sp", s_hout[s.u], (s.h + 1) * 16)
                alone(sp, "sp", s_x2out[s.u], (s.h + 1) * 16)

            def s_loadw(s):
                load_w(s.t + W_B, s.u, True)

            def c_rows_in(s):
                tile, half = shared_part(s)
                if half > 0 or isinstance(s.t, int) and s.t == 0:
                    return
                if isinstance(s.t, int) and tile == 1:
                    sp.wait_ge(b_T, J_B)
                sp.wait_ge(c_T, results_before(s))
                sp.dma_start(rows[s.u][:], tiles(hC_d, tile)).then_inc(c_shared[s.u], 16)

            def c_sum_in(s):
                tile, half = shared_part(s)
                if half > 0:
                    return
                if isinstance(s.t, int) and s.t == 0:
                    sp.wait_ge(b_out[0], 16 * ((J_B + 1) // 2))
                if s.first >= R1:
                    alone(sp, "sp", sh_x, tile * 16)
                    sp.dma_start(out_tiles(xF, tile), tiles(x2_d, tile)).then_inc(sh_x, 16)
                    return
                if not (isinstance(s.t, int) and s.t == 0):
                    alone(sp, "sp", sh_out, tile * 16)
                sp.dma_start(yrow[0][:], tiles(x2_d, tile)).then_inc(sh_x, 16)

            def c_store(s):
                if routed(s):
                    sp.wait_ge(c_yev, results_before(s) + 1)
                    sp.dma_start(tiles(yC_d, s.t - R0), yrow[s.u][:]).then_inc(c_out[s.u], 16)
                    return
                tile, half = shared_part(s)
                if half == SHARES - 1 and s.first < R0:
                    sp.wait_ge(c_yev, results_before(s) + 1)
                    sp.dma_start(tiles(x3_d, tile), yrow[0][:]).then_inc(sh_out, 16)

            sp.wait_ge(x1_out[0], 16 * HALF)
            sp.wait_ge(x1_out[1], 16 * HALF)
            sp.wait_ge(b_y, J_B)
            shared_first, shared_last = (0, R0), (R1, TILES)
            w_rest = (0, W_REST)
            pipeline(sp, TILES, [(W_LAG - 1, s_loadw, w_rest), (-2, s_stored, whole), (-2, c_rows_in, shared_first),
                                 (-3, s_storex2, whole), (-3, s_storeh, whole), (-5, s_load, whole), (1, c_store),
                                 (0, c_sum_in, shared_first)], end=S_ROUNDS)
            pipeline(sp, TILES, [(W_LAG - 1, s_loadw, w_rest), (-2, c_rows_in, shared_first), (1, c_store),
                                 (0, c_sum_in, shared_first)], begin=S_ROUNDS, end=R0, kind=(0, R0))
            pipeline(sp, TILES, [(1, c_store)], begin=R0, end=R1 - 2, kind=(R0, R1))

            def rows_of_pair(ap, pair):
                return ap[bass.ds(pair * (2 * P), 2 * P), :].rearrange("(a p) d -> p a d", p=P)

            def tiles_of_pair(pair):
                return xF[:, bass.ds(pair * (2 * D), 2 * D)].rearrange("p (a d) -> p a d", a=2)

            def f_load(s):
                pair, odd, turn = output_pair(s)
                if isinstance(pair, int) and pair == 0:
                    sp.wait_ge(c_dn, R1)
                    sp.wait_ge(sh_out, R0 // SHARES * 16)
                if not (isinstance(pair, int) and pair < 2):
                    alone(sp, "sp", f_x[odd], turn * 16)
                sp.dma_start(tiles_of_pair(pair), rows_of_pair(x3_d, pair)).then_inc(f_x[odd], 16)

            def f_store(s):
                pair, odd, _ = output_pair(s)
                alone(sp, "sp", f_o, pair * 2 + 2)
                sp.dma_start(rows_of_pair(out, pair), tiles_of_pair(pair)).then_inc(f_out[odd], 16)

            pipeline(sp, TILES, [(-2, c_rows_in, shared_last), (1, c_store), (0, f_load, summed_first),
                                 (0, c_sum_in, shared_last), (F_LAG, f_store, last)], begin=R1 - 2)
            for odd in range(2):
                sp.wait_ge(f_out[odd], 16 * PAIRS // 2)

        @block.gpsimd
        def _(pool):
            for m in (eyeF, onesF):
                pool.memset(m[:], 0.0 if m is eyeF else 1.0).then_inc(const_steps, 1)
            pool.memset(triH[:], 1.0).then_inc(const_steps, 1)
            pool.memset(onesH[:], 1.0).then_inc(consts, 1)
            pool.memset(powh[:], -0.5).then_inc(consts, 1)
            pool.iota(iotaI[:], pattern=[[1, P]], base=0, channel_multiplier=0).then_inc(consts, 1)
            pool.iota(tokidI[:], pattern=[[P, T]], base=0, channel_multiplier=1).then_inc(consts, 1)
            pool.wait_ge(const_steps, 3)
            pool.affine_select(out=eyeF[:], in_=eyeF[:], compare_op=ALU.not_equal, fill=1.0, base=0,
                               pattern=[[-1, P]], channel_multiplier=1).then_inc(consts, 1)
            pool.affine_select(out=triH[:], in_=triH[:], compare_op=ALU.is_gt, fill=0.0, base=0,
                               pattern=[[1, P]], channel_multiplier=-1).then_inc(consts, 1)
            pool.wait_ge(consts, CONSTS)

            def rsqrt_chain(done, n0, src, eps, tmp, dst, last):
                pool.tensor_scalar(tmp, src, eps, None, ALU.add).then_inc(done, 1)
                alone(pool, "pool", done, n0 + 1)
                pool.tensor_tensor(dst, tmp, powh[:], ALU.pow).then_inc(last, 1)

            def small_x(s):
                w, n0 = smA[s.u], s.t * 3
                alone(pool, "pool", x_mom, s.t + 1)
                before(pool, x_small, s.t, 2)
                before(pool, x_dq, s.t, 2)
                pool.sem_inc(passed["pool"], 1)
                pool.tensor_scalar(w[:, 0:1], mv[s.u][:, 1:2], 1.0 + EPS_RMS, EPS_RMS * EPS_LN, ALU.mult, ALU.add).then_inc(smA_s, 1)
                alone(pool, "pool", smA_s, n0 + 1)
                pool.tensor_tensor(w[:, 1:2], w[:, 0:1], powh[:], ALU.pow).then_inc(smA_s, 1)
                alone(pool, "pool", smA_s, n0 + 2)
                alone(pool, "pool", x_max, s.t + 1)
                pool.tensor_scalar(w[:, 2:3], xmax[s.u][:], w[:, 1:2], EPS_Q, ALU.mult, ALU.max).then_inc(smA_s, 1)

            def gains(s, half):
                at = slice(half * IA // HALVES, (half + 1) * IA // HALVES)
                alone(pool, "pool", sw_done, s.t * CA + (half + 1) * CA // HALVES)
                before(pool, d_q, s.t, 2)
                pool.sem_inc(passed["pool"], 1)
                if isinstance(s.t, int) and s.t == 0:
                    pool.wait_ge(gd_in, 16)
                pool.tensor_tensor(swg[s.u][:, at], sw[s.u][:, at], gd[:, at], ALU.mult).then_inc(swg_done, 1)

            def small_g(s):
                w, n0 = smG[s.u], s.t * 3
                alone(pool, "pool", sq_done, s.t + 1)
                alone(pool, "pool", g_max, s.t + 1)
                before(pool, g_small, s.t, 2)
                before(pool, g_dq, s.t, 2)
                pool.sem_inc(passed["pool"], 1)
                pool.tensor_scalar(w[:, 0:1], ssq[s.u][:], 1.0 / IA, EPS_RMS, ALU.mult, ALU.add).then_inc(smG_s, 1)
                alone(pool, "pool", smG_s, n0 + 1)
                pool.tensor_tensor(w[:, 1:2], w[:, 0:1], powh[:], ALU.pow).then_inc(smG_s, 1)
                alone(pool, "pool", smG_s, n0 + 2)
                pool.tensor_scalar(w[:, 2:3], gmax[s.u][:], w[:, 1:2], EPS_Q, ALU.mult, ALU.max).then_inc(smG_s, 1)

            def small_b(s):
                alone(pool, "pool", mo1, s.t + 1)
                rsqrt_chain(smB_s, s.t, mv1[:, 1:2], EPS_LN, var1[:], rstd1[:], rs1)

            def h_lo(s):
                alone(pool, "pool", hi_done, s.t + 1)
                before(pool, hb_out[s.u], s.h, 1, 16)
                pool.sem_inc(passed["pool"], 1)
                pool.tensor_tensor(rows[s.u][:, D:2 * D], hA, rows[s.u][:, 0:D], ALU.subtract).then_inc(lo_done, 1)

            pipeline(pool, T, [(-2, small_x), (1, small_g), (3, small_b), (0, lambda s: gains(s, 0)),
                               (0, lambda s: gains(s, 1)), (3, h_lo)])

            def gather(s, order, done, index, inv, dst, table, t0=0):
                pool.tensor_copy(index[s.u][:], inv[:, bass.ds(s.t - t0, 1)]).then_inc(order, 1)
                alone(pool, "pool", order, s.t + (1 - t0))
                pool.indirect_dma_start(out=dst[s.u][:] if dst is rows else dst[s.u], out_offset=None, in_=table[:, :],
                                        in_offset=bass.IndirectOffsetOnAxis(ap=index[s.u][:], axis=0)).then_inc(done[s.u], 16)

            for u in range(2):
                pool.wait_ge(hb_out[u], 16 * HALF)
            pool.wait_ge(routeB, 1)

            def b_gather(s):
                if not (isinstance(s.t, int) and s.t < 2):
                    alone(pool, "pool", b_T, s.t - 1)
                    alone(pool, "pool", b_rows[s.u], s.h * 16)
                gather(s, b_idx, b_rows, idx, invB, rows, hB_d)

            pipeline(pool, J_B, [(-1, b_gather)])

            for u in range(2):
                pool.wait_ge(b_out[u], 16 * ((J_B + 1 - u) // 2))
                pool.wait_ge(b_rows[u], 16 * ((J_B + 1 - u) // 2))

            def s_gather(s):
                if not (isinstance(s.t, int) and s.t < 2):
                    alone(pool, "pool", s_x2, s.t - 1)
                    alone(pool, "pool", s_y[s.u], s.h * 16)
                gather(s, s_idx, s_y, idx, posB[:, 0], yS, yB_d)

            def s_rstd(s):
                alone(pool, "pool", s_mo, s.t + 1)
                rsqrt_chain(s_small, s.t, mv1[:, 1:2], EPS_LN, var1[:], rstd1[:], s_rs)

            pipeline(pool, T, [(-4, s_gather), (-3, s_rstd)])

            for u in range(2):
                pool.wait_ge(s_hout[u], 16 * HALF)
                pool.wait_ge(s_y[u], 16 * HALF)
            pool.wait_ge(routeC, 1)

            def c_gather(s):
                alone(pool, "pool", c_T, results_before(s) - (0 if isinstance(s.t, int) and s.t == R0 else 1))
                if not (isinstance(s.t, int) and s.t < R0 + 2):
                    alone(pool, "pool", c_rows[s.u], (s.h - R0 // 2) * 16)
                gather(s, c_idx, c_rows, idx, invC, rows, hC_d, R0)

            pipeline(pool, TILES, [(-1, c_gather, (R0, R1))], kind=(R0, R1))

            for u in range(2):
                pool.wait_ge(c_out[u], 16 * ((J_C + 1 - u) // 2))

            for n in range(T):
                slot, turn = n % 4, n // 4
                if turn > 0:
                    alone(pool, "pool", f_y[slot], turn * 32)
                for c in range(2):
                    pool.indirect_dma_start(out=yF[c][:, n * D:(n + 1) * D], out_offset=None, in_=yC_d[:, :],
                                            in_offset=bass.IndirectOffsetOnAxis(ap=posC[:, c, n:n + 1], axis=0)
                                            ).then_inc(f_y[slot], 16)

        @block.scalar
        def _(act):
            act.wait_ge(consts, CONSTS)
            act.activation(dqx[0][:], powh[:], ACT.Silu).then_inc(silu_table, 1)
            for k in range(KD):
                act.wait_ge(wg_in[k], 16)
                act.activation(wgT[k], wg32[k], ACT.Abs, accum_out=asum[:, k:k + 1]).then_inc(abs_done, 1)
            act.wait_ge(gains_in, 32)
            act.activation(gw_hi[:], gw32[:], ACT.Copy, scale=SCALE_C).then_inc(gw_done, 1)

            def x_round(s):
                act.wait_ge(x_small, s.t + 1)
                act.wait_ge(x_cen, s.t + 1)
                before(act, x_q, s.t, 2)
                act.activation(xmag[s.u], xcen[s.u], ACT.Copy, bias=MAGIC, scale=cx[s.u][:]).then_inc(x_mag, 1)

            def x_evac(s):
                act.wait_ge(x_T, s.t + 1)
                before(act, gu_done, s.t, 2, CA)
                act.copy(xqT[s.u], bank(4, 256).bitcast(BF16)).then_inc(x_ev, 1)

            def silu(s, c):
                if c == 0:
                    act.wait_ge(x_dq, s.t + 1)
                act.wait_ge(gu_done, s.t * CA + (c + 1))
                if not (isinstance(s.t, int) and s.t == 0 and c < 2):
                    act.wait_ge(sw_done, s.t * CA + (c - 1))
                act.activation(sil[c % 2], bank(c % 2, CW), ACT.Silu, scale=dqx[s.u][:]).then_inc(sil_done, 1)

            def dequant_x(s):
                act.wait_ge(smA_s, (s.t + 1) * 3)
                before(act, sw_done, s.t, 2, CA)
                if isinstance(s.t, int) and s.t == 0:
                    act.wait_ge(silu_table, 1)
                act.activation(dqx[s.u][:], smA[s.u][:, 2:3], ACT.Copy, scale=wm127[:, 0:1]).then_inc(x_dq, 1)

            def dequant_g(s):
                act.wait_ge(smG_s, (s.t + 1) * 3)
                before(act, x1_done, s.t, 2)
                act.activation(dqg[s.u][:], smG[s.u][:, 2:3], ACT.Copy, scale=wm127[:, 1:2]).then_inc(g_dq, 1)

            def square(s):
                act.wait_ge(sw_done, (s.t + 1) * CA)
                before(act, g_small, s.t, 2)
                before(act, sq_done, s.t, 1)
                act.activation(squares, sw[s.u], ACT.Square, accum_out=ssq[s.u][:]).then_inc(sq_done, 1)

            def d_round(s):
                act.wait_ge(g_small, s.t + 1)
                act.wait_ge(g_max, s.t + 1)
                act.activation(swg[s.u], swg[s.u], ACT.Copy, bias=MAGIC, scale=cg[s.u][:]).then_inc(d_mag, 1)

            def d_evac(s):
                act.wait_ge(d_T, s.t + 1)
                before(act, z_done, s.t, 2)
                act.copy(qdT[s.u], wide(5, IA // 2).bitcast(BF16)).then_inc(d_ev, 1)

            def h_hi(s):
                act.wait_ge(h_done, s.t + 1)
                before(act, hb_out[s.u], s.h, 1, 16)
                act.copy(rows[s.u][:, 0:D], hA).then_inc(hi_done, 1)

            def ctx_split(s):
                act.wait_ge(ctx_in[s.u], (s.h + 1) * 16)
                at = bass.ds(s.t * CTX, CTX)
                act.activation(c_hi[:, at], wstage[s.u][:, 0:CTX], ACT.Copy, scale=SCALE_B).then_inc(ctx_hi, 1)

            stages = [(0, lambda s: silu(s, 0)), (2, d_evac), (0, lambda s: silu(s, 1)), (1, square), (-1, dequant_x),
                      (0, lambda s: silu(s, 2)), (-1, x_evac), (-2, x_round), (1, dequant_g),
                      (0, lambda s: silu(s, 3)), (1, d_round), (3, h_hi)]
            pipeline(act, T, stages, end=-1)
            act.wait_ge(means_done, 1)
            for k in range(KD):
                act.activation(wg32[k], wg32[k], ACT.Copy, bias=MAGIC, scale=winv[:, 0:1]).then_inc(round_done, 1)
            pipeline(act, T, stages, begin=-1, end=0)
            act.wait_ge(wd_in, 16)
            for half in range(2):
                at = slice(half * OG, (half + 1) * OG)
                act.activation(wdT[:, at], wd32[:, at], ACT.Abs, accum_out=asum[:, KD + half:KD + half + 1]).then_inc(abs_done, 1)
            pipeline(act, T, stages, begin=0, end=1)
            act.wait_ge(means_done, 2)
            for half in range(2):
                at = slice(half * OG, (half + 1) * OG)
                act.activation(wd32[:, at], wd32[:, at], ACT.Copy, bias=MAGIC, scale=winv[:, 1:2]).then_inc(round_done, 1)
            pipeline(act, T, stages, begin=1, end=CTX_FROM)
            pipeline(act, T, stages[:8] + [ctx_chunks(ctx_split)] + stages[8:], begin=CTX_FROM)

            def split_hi(s, first=0):
                act.wait_ge(w_in[s.u], (s.h + (first // 2 + 1)) * 16)
                act.activation(w_hi[:, bass.ds((s.t + first) * CHUNK, CHUNK)], wstage[s.u][:], ACT.Copy,
                               scale=SCALE_C).then_inc(whi_done, 1)

            def b_evac(s):
                act.wait_ge(b_T, s.t + 1)
                before(act, b_t, s.t, 2)
                act.copy(hT[s.u][:].rearrange("p a n -> p (a n)"), bank(0).bitcast(F16)).then_inc(b_ev, 1)

            def b_silu(s):
                act.wait_ge(b_t, s.t + 1)
                before(act, b_aT, s.t, 2)
                act.activation(bs[s.u], bank(1 + s.u), ACT.Silu, scale=1.0 / SCALE_B).then_inc(b_sil, 1)

            def b_split(s):
                act.wait_ge(b_aT, s.t + 1)
                before(act, b_y, s.t, 2)
                act.copy(bpT[s.u][:, 0, :], bank(3)).then_inc(b_hi, 1)

            act.wait_ge(z_done, T)
            act.wait_ge(x1_out[0], 16 * HALF)
            act.wait_ge(x1_out[1], 16 * HALF)
            pipeline(act, J_B, [(0, b_silu), (-1, b_evac), (0, b_split), (0, split_hi, (0, W_B))])

            def s_split(s):
                act.wait_ge(s_h, s.t + 1)
                before(act, s_hout[s.u], s.h, 1, 16)
                before(act, s_T, s.t, 2)
                if isinstance(s.t, int) and s.t == 2:
                    act.wait_ge(c_T, 1)
                act.copy(rowsS[s.u][:, 0:D], hS).then_inc(s_hi, 1)

            def s_evac(s):
                act.wait_ge(s_T, s.t + 1)
                before(act, s_lg, s.t, 1)
                act.copy(hTS.rearrange("p a n -> p (a n)"), bank(0).bitcast(F16)).then_inc(s_ev, 1)

            def s_w(s):
                if isinstance(s.t, int) and s.t == W_FREE:
                    slot_9_free(act)
                split_hi(s, W_B)

            def c_evac(s):
                if rows_slot(s) != s.u:
                    return
                act.wait_ge(c_T, results_before(s) + 1)
                if not (isinstance(s.t, int) and s.t == 0):
                    two_ago = routed(s) and not (isinstance(s.t, int) and s.t == R0)
                    act.wait_ge(c_gu, s.t - 1 if two_ago else s.t)
                act.copy(hT[s.u][:].rearrange("p a n -> p (a n)"), bank(0).bitcast(F16)).then_inc(c_ev, 1)

            def c_silu(s):
                act.wait_ge(c_gu, s.t + 1)
                before(act, c_pT, s.t, 1)
                act.activation(cs[:, 0:IC], bank(1 + s.u, IC), ACT.Silu, scale=1.0 / SCALE_C).then_inc(c_sil, 1)

            def c_split(s):
                act.wait_ge(c_pT, s.t + 1)
                before(act, c_dn, s.t, 1)
                act.copy(cpT[:, 0, :], bank(5, ICP)).then_inc(c_hi_s, 1)

            act.wait_ge(b_y, J_B)
            w_rest = (0, W_REST)
            pipeline(act, TILES, [(0, c_silu), (-1, c_evac), (-2, s_evac, whole), (-3, s_split, whole), (0, c_split),
                                  (W_LAG, s_w, w_rest)], end=S_ROUNDS)
            beside_stages = [(0, c_silu), (-1, c_evac), (0, c_split), (W_LAG, s_w, w_rest)]
            pipeline(act, TILES, beside_stages, begin=S_ROUNDS, end=S_ROUNDS + 2)
            act.wait_ge(exp_done, 1)
            act.activation(rt[:], rt[:], ACT.Exp).then_inc(exp_done, 1)
            pipeline(act, TILES, beside_stages, begin=S_ROUNDS + 2, end=R0, kind=(0, R0))
            pipeline(act, TILES, [(0, c_silu), (-1, c_evac), (0, c_split)], begin=R0, kind=(R0, R1))

        @block.vector
        def _(dve):
            r = [0]

            def step(ins):
                r[0] += 1
                ins.then_inc(route, 1)
                dve.wait_ge(route, r[0])

            def routing(experts, tiles_, choices, inv, experts_of, pos, done, rank_sums, inv_sums, n_mm, n_inv, beside):
                E, C = experts, choices
                dve.sem_inc(route_mm, 1)
                beside()
                dve.wait_ge(route_mm, n_mm + 2)
                step(dve.tensor_copy(rank[:, :, 0:E], rank_sums.rearrange("p (t e) -> p t e", e=E)))
                step(dve.tensor_scalar(eI[:, 0:E], rank[:, T, 0:E], float(P - 1), None, ALU.add))
                step(dve.tensor_scalar(eI[:, 0:E], eI[:, 0:E], 7, None, ALU.logical_shift_right))
                step(dve.tensor_copy(eF[:, 0, 0:E], eI[:, 0:E]))
                square = cmpJ[:, 0:E * E].rearrange("p (a e) -> p a e", e=E)
                step(dve.tensor_tensor(square, upto[:, 0:E, 0:E], eF[:, 0:1, 0:E].broadcast_to([P, E, E]), ALU.mult))
                step(dve.tensor_reduce(eF[:, 1, 0:E], square, AX.X, ALU.add))
                step(dve.tensor_tensor(eF[:, 2, 0:E], eF[:, 1, 0:E], eF[:, 0, 0:E], ALU.subtract))
                ended = cmpJ[:, 0:tiles_ * E].rearrange("p (j e) -> p j e", e=E)
                each_j = iotaF[:, 0:tiles_].rearrange("p (j a) -> p j a", a=1).broadcast_to([P, tiles_, E])
                step(dve.tensor_tensor(ended, each_j, eF[:, 1:2, 0:E].broadcast_to([P, tiles_, E]), ALU.is_ge))
                step(dve.tensor_reduce(jF[:, 0:tiles_], ended, AX.X, ALU.add))
                step(dve.tensor_scalar(experts_of[:], jF[:, 0:tiles_], float(E - 1), None, ALU.min))
                beside()
                rank_t, first_t, tile_t, slot_t = (rF[:, i, 0:C, :] for i in range(4))
                for c in range(C):
                    step(dve.tensor_tensor(rt2[:, c, :, 0:E], oh12[:, c, :, 0:E], rank[:, 0:T, 0:E], ALU.mult))
                step(dve.tensor_reduce(rank_t, rt2[:, 0:C, :, 0:E], AX.X, ALU.add))
                for c in range(C):
                    step(dve.tensor_tensor(rt2[:, c, :, 0:E], oh12[:, c, :, 0:E], eF[:, 2:3, 0:E].broadcast_to([P, T, E]),
                                           ALU.mult))
                step(dve.tensor_reduce(first_t, rt2[:, 0:C, :, 0:E], AX.X, ALU.add))
                step(dve.tensor_copy(rI[:, 0, 0:C, :], rank_t))
                step(dve.tensor_scalar(rI[:, 1, 0:C, :], rI[:, 0, 0:C, :], 7, None, ALU.logical_shift_right))
                step(dve.tensor_copy(tile_t, rI[:, 1, 0:C, :]))

                def flat(ap):
                    return ap.rearrange("p c t -> p (c t)")

                step(dve.scalar_tensor_tensor(out=flat(slot_t), in0=flat(tile_t), scalar=-float(P), in1=flat(rank_t),
                                              op0=ALU.mult, op1=ALU.add))
                step(dve.tensor_tensor(tile_t, tile_t, first_t, ALU.add))
                step(dve.scalar_tensor_tensor(out=flat(posF[:, 0:C, :]), in0=flat(tile_t), scalar=float(P), in1=flat(slot_t),
                                              op0=ALU.mult, op1=ALU.add))
                step(dve.tensor_copy(pos[:], posF[:, 0:C, :]))
                sel_j = selJ[:, 0:SELS * tiles_].rearrange("p (n j) -> p n j", j=tiles_)

                def each(ap, n):
                    return ap.rearrange("p (n a) -> p n a", a=1).broadcast_to([P, SELS, n])

                for g in range(C * T // SELS):
                    c, at = g * SELS // T, slice(g * SELS % T, g * SELS % T + SELS)
                    if g > 0:
                        dve.wait_ge(inv_mm, n_inv + g * SELS)
                    slots = iotaF[:].rearrange("p (a s) -> p a s", a=1).broadcast_to([P, SELS, P])
                    dve.tensor_tensor(selR[:], slots, each(rF[:, 3, c, at], P), ALU.is_equal).then_inc(sel_done, 1)
                    all_j = iotaF[:, 0:tiles_].rearrange("p (a j) -> p a j", a=1).broadcast_to([P, SELS, tiles_])
                    step(dve.tensor_tensor(sel_j, all_j, each(rF[:, 2, c, at], tiles_), ALU.is_equal))
                    dve.tensor_tensor(sel_j, sel_j, each(tokid[:, at], tiles_), ALU.mult).then_inc(sel_done, 1)
                    beside()
                dve.wait_ge(inv_mm, n_inv + C * T)
                step(dve.tensor_copy(inv[:], inv_sums))
                dve.sem_inc(done, 1)

            dve.wait_ge(consts, CONSTS)
            dve.tensor_copy(eyeH[:], eyeF[:]).then_inc(const_steps, 1)
            dve.tensor_copy(eyeB[:], eyeF[:]).then_inc(const_steps, 1)
            step(dve.tensor_copy(iotaF[:], iotaI[:]))
            step(dve.tensor_copy(tokid[:], tokidI[:]))
            step(dve.memset(zeroH[:], 0.0))
            step(dve.tensor_tensor(upto[:], iotaF[:, 0:E_C].rearrange("p (e a) -> p e a", a=1).broadcast_to([P, E_C, E_C]),
                                   iotaF[:, 0:E_C].rearrange("p (a e) -> p a e", a=1).broadcast_to([P, E_C, E_C]), ALU.is_ge))

            dve.wait_ge(tok_in, 16)
            step(dve.tensor_copy(tokF[:], tokI[:]))
            step(dve.memset(oh12[:, 0, :, 0:1], 1.0))
            for e in range(1, E_B):
                step(dve.tensor_scalar(oh12[:, 0, :, e], tokF[:], float(e * PER_EXPERT), None, ALU.is_ge))
            for e in range(E_B - 1):
                step(dve.tensor_tensor(oh12[:, 0, :, e], oh12[:, 0, :, e], oh12[:, 0, :, e + 1], ALU.subtract))
            step(dve.tensor_copy(oh[:, :, 0:E_B], oh12[:, 0, :, 0:E_B]))
            routing(E_B, J_B, 1, invB, expB, posB, routeB, bank(6, (T + 1) * E_B), bank(7, J_B), 0, 0, lambda: None)

            def x_spread(s):
                dve.wait_ge(x_in[s.u], (s.h + 1) * 16)
                before(dve, x_small, s.t, 2)
                dve.bn_stats(stats[s.u][:], xin[s.u]).then_inc(x_stats, 1)

            def x_moments(s):
                alone(dve, "dve", x_stats, s.t + 1)
                dve.bn_aggr(mv[s.u][:], stats[s.u][:]).then_inc(x_mom, 1)

            def x_center(s):
                before(dve, x_mag, s.t, 2)
                dve.wait_ge(x_mom, s.t + 1)
                if isinstance(s.t, int) and s.t == 0:
                    dve.wait_ge(gains_in, 32)
                dve.scalar_tensor_tensor(out=xcen[s.u], in0=xin[s.u], scalar=mv[s.u][:, 0:1], in1=gg,
                                         op0=ALU.subtract, op1=ALU.mult).then_inc(x_cen, 1)

            def x_absmax(s):
                dve.wait_ge(x_cen, s.t + 1)
                dve.tensor_reduce(xmax[s.u][:], xcen[s.u], AX.X, ALU.max, apply_absolute_value=True).then_inc(x_max, 1)

            def x_reciprocal(s):
                dve.wait_ge(smA_s, (s.t + 1) * 3)
                before(dve, x_mag, s.t, 2)
                dve.reciprocal(cx[s.u][:], smA[s.u][:, 2:3]).then_inc(x_rec, 1)

            def x_factor(s):
                dve.wait_ge(x_rec, s.t + 1)
                dve.tensor_scalar(cx[s.u][:], cx[s.u][:], smA[s.u][:, 1:2], 127.0, ALU.mult, ALU.mult).then_inc(x_small, 1)

            def g_reciprocal(s):
                dve.wait_ge(smG_s, (s.t + 1) * 3)
                before(dve, d_mag, s.t, 2)
                dve.reciprocal(cg[s.u][:], smG[s.u][:, 2:3]).then_inc(g_rec, 1)

            def g_factor(s):
                dve.wait_ge(g_rec, s.t + 1)
                dve.tensor_scalar(cg[s.u][:], cg[s.u][:], smG[s.u][:, 1:2], 127.0, ALU.mult, ALU.mult).then_inc(g_small, 1)

            def x_int(s):
                dve.wait_ge(x_mag, s.t + 1)
                before(dve, x_T, s.t, 2)
                dve.tensor_scalar(xq[s.u], xmag[s.u], MAGIC, 127.0, ALU.subtract, ALU.min).then_inc(x_q, 1)

            def swiglu(s, c):
                dve.wait_ge(sil_done, s.t * CA + (c + 1))
                if c == 0:
                    before(dve, sq_done, s.t, 2)
                    before(dve, swg_done, s.t, 2, HALVES)
                    dve.wait_ge(x_dq, s.t + 1)
                dve.scalar_tensor_tensor(out=sw[s.u][:, c * CW:(c + 1) * CW], in0=bank(2 + c % 2, CW), scalar=dqx[s.u][:],
                                         in1=sil[c % 2], op0=ALU.mult, op1=ALU.mult).then_inc(sw_done, 1)

            def g_absmax(s):
                dve.wait_ge(swg_done, (s.t + 1) * HALVES)
                before(dve, g_small, s.t, 2)
                dve.tensor_reduce(gmax[s.u][:], swg[s.u], AX.X, ALU.max, apply_absolute_value=True).then_inc(g_max, 1)

            def d_int(s):
                dve.wait_ge(d_mag, s.t + 1)
                before(dve, d_T, s.t, 2)
                dve.tensor_scalar(qd[s.u], swg[s.u], MAGIC, 127.0, ALU.subtract, ALU.min).then_inc(d_q, 1)

            def residual1(s):
                dve.wait_ge(z_done, s.t + 1)
                dve.wait_ge(g_dq, s.t + 1)
                dve.wait_ge(xr_in[s.u], (s.h + 1) * 16)
                before(dve, x1_out[s.u], s.h, 1, 16)
                before(dve, h_done, s.t, 2)
                dve.scalar_tensor_tensor(out=x1[s.u], in0=bank(7), scalar=dqg[s.u][:], in1=xres[s.u],
                                         op0=ALU.mult, op1=ALU.add).then_inc(x1_done, 1)

            def spread1(s):
                dve.wait_ge(x1_done, s.t + 1)
                before(dve, rs1, s.t, 1)
                dve.bn_stats(stats1[:], x1[s.u]).then_inc(st1, 1)

            def moments1(s):
                alone(dve, "dve", st1, s.t + 1)
                before(dve, h_done, s.t, 1)
                dve.sem_inc(passed["dve"], 1)
                dve.bn_aggr(mv1[:], stats1[:]).then_inc(mo1, 1)

            def norm1(s):
                dve.wait_ge(rs1, s.t + 1)
                before(dve, hi_done, s.t, 1)
                before(dve, lo_done, s.t, 1)
                dve.tensor_scalar(hA, x1[s.u], mv1[:, 0:1], rstd1[:], ALU.subtract, ALU.mult).then_inc(h_done, 1)

            def ctx_rest(s):
                dve.wait_ge(ctx_hi, s.t + 1)
                at = bass.ds(s.t * CTX, CTX)
                dve.scalar_tensor_tensor(out=c_lo[:, at], in0=wstage[s.u][:, 0:CTX], scalar=SCALE_B, in1=c_hi[:, at],
                                         op0=ALU.mult, op1=ALU.subtract).then_inc(ctx_lo, 1)

            stages = [(3, residual1), (0, lambda s: swiglu(s, 0)), (1, g_absmax), (-3, x_spread),
                      (0, lambda s: swiglu(s, 1)), (-1, x_int), (3, spread1), (-3, x_moments), (-2, x_reciprocal),
                      (3, moments1), (-2, x_factor), (0, lambda s: swiglu(s, 2)), (1, g_reciprocal), (3, norm1),
                      (1, g_factor), (-3, x_center), (0, lambda s: swiglu(s, 3)), (-3, x_absmax), (1, d_int)]
            pipeline(dve, T, stages, end=-1)

            dve.wait_ge(gw_done, 1)
            dve.scalar_tensor_tensor(out=gw_lo[:], in0=gw32[:], scalar=SCALE_C, in1=gw_hi[:],
                                     op0=ALU.mult, op1=ALU.subtract).then_inc(gw_done, 1)
            def mean(i, pieces, b_at, size):
                dve.wait_ge(tot_done, i + 1)
                step(dve.tensor_reduce(wmean[:, i:i + 1], bank(7, pieces, b_at), AX.X, ALU.add))
                step(dve.tensor_scalar(wmean[:, i:i + 1], wmean[:, i:i + 1], 1.0 / size, EPS_Q, ALU.mult, ALU.max))
                step(dve.tensor_scalar(wm127[:, i:i + 1], wmean[:, i:i + 1], 1.0 / 127.0, None, ALU.mult))
                dve.reciprocal(winv[:, i:i + 1], wmean[:, i:i + 1]).then_inc(means_done, 1)

            def ternary(dst, rounded, n):
                dve.wait_ge(round_done, n + 1)
                dve.tensor_scalar(dst, rounded, MAGIC, 1.0, ALU.subtract, ALU.min).then_inc(clip_done, 1)
                dve.wait_ge(clip_done, n + 1)
                dve.tensor_scalar(dst, dst, -1.0, None, ALU.max).then_inc(tern_done, 1)

            mean(0, KD, 128, OG * D)
            pipeline(dve, T, stages, begin=-1, end=0)
            for k in range(KD):
                ternary(wgT[k], wg32[k], k)
            pipeline(dve, T, stages, begin=0, end=1)
            mean(1, 2, 0, IA * D)
            for half in range(2):
                at = slice(half * OG, (half + 1) * OG)
                ternary(wdT[:, at], wd32[:, at], KD + half)
            pipeline(dve, T, stages, begin=1, end=CTX_FROM)
            pipeline(dve, T, stages[:-1] + [ctx_chunks(ctx_rest)] + stages[-1:], begin=CTX_FROM)

            def split_lo(s, first=0):
                at = bass.ds((s.t + first) * CHUNK, CHUNK)
                dve.wait_ge(whi_done, s.t + (first + 1))
                dve.scalar_tensor_tensor(out=w_lo[:, at], in0=wstage[s.u][:], scalar=SCALE_C, in1=w_hi[:, at],
                                         op0=ALU.mult, op1=ALU.subtract).then_inc(wlo_done, 1)

            def b_prod(s):
                dve.wait_ge(b_sil, s.t + 1)
                dve.tensor_tensor(bs[s.u], bank(1 + s.u), bs[s.u], ALU.mult).then_inc(b_a, 1)

            def b_rest(s):
                dve.wait_ge(b_hi, s.t + 1)
                dve.tensor_tensor(bpT[s.u][:, 1, :], bank(3), bpT[s.u][:, 0, :], ALU.subtract).then_inc(b_lo, 1)

            def b_rows_out(s):
                dve.wait_ge(b_y, s.t + 1)
                before(dve, b_out[s.u], s.h, 1, 16)
                dve.tensor_copy(yrow[s.u][:], bank(4 + s.u)).then_inc(b_yev, 1)

            pipeline(dve, J_B, [(0, b_prod), (0, b_rest), (1, b_rows_out), (0, split_lo, (0, W_B))])

            def residual2(s):
                dve.wait_ge(s_x[s.u], (s.h + 1) * 16)
                dve.wait_ge(s_y[s.u], (s.h + 1) * 16)
                dve.scalar_tensor_tensor(out=xS[s.u], in0=yS[s.u], scalar=1.0 / SCALE_B ** 2, in1=xS[s.u],
                                         op0=ALU.mult, op1=ALU.add).then_inc(s_x2, 1)

            def spread2(s):
                dve.wait_ge(s_x2, s.t + 1)
                before(dve, s_rs, s.t, 1)
                dve.bn_stats(stats1[:], xS[s.u]).then_inc(s_st, 1)

            def moments2(s):
                alone(dve, "dve", s_st, s.t + 1)
                before(dve, s_h, s.t, 1)
                dve.sem_inc(passed["dve"], 1)
                dve.bn_aggr(mv1[:], stats1[:]).then_inc(s_mo, 1)

            def norm2(s):
                dve.wait_ge(s_rs, s.t + 1)
                before(dve, s_hi, s.t, 1)
                before(dve, s_lo, s.t, 1)
                dve.tensor_scalar(hS, xS[s.u], mv1[:, 0:1], rstd1[:], ALU.subtract, ALU.mult).then_inc(s_h, 1)

            def s_rest(s):
                dve.wait_ge(s_hi, s.t + 1)
                dve.tensor_tensor(rowsS[s.u][:, D:2 * D], hS, rowsS[s.u][:, 0:D], ALU.subtract).then_inc(s_lo, 1)

            def s_w(s):
                if isinstance(s.t, int) and s.t == W_FREE:
                    slot_9_free(dve)
                split_lo(s, W_B)

            def keep_logits(s):
                dve.wait_ge(s_lg, s.t + 1)
                dve.tensor_scalar(logits[:, bass.ds(s.t, 1), :].rearrange("p a e -> p (a e)"), bank(7, E_C),
                                  1.0 / SCALE_C, None, ALU.mult).then_inc(s_lgev, 1)

            def c_prod(s):
                dve.wait_ge(c_sil, s.t + 1)
                dve.tensor_tensor(cs[:, 0:IC], bank(3 + s.u, IC), cs[:, 0:IC], ALU.mult).then_inc(c_p, 1)

            def c_rest(s):
                dve.wait_ge(c_hi_s, s.t + 1)
                dve.tensor_tensor(cpT[:, 1, :], bank(5, ICP), cpT[:, 0, :], ALU.subtract).then_inc(c_lo_s, 1)

            def c_rows_out(s):
                if not routed(s):
                    tile, half = shared_part(s)
                    if half == SHARES - 1:
                        total = yrow[0][:] if s.first < R0 else out_tiles(xF, tile)
                        dve.wait_ge(c_dn, s.t + 1)
                        dve.wait_ge(sh_x, (tile + 1) * 16)
                        dve.scalar_tensor_tensor(out=total, in0=bank(6), scalar=1.0 / SCALE_C ** 2, in1=total,
                                                 op0=ALU.mult, op1=ALU.add).then_inc(c_yev, 1)
                    return
                dve.wait_ge(c_dn, s.t + 1)
                if isinstance(s.t, int) and s.t == R0:
                    dve.wait_ge(sh_out, R0 // SHARES * 16)
                    dve.wait_ge(b_out[1], 16 * (J_B // 2))
                if not (isinstance(s.t, int) and s.t < R0 + 2):
                    dve.wait_ge(c_out[s.u], (s.h - R0 // 2) * 16)
                dve.tensor_copy(yrow[s.u][:], bank(6)).then_inc(c_yev, 1)

            dve.wait_ge(b_y, J_B)
            dve.memset(cs[:, IC:ICP], 0.0).then_inc(pad_done, 1)
            w_rest = (0, W_REST)
            beside_stages = [(0, c_prod), (0, c_rest), (1, c_rows_out), (W_LAG, s_w, w_rest)]
            pipeline(dve, TILES, [(-3, residual2, whole), (0, c_prod), (-3, spread2, whole), (-3, moments2, whole),
                                  (-1, keep_logits, whole), (-3, norm2, whole), (-3, s_rest, whole), (0, c_rest),
                                  (1, c_rows_out), (W_LAG, s_w, w_rest)], end=S_ROUNDS)
            rounds_beside = iter(range(S_ROUNDS, TILES))

            def beside():
                r = next(rounds_beside)
                pipeline(dve, TILES, beside_stages, begin=r, end=r + 1)

            dve.wait_ge(s_lgev, T)
            step(dve.tensor_copy(rt2[:, 0], logits[:]))
            iota_e = iotaF[:, 0:E_C].rearrange("p (a e) -> p a e", a=1).broadcast_to([P, T, E_C])

            def over_e(ap):
                return ap.rearrange("p (t a) -> p t a", a=1).broadcast_to([P, T, E_C])

            for c in range(2):
                step(dve.tensor_reduce(m12[:, c, :], rt2[:, 0], AX.X, ALU.max))
                step(dve.tensor_tensor(oh12[:, c], rt2[:, 0], over_e(m12[:, c, :]), ALU.not_equal))
                step(dve.tensor_scalar(oh12[:, c], oh12[:, c], 64.0, None, ALU.mult))
                step(dve.tensor_tensor(oh12[:, c], oh12[:, c], iota_e, ALU.add))
                step(dve.tensor_reduce(wsum[:], oh12[:, c], AX.X, ALU.min))
                step(dve.tensor_tensor(oh12[:, c], iota_e, over_e(wsum[:]), ALU.is_equal))
                if c == 0:
                    beside()
                    step(dve.tensor_scalar(rt[:], oh12[:, c], -3.0e38, None, ALU.mult))
                    step(dve.tensor_tensor(rt2[:, 0], rt2[:, 0], rt[:], ALU.add))
            step(dve.tensor_tensor(rt[:], logits[:], over_e(m12[:, 0, :]), ALU.subtract))
            dve.sem_inc(exp_done, 1)
            step(dve.tensor_tensor(oh[:], oh12[:, 0], oh12[:, 1], ALU.add))
            beside()
            routing(E_C, J_C, 2, invC, expC, posC, routeC, bank(7, (T + 1) * E_C), bank(7, J_C, 256), 2, T, beside)
            dve.wait_ge(exp_done, 2)
            step(dve.tensor_reduce(wsum[:], rt[:], AX.X, ALU.add))
            step(dve.reciprocal(wsum[:], wsum[:]))
            step(dve.tensor_scalar(wsum[:], wsum[:], 1.0 / SCALE_C ** 2, None, ALU.mult))
            for c in range(2):
                step(dve.tensor_tensor(rt2[:, 0], oh12[:, c], rt[:], ALU.mult))
                step(dve.tensor_reduce(posF[:, 0], rt2[:, 0], AX.X, ALU.add))
                step(dve.tensor_tensor(wtop[c][:], posF[:, 0], wsum[:], ALU.mult))
            pipeline(dve, TILES, beside_stages, begin=next(rounds_beside), end=R0, kind=(0, R0))
            pipeline(dve, TILES, [(0, c_prod), (0, c_rest), (1, c_rows_out)], begin=R0, end=R1 + 2, kind=(R0, R1))

            def f_sum(s, i):
                pair, odd, turn = output_pair(s)
                n = pair * 2 + i
                if s.first < summed_last[0]:
                    dve.wait_ge(f_x[odd], (turn + 1) * 16)
                else:
                    dve.wait_ge(c_yev, n + (J_C + 1))
                dve.wait_ge(f_y[odd * 2 + i], (turn + 1) * 32)
                for k, done in enumerate((f_a, f_o)):
                    if k > 0:
                        dve.wait_ge(f_a, n + 1)
                    dve.scalar_tensor_tensor(out=out_tiles(xF, n), in0=out_tiles(yF[k], n), scalar=wtop[k][:, bass.ds(n, 1)],
                                             in1=out_tiles(xF, n), op0=ALU.mult, op1=ALU.add).then_inc(done, 1)

            pipeline(dve, TILES, [(0, c_prod), (F_LAG, lambda s: f_sum(s, 0), last), (0, c_rest), (1, c_rows_out),
                                  (F_LAG, lambda s: f_sum(s, 1), last)], begin=R1 + 2)

        @block.tensor
        def _(pe):
            def route_sums(experts, n_mm, b):
                E = experts
                pe.wait_ge(route_mm, n_mm + 1)
                pe.matmul(bank(b, (T + 1) * E), onesH[:], zeroH[:, :, 0:E].broadcast_to([P, T + 1, E]), start=True, stop=False)
                for t in range(T):
                    pe.matmul(bank(b, (T - t) * E, (t + 1) * E), onesH[:], oh[:, t:t + 1, 0:E].broadcast_to([P, T - t, E]),
                              start=False, stop=False)
                pe.matmul(bank(b, T * E), triH[:], oh[:, :, 0:E], start=False, stop=True).then_inc(route_mm, 1)

            def route_inverse(to, tiles_, numbers, count, n_sel):
                for n in numbers:
                    pe.wait_ge(sel_done, n_sel + 2 * (n // SELS + 1))
                    pe.matmul(to, selR[:, n % SELS], selJ[:, n % SELS * tiles_:(n % SELS + 1) * tiles_],
                              start=(n == 0), stop=(n == count - 1)).then_inc(inv_mm, 1)

            pe.wait_ge(consts, CONSTS)
            pe.wait_ge(const_steps, 5)
            route_sums(E_B, 0, 6)
            route_inverse(bank(7, J_B), J_B, range(T), T, 0)
            pe.wait_ge(abs_done, KD)
            pe.wait_ge(routeB, 1)
            pe.matmul(bank(7, KD, 128), onesF[:], asum[:, 0:KD], start=True, stop=True).then_inc(tot_done, 1)

            def x_turn(s):
                pe.wait_ge(x_q, s.t + 1)
                before(pe, x_ev, s.t, 1)
                for k in range(KD):
                    mm = pe.transpose(bank(4, 256).bitcast(BF16)[:, k * P:(k + 1) * P], xq[s.u][:, k * P:(k + 1) * P], eyeB[:])
                mm.then_inc(x_T, 1)

            def gate_up(s, c):
                if c == 0:
                    if isinstance(s.t, int) and s.t == 0:
                        pe.wait_ge(tern_done, KD)
                    pe.wait_ge(x_ev, s.t + 1)
                if not (isinstance(s.t, int) and s.t == 0 and c < 2):
                    pe.wait_ge(sw_done, s.t * CA + (c - 1))
                for half in range(2):
                    at = half * IA + c * CW
                    for k in range(KD):
                        mm = pe.matmul(bank(2 * half + c % 2, CW), xqT[s.u][:, k * P:(k + 1) * P], wgT[k][:, at:at + CW],
                                       start=(k == 0), stop=(k == KD - 1))
                mm.then_inc(gu_done, 1)

            def d_turn(s):
                pe.wait_ge(d_q, s.t + 1)
                before(pe, d_ev, s.t, 1)
                for k in range(KI):
                    mm = pe.transpose(wide(5, IA // 2).bitcast(BF16)[:, k * P:(k + 1) * P], qd[s.u][:, k * P:(k + 1) * P], eyeB[:])
                mm.then_inc(d_T, 1)

            def down(s):
                if isinstance(s.t, int) and s.t == 0:
                    pe.wait_ge(tern_done, KD + 2)
                pe.wait_ge(d_ev, s.t + 1)
                before(pe, x1_done, s.t, 1)
                for k in range(KI):
                    mm = pe.matmul(bank(7), qdT[s.u][:, k * P:(k + 1) * P], wdT[:, k * D:(k + 1) * D],
                                   start=(k == 0), stop=(k == KI - 1))
                mm.then_inc(z_done, 1)

            stages = [(0, lambda s: gate_up(s, 0)), (0, lambda s: gate_up(s, 1)), (2, d_turn),
                      (0, lambda s: gate_up(s, 2)), (2, down), (-1, x_turn), (0, lambda s: gate_up(s, 3))]
            pipeline(pe, T, stages, end=1)
            pe.wait_ge(abs_done, KD + 2)
            pe.matmul(bank(7, 2), onesF[:], asum[:, KD:KD + 2], start=True, stop=True).then_inc(tot_done, 1)
            pipeline(pe, T, stages, begin=1)

            def turn_rows(source, done):
                for k in range(2 * KD):
                    mm = pe.transpose(bank(0).bitcast(F16)[:, k * P:(k + 1) * P], source[:, k * P:(k + 1) * P], eyeH[:])
                mm.then_inc(done, 1)

            def split_product(to, a, w, steps, begins=True, ends=True):
                for k in range(steps):
                    for n, (pa, pw) in enumerate(((0, 0), (0, 1), (1, 0))):
                        mm = pe.matmul(to, a(k, pa), w(k, pw), start=(begins and k == 0 and n == 0),
                                       stop=(ends and k == steps - 1 and n == 2))
                return mm

            def b_turn(s):
                pe.wait_ge(b_rows[s.u], (s.h + 1) * 16)
                before(pe, b_ev, s.t, 1)
                turn_rows(rows[s.u], b_T)

            def b_first(s):
                pe.wait_ge(b_ev, s.t + 1)
                before(pe, b_a, s.t, 2)
                pe.sem_inc(passed["pe"], 1)
                e = pe.value_load(expB[0:1, bass.ds(s.t, 1)], min_val=0, max_val=E_B - 1)
                split_product(bank(1 + s.u), lambda k, p: hT[s.u][:, p * KD + k, :],
                              lambda k, p: (c_hi, c_lo)[p][:, bass.ds(e * (KD * D) + k * D, D)], KD).then_inc(b_t, 1)

            def b_turn_a(s):
                pe.wait_ge(b_a, s.t + 1)
                before(pe, b_lo, s.t, 1)
                for k in range(KD):
                    mm = pe.transpose(bank(3, P, k * P), bs[s.u][:, k * P:(k + 1) * P], eyeF[:])
                mm.then_inc(b_aT, 1)

            def b_second(s):
                pe.wait_ge(b_lo, s.t + 1)
                before(pe, b_yev, s.t, 2)
                pe.sem_inc(passed["pe"], 1)
                e = pe.value_load(expB[0:1, bass.ds(s.t, 1)], min_val=0, max_val=E_B - 1)
                split_product(bank(4 + s.u), lambda k, p: bpT[s.u][:, p, k * P:(k + 1) * P],
                              lambda k, p: (c_hi, c_lo)[p][:, bass.ds(e * (KD * D) + k * D, D)], KD).then_inc(b_y, 1)

            pe.wait_ge(ctx_lo, CTX_CHUNKS)
            pe.wait_ge(x1_done, T)
            pipeline(pe, J_B, [(0, b_first), (-1, b_turn), (1, b_second), (0, b_turn_a)])

            def s_turn(s):
                pe.wait_ge(s_hi, s.t + 1)
                pe.wait_ge(s_lo, s.t + 1)
                if not (isinstance(s.t, int) and s.t == 0):
                    pe.wait_ge(c_ev, s.h + s.u)
                turn_rows(rowsS[s.u], s_T)

            def s_router(s):
                pe.wait_ge(s_ev, s.t + 1)
                before(pe, s_lgev, s.t, 1)
                split_product(bank(7, E_C), lambda k, p: hTS[:, p * KD + k, :],
                              lambda k, p: (gw_hi, gw_lo)[p][:, k * E_C:(k + 1) * E_C], KD).then_inc(s_lg, 1)

            def c_turn(s):
                if rows_slot(s) != s.u:
                    return
                pe.wait_ge(s_ev, s.t + 1 if s.first < S_ROUNDS else T)
                if not (isinstance(s.t, int) and s.t == 0):
                    pe.wait_ge(c_ev, results_before(s))
                if routed(s):
                    pe.wait_ge(c_rows[s.u], (s.h - (R0 // 2 - 1)) * 16)
                elif s.first >= R1:
                    pe.wait_ge(c_shared[s.u], (shared_part(s)[0] - (R0 // SHARES - 1)) * 16)
                elif not (isinstance(s.t, int) and s.t == 0):
                    pe.wait_ge(c_shared[s.u], shared_part(s)[0] * 16)
                turn_rows(rowsS[0] if isinstance(s.t, int) and s.t == 0 else rows[s.u], c_T)

            def slot_of(s):
                if not routed(s):
                    return shared_part(s)[1] * SLOT
                e = pe.value_load(expC[0:1, bass.ds(s.t - R0, 1)], min_val=0, max_val=E_C - 1)
                return e * SLOT + SHARES * SLOT

            def weights(slot, p, at, n):
                return (w_hi, w_lo)[p][:, bass.ds(slot + at, n)]

            def c_gate_up(s):
                pe.wait_ge(c_ev, results_before(s) + 1)
                before(pe, c_p, s.t, 2)
                pe.sem_inc(passed["pe"], 1)
                slot = slot_of(s)
                for half in range(2):
                    mm = split_product(bank(1 + 2 * half + s.u, IC), lambda k, p: hT[rows_slot(s)][:, p * KD + k, :],
                                       lambda k, p: weights(slot, p, (2 * k + half) * IC, IC), KD)
                mm.then_inc(c_gu, 1)

            def c_turn_p(s):
                pe.wait_ge(c_p, s.t + 1)
                before(pe, c_lo_s, s.t, 1)
                for k in range(ICP // P):
                    mm = pe.transpose(bank(5, P, k * P), cs[:, k * P:(k + 1) * P], eyeF[:])
                mm.then_inc(c_pT, 1)

            def c_down(s):
                half = 0 if routed(s) else shared_part(s)[1]
                pe.wait_ge(c_lo_s, s.t + 1)
                if half == 0 and not (isinstance(s.t, int) and s.t == 0):
                    pe.wait_ge(c_yev, results_before(s))
                pe.sem_inc(passed["pe"], 1)
                slot = slot_of(s)
                split_product(bank(6), lambda k, p: cpT[:, p, k * P:(k + 1) * P],
                              lambda k, p: weights(slot, p, KD * 2 * IC + k * D, D), ICP // P,
                              half == 0, routed(s) or half == SHARES - 1).then_inc(c_dn, 1)

            c_stages = [(0, c_gate_up), (-1, c_turn), (1, c_down), (0, c_turn_p)]
            pe.wait_ge(gw_done, 2)
            pe.wait_ge(wlo_done, SHARES * LOADS_PER_SLOT)
            pe.wait_ge(b_yev, J_B)
            pe.wait_ge(pad_done, 1)
            pipeline(pe, TILES, [(0, c_gate_up), (-1, c_turn), (-1, s_router, whole), (1, c_down), (-2, s_turn, whole),
                                 (0, c_turn_p)], end=S_ROUNDS)
            pipeline(pe, TILES, c_stages, begin=S_ROUNDS, end=S_ROUNDS + 3)
            pe.wait_ge(s_lgev, T)
            route_sums(E_C, 2, 7)
            pipeline(pe, TILES, c_stages, begin=S_ROUNDS + 3, end=S_ROUNDS + 4)
            groups = S_ROUNDS + 4
            for r in range(groups, groups + 2 * T // SELS):
                pipeline(pe, TILES, c_stages, begin=r, end=r + 1)
                route_inverse(bank(7, J_C, 256), J_C, range((r - groups) * SELS, (r - groups + 1) * SELS), 2 * T, 2 * T // SELS)
            pipeline(pe, TILES, c_stages, begin=groups + 2 * T // SELS, end=R0, kind=(0, R0))
            pe.wait_ge(routeC, 1)
            pe.wait_ge(wlo_done, CHUNKS)
            pipeline(pe, TILES, c_stages, begin=R0, kind=(R0, R1))


def layouts(x, tok, w_gate, g_gate, w_down, g_down, ctx, gate_w, we_gate, we_up, we_down, sw_gate, sw_up, sw_down):
    def steps(w):
        return w.reshape(-1, P, w.shape[1]).transpose(1, 0, 2)

    def padded(w, rows):
        return np.concatenate([w, np.zeros((rows - w.shape[0], w.shape[1]), w.dtype)])

    def slot(gate, up, down):
        both = np.concatenate([steps(gate), steps(up)], axis=2).reshape(P, -1)
        return np.concatenate([both, steps(padded(down, ICP)).reshape(P, -1)], axis=1)

    parts = [slice(h * IC, (h + 1) * IC) for h in range(SHARES)]
    slots = [slot(sw_gate[:, a], sw_up[:, a], sw_down[a]) for a in parts]
    slots += [slot(we_gate[e], we_up[e], we_down[e]) for e in range(E_C)]
    moe = np.concatenate(slots, axis=1)
    return {
        "x": x.reshape(N, D),
        "tok": tok.reshape(T, P).T,
        "wgate": steps(w_gate.T).reshape(P, -1),
        "wdown": steps(w_down.T).reshape(P, -1),
        "ggate": g_gate.reshape(1, D),
        "gdown": g_down.reshape(1, IA),
        "ctxt": np.concatenate([steps(ctx[e].T) for e in range(E_B)], axis=1).reshape(P, -1),
        "gatew": steps(gate_w.T).reshape(P, -1),
        "wmoe": moe.reshape(P, CHUNKS, CHUNK).transpose(1, 0, 2).reshape(CHUNKS * P, CHUNK),
    }


_NAMES = ["x", "itok_BxS_13_99985", "L0_attn_w_gate", "L0_attn_g_gate", "L0_attn_w_down", "L0_attn_g_down", "ctx_2048",
          "L0_ffn_gate_w", "L0_ffn_w_gate", "L0_ffn_w_up", "L0_ffn_w_down", "L0_ffn_sw_gate", "L0_ffn_sw_up", "L0_ffn_sw_down"]


def kernel(**inputs):
    import concourse.bacc as bacc
    from concourse.bass_utils import run_bass_kernel_spmd

    given = [np.asarray(inputs[n]) for n in _NAMES]
    arrays = {f"in_{n}": np.ascontiguousarray(a) for n, a in layouts(*given).items()}
    nc = bacc.Bacc("TRN2", target_bir_lowering=False, num_devices=1)
    args = {n[3:]: nc.dram_tensor(n, a.shape, mybir.dt.from_np(a.dtype), kind="ExternalInput").ap() for n, a in arrays.items()}
    out = nc.dram_tensor("out_x", (N, D), F32, kind="ExternalOutput").ap()
    build(nc, out=out, **args)
    result = run_bass_kernel_spmd(nc, [arrays], core_ids=[0])
    return result.results[0]["out_x"].reshape(given[0].shape)
```
